# Optimizing a Trainium2 kernel written in Bass

```python
import numpy as np
import jax
import jax.numpy as jnp

def _softmax(x, axis=-1):
    return jax.nn.softmax(x, axis=axis)

def _gelu(x):
    return jax.nn.gelu(x, approximate=True)

def _silu(x):
    return jax.nn.silu(x)

def _sigmoid(x):
    return jax.nn.sigmoid(x)

def _layernorm(x, axis=-1, eps=1e-05):
    m = jnp.mean(x, axis=axis, keepdims=True)
    v = jnp.var(x, axis=axis, keepdims=True)
    return (x - m) / jnp.sqrt(v + eps)

def _scatter_add(tgt, idx, src, axis=0):
    return tgt.at[idx].add(src)

def _segment_sum(src, seg, n):
    return jax.ops.segment_sum(src, seg, n)
kernel_name = 'mk_adaln_d1_jaxref_r8_c6b569'

def setup_inputs(seed: int=0):
    np.random.seed(seed)
    _w = jnp.asarray

    def _L0_attn_setup():
        import jax, jax.numpy as jnp
        import numpy as np
        B, S, D, H = (4, 256, 256, 16)
        DH = D // H
        key = jax.random.key(seed)
        ks = jax.random.split(key, 11)
        p = 0.02
        return {'x': jax.random.normal(ks[0], (B, S, D), jnp.float32), 'Wq': jax.random.normal(ks[1], (D, D), jnp.float32) * p, 'bq': jax.random.normal(ks[2], (D,), jnp.float32) * p, 'Wk': jax.random.normal(ks[3], (D, D), jnp.float32) * p, 'bk': jax.random.normal(ks[4], (D,), jnp.float32) * p, 'Wv': jax.random.normal(ks[5], (D, D), jnp.float32) * p, 'bv': jax.random.normal(ks[6], (D,), jnp.float32) * p, 'Wo': jax.random.normal(ks[7], (D, D), jnp.float32) * p, 'bo': jax.random.normal(ks[8], (D,), jnp.float32) * p, 'spiral_weight': jax.random.normal(ks[9], (H,), jnp.float32), 'helix_rotation': jax.random.normal(ks[10], (D,), jnp.float32)}
    _L0_attn_in = _L0_attn_setup()

    def _L0_ffn_setup():
        import jax, jax.numpy as jnp
        import numpy as np
        HID = 256
        N_EXP = 32
        F_EXP = 96
        TOP_K = 6
        F_SH = 192
        B, S = (1, 128)
        key = jax.random.key(seed)
        ks = jax.random.split(key, 8)
        s = 0.02
        return {'hidden_states': jax.random.normal(ks[0], (B, S, HID), dtype=jnp.float32), 'gate_w': jax.random.normal(ks[1], (HID, N_EXP), dtype=jnp.float32) * s, 'wg': jax.random.normal(ks[2], (N_EXP, HID, F_EXP), dtype=jnp.float32) * s, 'wu': jax.random.normal(ks[3], (N_EXP, HID, F_EXP), dtype=jnp.float32) * s, 'wd': jax.random.normal(ks[4], (N_EXP, F_EXP, HID), dtype=jnp.float32) * s, 'sg': jax.random.normal(ks[5], (HID, F_SH), dtype=jnp.float32) * s, 'su': jax.random.normal(ks[6], (HID, F_SH), dtype=jnp.float32) * s, 'sd': jax.random.normal(ks[7], (F_SH, HID), dtype=jnp.float32) * s}
    _L0_ffn_in = _L0_ffn_setup()
    _L0_c = _w((lambda *s: np.random.randn(*s).astype(np.float32) * 0.05)(16, 256))
    _L0_wmod = _w((lambda *s: np.random.randn(*s).astype(np.float32) * 0.05)(256, 6 * 256) * 256 ** (-0.5))
    _d = {'L0_attn_x': _L0_attn_in['x'], 'L0_attn_Wq': _L0_attn_in['Wq'], 'L0_attn_bq': _L0_attn_in['bq'], 'L0_attn_Wk': _L0_attn_in['Wk'], 'L0_attn_bk': _L0_attn_in['bk'], 'L0_attn_Wv': _L0_attn_in['Wv'], 'L0_attn_bv': _L0_attn_in['bv'], 'L0_attn_Wo': _L0_attn_in['Wo'], 'L0_attn_bo': _L0_attn_in['bo'], 'L0_attn_spiral_weight': _L0_attn_in['spiral_weight'], 'L0_attn_helix_rotation': _L0_attn_in['helix_rotation'], 'L0_ffn_gate_w': _L0_ffn_in['gate_w'], 'L0_ffn_wg': _L0_ffn_in['wg'], 'L0_ffn_wu': _L0_ffn_in['wu'], 'L0_ffn_wd': _L0_ffn_in['wd'], 'L0_ffn_sg': _L0_ffn_in['sg'], 'L0_ffn_su': _L0_ffn_in['su'], 'L0_ffn_sd': _L0_ffn_in['sd'], 'L0_c': _L0_c, 'L0_wmod': _L0_wmod}
    _x0 = _d['L0_attn_x']
    _d['L0_attn_x'] = jax.random.normal(jax.random.fold_in(jax.random.key(seed), 1), (16, 256, 256), dtype=_x0.dtype)
    del _x0
    return _d

def reference(L0_attn_x, L0_attn_Wq, L0_attn_bq, L0_attn_Wk, L0_attn_bk, L0_attn_Wv, L0_attn_bv, L0_attn_Wo, L0_attn_bo, L0_attn_spiral_weight, L0_attn_helix_rotation, L0_ffn_gate_w, L0_ffn_wg, L0_ffn_wu, L0_ffn_wd, L0_ffn_sg, L0_ffn_su, L0_ffn_sd, L0_c, L0_wmod):

    def _L0_attn_ref(x, Wq, bq, Wk, bk, Wv, bv, Wo, bo, spiral_weight, helix_rotation):
        import jax, jax.numpy as jnp
        import numpy as np
        B, S, D, H = (4, 256, 256, 16)
        DH = D // H
        b, s, d = x.shape
        h, dh = (H, d // H)
        q = (x @ Wq.T + bq).reshape(b, s, h, dh)
        k = (x @ Wk.T + bk).reshape(b, s, h, dh)
        v = (x @ Wv.T + bv).reshape(b, s, h, dh)
        rot = helix_rotation.reshape(h, dh)
        q = q * jnp.cos(rot)
        k = k * jnp.sin(rot)
        scores = jnp.einsum('bshd,bthd->bhst', q, k) / np.sqrt(dh).astype(np.float32)
        scores = scores * spiral_weight[None, :, None, None]
        attn = jax.nn.softmax(scores, axis=-1)
        out = jnp.einsum('bhst,bthd->bshd', attn, v).reshape(b, s, d)
        return out @ Wo.T + bo

    def _L0_ffn_ref(hidden_states, gate_w, wg, wu, wd, sg, su, sd):
        import jax, jax.numpy as jnp
        import numpy as np
        HID = 256
        N_EXP = 32
        F_EXP = 96
        TOP_K = 6
        F_SH = 192
        B, S = (1, 128)
        orig_shape = hidden_states.shape
        x = hidden_states.reshape(-1, HID)
        scores = jax.nn.sigmoid(x @ gate_w)
        topk_w, topk_i = jax.lax.top_k(scores, TOP_K)
        topk_w = topk_w / (jnp.sum(topk_w, axis=-1, keepdims=True) + 1e-20)
        combine = jnp.sum(jax.nn.one_hot(topk_i, N_EXP, dtype=topk_w.dtype) * topk_w[..., None], axis=1)
        g = jnp.einsum('td,edf->tef', x, wg)
        u = jnp.einsum('td,edf->tef', x, wu)
        act = jax.nn.silu(g) * u
        routed = jnp.einsum('tef,efd,te->td', act, wd, combine)
        routed = routed.reshape(orig_shape)
        shared = jax.nn.silu(hidden_states @ sg) * (hidden_states @ su) @ sd
        return routed + shared
    x = L0_attn_x
    mod = (_silu(L0_c) @ L0_wmod).reshape(L0_c.shape[0], 6, 1, -1)
    sa, ca, ga, sb, cb, gb = (mod[:, 0], mod[:, 1], mod[:, 2], mod[:, 3], mod[:, 4], mod[:, 5])
    ga = (2 * (ga >= 0) - 1) * jnp.maximum(jnp.abs(ga), 0.25)
    gb = (2 * (gb >= 0) - 1) * jnp.maximum(jnp.abs(gb), 0.25)
    h = _layernorm(x, axis=-1) * (1 + ca) + sa
    x = x + ga * _L0_attn_ref(h, L0_attn_Wq, L0_attn_bq, L0_attn_Wk, L0_attn_bk, L0_attn_Wv, L0_attn_bv, L0_attn_Wo, L0_attn_bo, L0_attn_spiral_weight, L0_attn_helix_rotation)
    h = _layernorm(x, axis=-1) * (1 + cb) + sb
    x = x + gb * _L0_ffn_ref(h, L0_ffn_gate_w, L0_ffn_wg, L0_ffn_wu, L0_ffn_wd, L0_ffn_sg, L0_ffn_su, L0_ffn_sd)
    return x

_drawn_inputs = setup_inputs


def setup_inputs(seed=0):
    import zlib

    import numpy as np

    out = dict(_drawn_inputs(seed))
    spreads = {}
    factors = {'L0_attn_Wq': 8.0,
     'L0_attn_bq': 8.0,
     'L0_attn_Wk': 8.0,
     'L0_attn_bk': 8.0,
     'L0_attn_Wv': 8.0,
     'L0_attn_bv': 8.0,
     'L0_attn_Wo': 8.0,
     'L0_attn_bo': 8.0,
     'L0_attn_spiral_weight': 8.0,
     'L0_attn_helix_rotation': 8.0,
     'L0_ffn_gate_w': 8.0,
     'L0_ffn_wg': 8.0,
     'L0_ffn_wu': 8.0,
     'L0_ffn_wd': 8.0,
     'L0_ffn_sg': 8.0,
     'L0_ffn_su': 8.0,
     'L0_ffn_sd': 8.0,
     'L0_c': 8.0,
     'L0_wmod': 8.0}
    for name, (base, spread) in spreads.items():
        noise = np.random.default_rng([zlib.crc32(name.encode()), seed]).standard_normal(out[name].shape)
        drawn = base * np.exp(spread * noise) if base else spread * noise
        out[name] = jnp.asarray(drawn.astype(out[name].dtype))
    for name, factor in factors.items():
        out[name] = (out[name] * factor).astype(out[name].dtype)
    return out
```

```python
from contextlib import ExitStack

import numpy as np

import concourse.bass as bass
from concourse import mybir

F32 = mybir.dt.float32
F32R = mybir.dt.float32r
I32 = mybir.dt.int32
U32 = mybir.dt.uint32
ACT = mybir.ActivationFunctionType
ALU = mybir.AluOpType
AX = mybir.AxisListType

B, S, D = 16, 256, 256
H, DH = 16, 16
P = 128
KD = D // P
TT = S // P
HG = 4
NHG = NG = H // HG
LAG = 10
TOK = B * S
E, FE, FS, TOPK = 32, 96, 192, 6
FT = (E * FE + FS + P - 1) // P
WCOL = 2 * KD * P + D
REP = 32
CH = 512
NCH = TOK // CH
EPS = 1e-5
TWO_PI = float(2 * np.pi)
ROUND = 12582912.0

Q_ROWS = (("hi", 0), ("lo", 16), ("hi", 48), ("lo", 64))
K_ROWS = (("hi", 0), ("hi", 16), ("lo", 48), ("lo", 64))
MAX_ROW = 32
STACK = 80
MAX_BANK = (1, 1, 0, 0)

LN_SHIFT1, LN_SCALE1, GATE1, LN_SHIFT2, LN_SCALE2, GATE2 = 0, 2, 4, 6, 8, 10


def ge(eng, sem, value):
    if isinstance(value, int) and value <= 0:
        return
    eng.wait_ge(sem, value)


def wait_apart(eng, sem, value, waits_apart):
    ge(eng, sem, value)
    if not isinstance(value, int):
        eng.sem_inc(waits_apart, 1)


class Batch:

    def __init__(self, n, pair, parity):
        self.n, self.pair, self.p = n, pair, parity

    def done(self, per=1, k=None):
        return self.n * per + (per if k is None else k)


def steps(fori, body, loop_begins=None, loop_ends=None):
    def batches(t, i=None):
        out = []
        for n in range(t + 1, t - 5, -1):
            if i is None:
                out.append(Batch(n, n // 2, n % 2) if 0 <= n < B else None)
            else:
                out.append(Batch(2 * i + n, i + n // 2, n % 2))
        return out

    for t in range(-1, 5):
        body(*batches(t))
    with fori(0, 5) as i:
        for t in (5, 6):
            if loop_begins:
                loop_begins(*batches(t, i))
            body(*batches(t, i))
    if loop_ends:
        loop_ends(*batches(14))
    for t in range(15, 20):
        body(*batches(t))


def attention(nc, x, cT, wmod, wqT, wkT, wvT, woT, bq, bk, bv, bo, spiral, helix, gate_w, h2_dram, x1_dram, cw_dram,
              qk_dram, max_dram, gate2):
    ctx = ExitStack()
    with ctx:
        def sb(name, shape, dt=F32):
            return ctx.enter_context(nc.sbuf_tensor(name, shape, dt))

        def sem(name):
            return ctx.enter_context(nc.semaphore(name))

        ident = sb("ident", [P, P])
        iota_i = sb("iota_i", [P, E], I32)
        iota = sb("iota", [P, E])
        cT_sb = sb("cT_sb", [P, KD, B])
        c_exp = sb("c_exp", [P, KD, B])
        mod = sb("mod", [P, B, 12])
        mod_t = sb("mod_t", [P, B, 12])
        w_hi = sb("w_hi", [P, 3, KD, D], F32R)
        w_lo = sb("w_lo", [P, 3, KD, D], F32R)
        wo_hi = sb("wo_hi", [P, NHG, D], F32R)
        wo_lo = sb("wo_lo", [P, NHG, D], F32R)
        bias_qk = sb("bias_qk", [P, 2, KD])
        bo_sb = sb("bo_sb", [P, KD])
        bv_row = sb("bv_row", [P, D])
        spi = sb("spi", [P, KD])
        rot = sb("rot", [P, 2, KD])
        rot_t = sb("rot_t", [P, 2, KD])
        trig = sb("trig", [P, 2, KD])
        bias_s = sb("bias_s", [P, 2, KD])
        gw = sb("gw", [P, KD, E])
        ones_blk = sb("ones_blk", [8, CH])
        zero_blk = sb("zero_blk", [2, S], F32R)
        xs = sb("xs", [P, 2, TT, D])
        stats = sb("stats", [P, TT, 6])
        mv = sb("mv", [P, 2, TT, 2])
        rs = sb("rs", [P, 2, TT])
        nt = sb("nt", [P, 3, TT])
        z = sb("z", [P, TT, D])
        h1 = sb("h1", [P, KD, S])
        h1_hi = sb("h1_hi", [P, KD, S], F32R)
        h1_lo = sb("h1_lo", [P, KD, S], F32R)
        qk = sb("qk", [P, 2, KD, S])
        qk_hi = sb("qk_hi", [P, 2, KD, S], F32R)
        qk_lo = sb("qk_lo", [P, 2, KD, S], F32R)
        q_st = sb("q_st", [P, 2, H, S], F32R)
        k_st = sb("k_st", [P, 2, H, S], F32R)
        v_aug = sb("v_aug", [P, 2, TT, H, 2 * DH])
        mx = sb("mx", [P, TT, H])
        nmx = sb("nmx", [HG, NG, 2, S], F32R)
        pt = sb("pt", [P, 8, TT, S])
        o_sb2 = sb("o_sb2", [P, 2 * NHG * S])
        o_sb = o_sb2[:, 0:NHG * S].rearrange("p (a c) -> p a c", a=NHG)
        o_sum = o_sb2[:, NHG * S:2 * NHG * S].rearrange("p (a c) -> p a c", a=NHG)
        o_n = sb("o_n", [P, NHG, S])
        o_hi = sb("o_hi", [P, NHG, S], F32R)
        o_lo = sb("o_lo", [P, NHG, S], F32R)
        wmod_sb = pt[:].rearrange("p a b c -> p (a b c)")[:, 0:KD * 6 * D].rearrange("p (k n) -> p k n", k=KD)
        w_raw = o_sb2[:].rearrange("p (i k n) -> p i k n", i=4, k=KD)[:, 0:3]
        wo_raw = o_n
        cm1 = sb("cm1", [P, 2, 12])
        cm4 = sb("cm4", [P, 2, 14])
        att = sb("att", [P, KD, S])
        x4 = sb("x4", [P, TT, D])
        x1 = sb("x1", [P, TT, D])
        mv4 = sb("mv4", [P, TT, 2])
        stats4 = sb("stats4", [P, TT, 6])
        rs4 = sb("rs4", [P, TT])
        nt4 = sb("nt4", [P, 3, TT])
        z2 = sb("z2", [P, TT, D])
        h2 = sb("h2", [P, KD, S])
        g_exp = sb("g_exp", [P, TT, E])
        sc1 = sb("sc1", [P, TT, E])
        sc = sb("sc", [P, TT, E])
        top = sb("top", [P, TT, 8])
        top_i = sb("top_i", [P, TT, 8], U32)
        top_f = sb("top_f", [P, TT, 8])
        eq = sb("eq", [P, TT, E, TOPK])
        mask = sb("mask", [P, TT, E])
        kept = sb("kept", [P, TT, E])
        ksum = sb("ksum", [P, TT])
        kinv = sb("kinv", [P, TT])
        comb = sb("comb", [P, TT, E])
        combT = sb("combT", [E, S])

        ps1 = [ctx.enter_context(nc.psum_tensor(f"ps1_{i}", [P, TT, S], F32)) for i in range(2)]
        ps2 = [ctx.enter_context(nc.psum_tensor(f"ps2_{i}", [P, TT, S], F32)) for i in range(2)]
        ps_o = [ctx.enter_context(nc.psum_tensor(f"ps_o{i}", [P, 2, S], F32)) for i in range(2)]
        ps_m = [ctx.enter_context(nc.psum_tensor(f"ps_m{i}", [P, 2, 256], F32)) for i in range(2)]

        names = """c_loaded mod_loaded w_loaded wo_zero wo_loaded b_loaded ident_zero ident_done iota_int iota_done
            c_exp_done silu_c mod_ready mod_done mod_step rot_step trig_done wsplit wo_split bias_done blocks_set
            zeros_set ones_set consts_stored stack_init v_ones
            aggr1 seed1 newton1 rstd1 z_ready zT_ready h1_ready h1_hi_ready h1_lo_ready
            q_ready k_ready q_evac k_evac qk_hi_ready qk_split v_ready v_evac
            scores1 max_done mxT_ready nmx_hi nmx_ready scores2 probs pv_done o_evac
            o_shuffled o_recip o_norm o_hi_ready o_lo_ready
            att_ready att_evac attT_ready x1_ready aggr4 seed4 newton4 rstd4 z2_ready z2T_ready h2_ready
            logits g_exp_done sc1_done sc_done top_done idx_done idxf_done eq_done mask_done kept_done ksum_done
            keps_done kinv_done comb_ready combT_ready combT_evac
            cm1_ready cm4_ready x4_loaded x1_stored h2_stored comb_stored
            stats1 stats4 qk_stored pool_apart dve_apart sp_apart""".split()
        s = {n: sem(n) for n in names}
        x_loaded = [sem(f"x_loaded{i}") for i in range(2)]
        stacked = [[sem(f"stacked{i}{m}") for m in range(KD)] for i in range(2)]
        max_stored = [sem(f"max_stored{i}") for i in range(NG)]
        max_rows = [sem(f"max_rows{i}") for i in range(NG)]
        block = ctx.enter_context(nc.Block())

        def loads(m):
            return len(Q_ROWS) + len(K_ROWS) + (1 if m == 0 else 0)

        @block.sync
        def _(sp):
            sp.dma_start(cT_sb[:], cT.rearrange("(k p) b -> p k b", p=P)).then_inc(s["c_loaded"], 16)
            sp.dma_start(wmod_sb, wmod.rearrange("(k p) n -> p k n", p=P)).then_inc(s["mod_loaded"], 16)
            for i, w in enumerate((wqT, wkT, wvT)):
                sp.dma_start(w_raw[:, i], w.rearrange("(k p) n -> p k n", p=P)).then_inc(s["w_loaded"], 16)
            sp.dma_start(bias_qk[:, 0], bq).then_inc(s["b_loaded"], 16)
            sp.dma_start(bias_qk[:, 1], bk).then_inc(s["b_loaded"], 16)
            sp.dma_start(bo_sb[:], bo).then_inc(s["b_loaded"], 16)
            sp.dma_start(spi[:], spiral).then_inc(s["b_loaded"], 16)
            sp.dma_start(rot[:, 1], helix).then_inc(s["b_loaded"], 16)
            sp.dma_start(bv_row[:], bv.partition_broadcast(P)).then_inc(s["b_loaded"], 16)
            sp.dma_start(gw[:], gate_w.rearrange("(k p) e -> p k e", p=P)).then_inc(s["b_loaded"], 16)
            sp.wait_ge(s["wo_zero"], 1)
            for g in range(HG):
                sp.dma_start(wo_raw[32 * g:32 * g + DH], woT.rearrange("(a g d) n -> g d a n", g=HG, d=DH)[g])\
                    .then_inc(s["wo_loaded"], 16)
            sp.wait_ge(s["blocks_set"], 1)
            sp.dma_start(cw_dram[3 * E:3 * E + 8].rearrange("r (a c) -> r a c", c=CH),
                         ones_blk[:].unsqueeze(1).broadcast_to([8, NCH, CH])).then_inc(s["consts_stored"], 16)

            def step(n0, n1, n2, n3, n4, n5):
                if n0:
                    ge(sp, s["z_ready"], n0.n - 1)
                    sp.dma_start(xs[:, n0.p], tokens(x, n0)).then_inc(x_loaded[n0.p], 16)
                if n4:
                    ge(sp, s["x1_ready"], n4.n)
                    sp.dma_start(x4[:], tokens(x, n4)).then_inc(s["x4_loaded"], 16)
                if n1:
                    for m in range(KD):
                        wait_apart(sp, stacked[n1.p][m], n1.pair * (16 * loads(m)), s["sp_apart"])
                    for i in range(2):
                        sp.wait_ge(s["qk_split"], n1.done(2, i + 1))
                        for j, part in enumerate((qk_hi, qk_lo)):
                            sp.dma_start(qk_dram[n1.p, i, j].rearrange("(m p) c -> p m c", p=P),
                                         part[:, i].bitcast(F32)).then_inc(s["qk_stored"], 16)
                if n4:
                    sp.wait_ge(s["x1_ready"], n4.done())
                    sp.dma_start(tokens(x1_dram, n4), x1[:]).then_inc(s["x1_stored"], 16)
                if n1:
                    ge(sp, s["scores2"], (n1.n - 1) * H)
                    ge(sp, s["stack_init"], 4)
                    ge(sp, s["zeros_set"], 1)
                    sp.wait_ge(s["qk_stored"], n1.done(64))
                    sp.dma_start(q_st[MAX_ROW:MAX_ROW + 2, n1.p].bitcast(F32),
                                 zero_blk[:].bitcast(F32).unsqueeze(1).broadcast_to([2, H, S]))\
                        .then_inc(stacked[n1.p][0], 16)
                    for m in range(KD):
                        for i, (st, rows) in enumerate(((q_st, Q_ROWS), (k_st, K_ROWS))):
                            for part, r0 in rows:
                                src = qk_dram[n1.p, i, int(part == "lo")].rearrange("(h d) c -> d h c", d=DH)
                                sp.dma_start(st[r0:r0 + DH, n1.p, m * 8:(m + 1) * 8].bitcast(F32),
                                             src[:, m * 8:(m + 1) * 8]).then_inc(stacked[n1.p][m], 16)
                if n4:
                    sp.wait_ge(s["h2_ready"], n4.done())
                    sp.dma_start(h2_dram[:, :, bass.ds(n4.n * S, S)].rearrange("k p c -> p k c"), h2[:])\
                        .then_inc(s["h2_stored"], 16)
                if n5:
                    sp.wait_ge(s["combT_evac"], n5.done())
                    for r in range(FE // REP):
                        sp.dma_start(cw_dram[0:3 * E, bass.ds(n5.n * S, S)].rearrange("(e r) c -> e r c", r=3)[:, r],
                                     combT[:]).then_inc(s["comb_stored"], 16)

            def tokens(dram, n):
                return dram[bass.ds(n.n, 1)].rearrange("a (t p) d -> p (a t) d", p=P)

            steps(sp.Fori, step)
            sp.wait_ge(s["consts_stored"], 16)
            sp.wait_ge(s["x1_stored"], 16 * B)
            sp.wait_ge(s["h2_stored"], 16 * B)
            sp.wait_ge(s["comb_stored"], 48 * B)

        @block.gpsimd
        def _(pool):
            g = nc.gpsimd
            g.memset(ident[:], 0.0).then_inc(s["ident_zero"], 1)
            pool.wait_ge(s["ident_zero"], 1)
            g.affine_select(out=ident[:], in_=ident[:], compare_op=ALU.not_equal, fill=1.0, base=0,
                            pattern=[[-1, P]], channel_multiplier=1).then_inc(s["ident_done"], 1)
            g.iota(iota_i[:], pattern=[[1, E]], base=0, channel_multiplier=0).then_inc(s["iota_int"], 1)
            pool.wait_ge(s["iota_int"], 1)
            g.memset(ones_blk[:], 1.0).then_inc(s["blocks_set"], 1)
            pool.wait_ge(s["blocks_set"], 1)
            g.memset(zero_blk[:].bitcast(F32), 0.0).then_inc(s["zeros_set"], 1)
            pool.wait_ge(s["zeros_set"], 1)
            g.memset(q_st[32:64].bitcast(F32), 0.0).then_inc(s["stack_init"], 1)
            pool.wait_ge(s["stack_init"], 1)
            g.memset(k_st[32:64].bitcast(F32), 0.0).then_inc(s["stack_init"], 1)
            pool.wait_ge(s["stack_init"], 2)
            g.memset(k_st[MAX_ROW:MAX_ROW + 2].bitcast(F32), 1.0).then_inc(s["stack_init"], 1)
            pool.wait_ge(s["stack_init"], 3)
            g.memset(v_aug[:], 1.0).then_inc(s["stack_init"], 1)
            g.tensor_copy(iota[:], iota_i[:]).then_inc(s["iota_done"], 1)

            def newton(y, t, n):
                wait_apart(pool, s["seed1"], n.done(), s["pool_apart"])
                for i in range(3):
                    ops = ((t[:, 1], y, y, None), (t[:, 1], t[:, 1], t[:, 0], None), (t[:, 2], t[:, 1], None, 1.5),
                           (y, y, t[:, 2], None))
                    for j, (o, a, b, c) in enumerate(ops):
                        if i or j:
                            wait_apart(pool, s["rstd1"], n.n * 12 + 4 * i + j, s["pool_apart"])
                        if c is None:
                            g.tensor_tensor(o, a, b, ALU.mult).then_inc(s["rstd1"], 1)
                        else:
                            g.tensor_scalar(o, a, c, None, ALU.add).then_inc(s["rstd1"], 1)

            def step(n0, n1, n2, n3, n4, n5):
                if n4:
                    low_output(n4, 1)
                if n1:
                    for i, name in enumerate(("q_evac", "k_evac")):
                        ge(pool, s["qk_stored"], n1.n * 64)
                        wait_apart(pool, s[name], n1.done(), s["pool_apart"])
                        g.tensor_copy(qk_hi[:, i], qk[:, i]).then_inc(s["qk_hi_ready"], 1)
                        pool.wait_ge(s["qk_hi_ready"], n1.done(2, i + 1))
                        g.tensor_tensor(qk_lo[:, i], qk[:, i], qk_hi[:, i].bitcast(F32), ALU.subtract)\
                            .then_inc(s["qk_split"], 1)
                if n3:
                    low_output(n3, 0)
                    ge(pool, s["mod_done"], 1)
                    wait_apart(pool, s["h2_ready"], n3.n - 1, s["pool_apart"])
                    g.tensor_copy(cm4[:, n3.p, 0:12], mod[:, bass.ds(n3.n, 1)].rearrange("p a c -> p (a c)"))\
                        .then_inc(s["cm4_ready"], 1)
                    pool.wait_ge(s["cm4_ready"], n3.done(2, 1))
                    g.tensor_tensor(cm4[:, n3.p, 12:14], cm4[:, n3.p, GATE1:GATE1 + 2], bo_sb[:], ALU.mult)\
                        .then_inc(s["cm4_ready"], 1)
                if n0:
                    ge(pool, s["mod_done"], 1)
                    wait_apart(pool, s["h1_ready"], n0.n - 1, s["pool_apart"])
                    g.tensor_copy(cm1[:, n0.p], mod[:, bass.ds(n0.n, 1)].rearrange("p a c -> p (a c)"))\
                        .then_inc(s["cm1_ready"], 1)
                    newton(rs[:, n0.p], nt, n0)

            def low_output(n, half):
                cols = slice(2 * half, 2 * half + 2)
                pool.wait_ge(s["o_hi_ready"], n.done(2, half + 1))
                ge(pool, s["att_ready"], n.n)
                g.tensor_tensor(o_lo[:, cols], o_n[:, cols], o_hi[:, cols].bitcast(F32), ALU.subtract)\
                    .then_inc(s["o_lo_ready"], 1)

            steps(pool.Fori, step)

        @block.scalar
        def _(act):
            a = nc.scalar
            act.wait_ge(s["c_loaded"], 16)
            a.activation(c_exp[:], cT_sb[:], ACT.Exp, scale=-1.0).then_inc(s["c_exp_done"], 1)
            act.wait_ge(s["rot_step"], 6)
            a.activation(trig[:], rot[:], ACT.Sin).then_inc(s["trig_done"], 1)

            def affine(out, bank, scales, shifts):
                for k in range(KD):
                    ins = a.activation(out[:, k], bank[:, k], ACT.Identity, bias=shifts[:, k:k + 1],
                                       scale=scales[:, k:k + 1])
                return ins

            def step(n0, n1, n2, n3, n4, n5):
                if n5:
                    act.wait_ge(s["logits"], n5.done())
                    ge(act, s["sc1_done"], n5.n)
                    a.activation(g_exp[:], ps_m[0][:, 0, 0:TT * E].rearrange("p (t e) -> p t e", t=TT),
                                 ACT.Exp, scale=-1.0).then_inc(s["g_exp_done"], 1)
                if n4:
                    high_output(n4, 1)
                if n1:
                    act.wait_ge(s["zT_ready"], n1.done())
                    act.wait_ge(s["cm1_ready"], n1.done())
                    ge(act, s["h1_lo_ready"], n1.n)
                    affine(h1, ps_m[1], cm1[:, n1.p, LN_SCALE1:], cm1[:, n1.p, LN_SHIFT1:]).then_inc(s["h1_ready"], 1)
                for i in range(H):
                    if n3 and i == 1:
                        store_max(n3, 3)
                    if n2 and i % 4 == 1 and i > 1:
                        store_max(n2, i // 4 - 1)
                    if n3 and i in (0, 4):
                        load_max(n3, 2 + i // 4)
                    if n2 and i % 4 == 0 and i > 4:
                        load_max(n2, i // 4 - 2)
                    if n4 and i == 3:
                        act.wait_ge(s["att_ready"], n4.done())
                        act.wait_ge(s["cm4_ready"], n4.done(2))
                        ge(act, s["attT_ready"], n4.n)
                        affine(att, ps_m[0], cm4[:, n4.p, GATE1:], cm4[:, n4.p, 12:]).then_inc(s["att_evac"], 1)
                    if n3 and i == 4:
                        o_copy(n3, 0)
                    if n1 and i in (5, 6):
                        j = i - 5
                        act.wait_ge(s["qk"[j] + "_ready"], n1.done())
                        ge(act, s["qk_split"], n1.n * 2 - 1 + j)
                        ge(act, s["bias_done"], 1)
                        affine(qk[:, j], ps_m[j], trig[:, j], bias_s[:, j]).then_inc(s["qk"[j] + "_evac"], 1)
                    if n3 and i == 8:
                        high_output(n3, 0)
                    if n3 and i == 12:
                        o_copy(n3, 1)
                    if n4 and i == 13:
                        act.wait_ge(s["z2T_ready"], n4.done())
                        ge(act, s["h2_stored"], n4.n * 16)
                        ge(act, s["logits"], n4.n)
                        affine(h2, ps_m[1], cm4[:, n4.p, LN_SCALE2:], cm4[:, n4.p, LN_SHIFT2:])\
                            .then_inc(s["h2_ready"], 1)
                    if n5 and i == 14:
                        act.wait_ge(s["combT_ready"], n5.done())
                        ge(act, s["comb_stored"], n5.n * 48)
                        a.activation(combT[:], ps_m[1][0:E].rearrange("p a c -> p (a c)")[:, 0:S], ACT.Copy)\
                            .then_inc(s["combT_evac"], 1)
                    if i < LAG and n3:
                        exp(n3, i + H - LAG)
                    if i >= LAG and n2:
                        exp(n2, i - LAG)

            def exp(n, h):
                act.wait_ge(s["scores2"], n.done(H, h + 1))
                ge(act, s["pv_done"], n.n * NHG + h // HG - 1)
                a.activation(pt[:, h % 8], ps2[h % 2][:], ACT.Exp).then_inc(s["probs"], 1)

            def o_copy(n, half):
                act.wait_ge(s["pv_done"], n.done(NHG, 2 * half + 2))
                ge(act, s["o_norm"], n.n * 2 + half - 1)
                a.activation(o_sb[:, 2 * half:2 * half + 2], ps_o[half][:], ACT.Copy).then_inc(s["o_evac"], 1)

            def high_output(n, half):
                cols = slice(2 * half, 2 * half + 2)
                act.wait_ge(s["o_norm"], n.done(2, half + 1))
                ge(act, s["att_ready"], n.n)
                a.activation(o_hi[:, cols], o_n[:, cols], ACT.Copy).then_inc(s["o_hi_ready"], 1)

            def store_max(n, g):
                act.wait_ge(s["nmx_ready"], n.done(NG, g + 1))
                ge(act, max_rows[g], n.n * 16)
                act.dma_start(max_dram[g].rearrange("r j c -> j r c"), nmx[:, g].bitcast(F32))\
                    .then_inc(max_stored[g], 16)

            def load_max(n, g):
                act.wait_ge(max_stored[g], n.done(16))
                act.wait_ge(s["scores1"], n.done(H, HG * g + HG))
                act.dma_start(q_st[MAX_ROW:MAX_ROW + 2, n.p, HG * g:HG * g + HG].bitcast(F32), max_dram[g])\
                    .then_inc(max_rows[g], 16)

            steps(act.Fori, step)

        @block.vector
        def _(dve):
            v = nc.vector
            dve.wait_ge(s["c_exp_done"], 1)
            v.tensor_scalar(c_exp[:], c_exp[:], 1.0, None, ALU.add).then_inc(s["silu_c"], 1)
            dve.wait_ge(s["silu_c"], 1)
            v.reciprocal(c_exp[:], c_exp[:]).then_inc(s["silu_c"], 1)
            dve.wait_ge(s["silu_c"], 2)
            v.tensor_tensor(cT_sb[:], cT_sb[:], c_exp[:], ALU.mult).then_inc(s["silu_c"], 1)
            v.memset(wo_raw[:], 0.0).then_inc(s["wo_zero"], 1)
            dve.wait_ge(s["b_loaded"], 7 * 16)
            v.tensor_scalar(rot[:, 0], rot[:, 1], TWO_PI / 4, None, ALU.add).then_inc(s["rot_step"], 1)
            dve.wait_ge(s["rot_step"], 1)
            v.tensor_scalar(rot_t[:], rot[:], 1.0 / TWO_PI, ROUND, ALU.mult, ALU.add).then_inc(s["rot_step"], 1)
            dve.wait_ge(s["rot_step"], 2)
            v.tensor_scalar(rot_t[:], rot_t[:], ROUND, None, ALU.subtract).then_inc(s["rot_step"], 1)
            high = 6.28125
            dve.wait_ge(s["rot_step"], 3)
            v.scalar_tensor_tensor(out=rot[:], in0=rot_t[:], scalar=-high, in1=rot[:], op0=ALU.mult, op1=ALU.add)\
                .then_inc(s["rot_step"], 1)
            dve.wait_ge(s["rot_step"], 4)
            v.scalar_tensor_tensor(out=rot[:], in0=rot_t[:], scalar=-(TWO_PI - high), in1=rot[:], op0=ALU.mult,
                                   op1=ALU.add).then_inc(s["rot_step"], 1)
            dve.wait_ge(s["rot_step"], 5)
            v.tensor_scalar(rot[:], rot[:], 3.1415925, -3.1415925, ALU.min, ALU.max).then_inc(s["rot_step"], 1)
            dve.wait_ge(s["w_loaded"], 48)
            v.tensor_copy(w_hi[:], w_raw).then_inc(s["wsplit"], 1)
            dve.wait_ge(s["wsplit"], 1)
            v.tensor_tensor(w_lo[:], w_raw, w_hi[:].bitcast(F32), ALU.subtract).then_inc(s["wsplit"], 1)
            dve.wait_ge(s["wo_loaded"], 64)
            v.tensor_copy(wo_hi[:], wo_raw[:]).then_inc(s["wo_split"], 1)
            dve.wait_ge(s["wo_split"], 1)
            v.tensor_tensor(wo_lo[:], wo_raw[:], wo_hi[:].bitcast(F32), ALU.subtract).then_inc(s["wo_split"], 1)
            dve.wait_ge(s["trig_done"], 1)
            v.scalar_tensor_tensor(out=trig[:, 0], in0=trig[:, 0], scalar=float(DH) ** -0.5, in1=spi[:],
                                   op0=ALU.mult, op1=ALU.mult).then_inc(s["trig_done"], 1)
            dve.wait_ge(s["trig_done"], 2)
            v.tensor_tensor(bias_s[:], bias_qk[:], trig[:], ALU.mult).then_inc(s["bias_done"], 1)
            dve.wait_ge(s["mod_ready"], 1)
            v.tensor_copy(mod[:], ps1[0][:].rearrange("p a c -> p (a c)")[:, 0:12 * B]
                          .rearrange("p (j b) -> p b j", b=B)).then_inc(s["mod_step"], 1)
            n = 1
            for col in (LN_SCALE1, LN_SCALE2):
                dve.wait_ge(s["mod_step"], n)
                v.tensor_scalar(mod[:, :, col:col + 2], mod[:, :, col:col + 2], 1.0, None, ALU.add)\
                    .then_inc(s["mod_step"], 1)
                n += 1
            for col in (GATE1, GATE2):
                gate, tmp = mod[:, :, col:col + 2], mod_t[:, :, col:col + 2]
                dve.wait_ge(s["mod_step"], n)
                v.scalar_tensor_tensor(out=tmp, in0=gate, scalar=-1.0, in1=gate, op0=ALU.mult, op1=ALU.max)\
                    .then_inc(s["mod_step"], 1)
                v.tensor_scalar(mod_t[:, :, 0:2], gate, 0.0, 2.0, ALU.is_ge, ALU.mult).then_inc(s["mod_step"], 1)
                dve.wait_ge(s["mod_step"], n + 2)
                v.tensor_scalar(tmp, tmp, 0.25, None, ALU.max).then_inc(s["mod_step"], 1)
                dve.wait_ge(s["mod_step"], n + 3)
                v.scalar_tensor_tensor(out=gate, in0=mod_t[:, :, 0:2], scalar=-1.0, in1=tmp, op0=ALU.add,
                                       op1=ALU.mult).then_inc(s["mod_step"], 1)
                n += 4
            dve.wait_ge(s["mod_step"], n)
            v.tensor_copy(gate2[:], mod[:, :, GATE2:GATE2 + 2]).then_inc(s["mod_done"], 1)

            def stats_of(src, st, out_mv, i, y, t, n):
                bn, aggr, half_v, seed = (s[f"{name}{i}"] for name in ("stats", "aggr", "newton", "seed"))
                for j in range(TT):
                    ins = v.bn_stats(st[:, j], src[:, j])
                ins.then_inc(bn, 1)
                wait_apart(dve, bn, n.done(), s["dve_apart"])
                for j in range(TT):
                    ins = v.bn_aggr(out_mv[:, j], st[:, j])
                ins.then_inc(aggr, 1)
                dve.wait_ge(aggr, n.done())
                v.tensor_scalar(t[:, 1], out_mv[:, :, 1], EPS, None, ALU.add).then_inc(half_v, 1)
                dve.wait_ge(half_v, n.done(2, 1))
                v.tensor_scalar(t[:, 2].bitcast(I32), t[:, 1].bitcast(I32), 1, None, ALU.logical_shift_right)\
                    .then_inc(half_v, 1)
                v.tensor_scalar(t[:, 0], t[:, 1], -0.5, None, ALU.mult)
                dve.wait_ge(half_v, n.done(2, 2))
                v.tensor_scalar(y.bitcast(I32), t[:, 2].bitcast(I32), -1.0, float(0x5F3759DF), ALU.mult, ALU.add)\
                    .then_inc(seed, 1)

            def newton4(n, i):
                if i == 0:
                    dve.wait_ge(s["seed4"], n.done())
                else:
                    dve.wait_ge(s["rstd4"], n.n * 9 + 3 * i)
                v.tensor_tensor(nt4[:, 1], rs4[:], nt4[:, 0], ALU.mult).then_inc(s["rstd4"], 1)
                dve.wait_ge(s["rstd4"], n.n * 9 + 3 * i + 1)
                v.tensor_tensor(nt4[:, 2], rs4[:], nt4[:, 1], ALU.mult).then_inc(s["rstd4"], 1)
                dve.wait_ge(s["rstd4"], n.n * 9 + 3 * i + 2)
                v.scalar_tensor_tensor(out=rs4[:], in0=nt4[:, 2], scalar=1.5, in1=rs4[:], op0=ALU.add, op1=ALU.mult)\
                    .then_inc(s["rstd4"], 1)

            def reduce(n2, h):
                dve.wait_ge(s["scores1"], n2.done(H, h + 1))
                if h % HG == 0:
                    ge(dve, s["mxT_ready"], (n2.n - 1) * NG + h // HG + 1)
                v.tensor_reduce(mx[:, :, h], ps1[h % 2][:], axis=AX.X, op=ALU.max).then_inc(s["max_done"], 1)

            def negate_max(n, g):
                bank = ps_m[MAX_BANK[g]][0:HG].rearrange("p a c -> p (a c)")[:, 0:S]
                dve.wait_ge(s["mxT_ready"], n.done(NG, g + 1))
                ge(dve, max_stored[g], n.n * 16)
                v.tensor_scalar(nmx[:, g, 0], bank, -1.0, None, ALU.mult).then_inc(s["nmx_hi"], 1)
                dve.wait_ge(s["nmx_hi"], n.done(NG, g + 1))
                v.scalar_tensor_tensor(out=nmx[:, g, 1], in0=bank, scalar=-1.0, in1=nmx[:, g, 0].bitcast(F32),
                                       op0=ALU.mult, op1=ALU.subtract).then_inc(s["nmx_ready"], 1)

            def normalise(n, half, part):
                cols = slice(2 * half, 2 * half + 2)
                if part == 0:
                    wait_apart(dve, s["o_evac"], n.done(2, half + 1), s["dve_apart"])
                    v.stream_shuffle(flat(o_sum[:, cols]), flat(o_sb[:, cols]), [DH + i % DH for i in range(32)])\
                        .then_inc(s["o_shuffled"], 1)
                elif part == 1:
                    dve.wait_ge(s["o_shuffled"], n.done(2, half + 1))
                    v.reciprocal(o_sum[:, cols], o_sum[:, cols]).then_inc(s["o_recip"], 1)
                else:
                    dve.wait_ge(s["o_recip"], n.done(2, half + 1))
                    ge(dve, s["o_lo_ready"], n.n * 2 + half - 1)
                    v.tensor_tensor(o_n[:, cols], o_sb[:, cols], o_sum[:, cols], ALU.mult).then_inc(s["o_norm"], 1)

            def flat(ap):
                return ap.rearrange("p a c -> p (a c)")

            def route(n5, i):
                if i == 0:
                    dve.wait_ge(s["g_exp_done"], n5.done())
                    v.tensor_scalar(sc1[:], g_exp[:], 1.0, None, ALU.add).then_inc(s["sc1_done"], 1)
                if i == 1:
                    dve.wait_ge(s["sc1_done"], n5.done())
                    v.reciprocal(sc[:], sc1[:]).then_inc(s["sc_done"], 1)
                if i == 2:
                    wait_apart(dve, s["sc_done"], n5.done(), s["dve_apart"])
                    for j in range(TT):
                        ins = v.max(top[:, j], sc[:, j])
                    ins.then_inc(s["top_done"], 1)
                if i == 3:
                    wait_apart(dve, s["top_done"], n5.done(), s["dve_apart"])
                    for j in range(TT):
                        ins = v.max_index(top_i[:, j], top[:, j], sc[:, j])
                    ins.then_inc(s["idx_done"], 1)
                if i == 4:
                    dve.wait_ge(s["idx_done"], n5.done())
                    v.tensor_copy(top_f[:], top_i[:]).then_inc(s["idxf_done"], 1)
                if i == 5:
                    dve.wait_ge(s["idxf_done"], n5.done())
                    ge(dve, s["iota_done"], 1)
                    for j in range(TT):
                        ins = v.tensor_tensor(eq[:, j], iota[:].unsqueeze(2).broadcast_to([P, E, TOPK]),
                                              top_f[:, j, 0:TOPK].unsqueeze(1).broadcast_to([P, E, TOPK]),
                                              ALU.is_equal)
                    ins.then_inc(s["eq_done"], 1)
                if i == 6:
                    dve.wait_ge(s["eq_done"], n5.done())
                    v.tensor_reduce(mask[:].rearrange("p t e -> p (t e)"),
                                    eq[:].rearrange("p t e k -> p (t e) k"), axis=AX.X, op=ALU.add)\
                        .then_inc(s["mask_done"], 1)
                if i == 7:
                    dve.wait_ge(s["mask_done"], n5.done())
                    v.tensor_tensor(kept[:], mask[:], sc[:], ALU.mult).then_inc(s["kept_done"], 1)
                if i == 8:
                    dve.wait_ge(s["kept_done"], n5.done())
                    v.tensor_reduce(ksum[:], kept[:], axis=AX.X, op=ALU.add).then_inc(s["ksum_done"], 1)
                if i == 9:
                    dve.wait_ge(s["ksum_done"], n5.done())
                    v.tensor_scalar(kinv[:], ksum[:], 1e-20, None, ALU.add).then_inc(s["keps_done"], 1)
                if i == 10:
                    dve.wait_ge(s["keps_done"], n5.done())
                    v.reciprocal(kinv[:], kinv[:]).then_inc(s["kinv_done"], 1)
                if i == 11:
                    dve.wait_ge(s["kinv_done"], n5.done())
                    ge(dve, s["combT_ready"], n5.n)
                    v.tensor_tensor(comb[:], kept[:], kinv[:].unsqueeze(2).broadcast_to([P, TT, E]), ALU.mult)\
                        .then_inc(s["comb_ready"], 1)

            def step(n0, n1, n2, n3, n4, n5):
                if n1:
                    dve.wait_ge(s["rstd1"], n1.done(12))
                    ge(dve, s["zT_ready"], n1.n)
                    for i in range(TT):
                        ins = v.tensor_scalar(z[:, i], xs[:, n1.p, i], mv[:, n1.p, i, 0:1], rs[:, n1.p, i:i + 1],
                                              ALU.subtract, ALU.mult)
                    ins.then_inc(s["z_ready"], 1)
                for h in range(H):
                    if n2:
                        reduce(n2, h)
                    if n3 and h == 0:
                        negate_max(n3, 3)
                    if n2 and h in (4, 8, 12):
                        negate_max(n2, h // 4 - 1)
                    if n5:
                        route(n5, h)
                    if n1 and h == 2:
                        dve.wait_ge(s["h1_ready"], n1.done())
                        ge(dve, s["v_ready"], n1.n)
                        v.tensor_copy(h1_hi[:], h1[:]).then_inc(s["h1_hi_ready"], 1)
                    if n1 and h == 3:
                        dve.wait_ge(s["h1_hi_ready"], n1.done())
                        v.tensor_tensor(h1_lo[:], h1[:], h1_hi[:].bitcast(F32), ALU.subtract)\
                            .then_inc(s["h1_lo_ready"], 1)
                    if n3 and h in (5, 6, 7):
                        normalise(n3, 0, h - 5)
                    if n4 and h == 6:
                        dve.wait_ge(s["attT_ready"], n4.done())
                        dve.wait_ge(s["x4_loaded"], n4.done(16))
                        ge(dve, s["x1_stored"], 16 * n4.n)
                        ge(dve, s["z2_ready"], n4.n)
                        v.tensor_tensor(x1[:], ps_m[0][:], x4[:], ALU.add).then_inc(s["x1_ready"], 1)
                    if n4 and h == 7:
                        dve.wait_ge(s["x1_ready"], n4.done())
                        stats_of(x1, stats4, mv4, 4, rs4[:], nt4, n4)
                    if n4 and h in (8, 9, 10):
                        newton4(n4, h - 8)
                    if n4 and h == 11:
                        dve.wait_ge(s["rstd4"], n4.done(9))
                        ge(dve, s["z2T_ready"], n4.n)
                        for i in range(TT):
                            ins = v.tensor_scalar(z2[:, i], x1[:, i], mv4[:, i, 0:1], rs4[:, i:i + 1],
                                                  ALU.subtract, ALU.mult)
                        ins.then_inc(s["z2_ready"], 1)
                    if n1 and h == 14:
                        dve.wait_ge(s["v_ready"], n1.done())
                        ge(dve, s["pv_done"], (n1.n - 1) * NHG)
                        ge(dve, s["stack_init"], 4)
                        for i in range(TT):
                            ins = v.tensor_tensor(v_aug[:, n1.p, i, :, 0:DH],
                                                  ps_m[0][:, i].rearrange("p (h d) -> p h d", d=DH),
                                                  bv_row[:].rearrange("p (h d) -> p h d", d=DH), ALU.add)
                        ins.then_inc(s["v_evac"], 1)
                    if n3 and h in (13, 14, 15):
                        normalise(n3, 1, h - 13)
                if n0:
                    dve.wait_ge(x_loaded[n0.p], (n0.pair + 1) * 16)
                    ge(dve, s["rstd1"], n0.n * 12)
                    stats_of(xs[:, n0.p], stats, mv[:, n0.p], 1, rs[:, n0.p], nt, n0)

            steps(dve.Fori, step)

        @block.tensor
        def _(pe):
            t = nc.tensor
            pe.wait_ge(s["silu_c"], 3)
            pe.wait_ge(s["mod_loaded"], 16)
            pm = ps1[0][:].rearrange("p a c -> p (a c)")
            for j in range(12):
                for k in range(KD):
                    ins = t.matmul(pm[:, j * B:(j + 1) * B], wmod_sb[:, k, j * P:(j + 1) * P], cT_sb[:, k],
                                   start=k == 0, stop=k == KD - 1)
            ins.then_inc(s["mod_ready"], 1)
            pe.wait_ge(s["ident_done"], 1)

            def products(out, pairs):
                terms = [(a, b) for (ah, al), (bh, bl) in pairs for a, b in ((ah, bh), (ah, bl), (al, bh))]
                for i, (a, b) in enumerate(terms):
                    ins = t.matmul(out, a, b, start=i == 0, stop=i == len(terms) - 1)
                return ins

            last = [None, None]

            def use(bank, evacuated, value):
                if last[bank]:
                    pe.wait_ge(*last[bank])
                last[bank] = s[evacuated], value
                return ps_m[bank]

            def transposes(out, src):
                for i in range(TT):
                    for k in range(2):
                        ins = t.transpose(out[:, k, i * P:(i + 1) * P], src[:, i, k * P:(k + 1) * P], ident[:])
                return ins

            def scores1(n, h):
                if h % 8 == 0:
                    pe.wait_ge(stacked[n.p][h // 8], (n.pair + 1) * (16 * loads(h // 8)))
                    ge(pe, s["mod_done"], 1)
                ge(pe, s["max_done"], n.n * H + h - 1)
                for i in range(TT):
                    ins = t.matmul(ps1[h % 2][:, i], q_st[0:STACK, n.p, h, i * P:(i + 1) * P], k_st[0:STACK, n.p, h],
                                   start=True, stop=True)
                ins.then_inc(s["scores1"], 1)

            def scores2(n, h):
                if h % HG == 0:
                    pe.wait_ge(max_rows[h // HG], n.done(16))
                ge(pe, s["probs"], n.n * H + h - 1)
                for i in range(TT):
                    ins = t.matmul(ps2[h % 2][:, i], k_st[0:STACK, n.p, h, i * P:(i + 1) * P], q_st[0:STACK, n.p, h],
                                   start=True, stop=True)
                ins.then_inc(s["scores2"], 1)

            def pv(n, hg):
                pe.wait_ge(s["probs"], n.done(H, HG * (hg + 1)))
                if hg == 0:
                    pe.wait_ge(s["v_evac"], n.done())
                if hg % 2 == 0:
                    ge(pe, s["o_evac"], n.n * 2 + hg // 2 - 1)
                for i in range(TT):
                    for g in range(HG):
                        h = hg * HG + g
                        ins = t.matmul(ps_o[hg // 2][32 * g:32 * g + 32, hg % 2], v_aug[:, n.p, i, h], pt[:, h % 8, i],
                                       start=i == 0, stop=i == TT - 1, tile_position=(0, 32 * g))
                ins.then_inc(s["pv_done"], 1)

            def transpose_max(n, g):
                pe.wait_ge(s["max_done"], n.done(H, HG * g + HG))
                bank = use(MAX_BANK[g], "nmx_ready", n.done(NG, g + 1))
                for i in range(TT):
                    ins = t.transpose(bank[0:HG].rearrange("p a c -> p (a c)")[:, i * P:(i + 1) * P],
                                      mx[:, i, HG * g:HG * g + HG], ident[:])
                ins.then_inc(s["mxT_ready"], 1)

            def project(n1, i, name, bank):
                if i == 0:
                    pe.wait_ge(s["wsplit"], 2)
                    pe.wait_ge(s["h1_lo_ready"], n1.done())
                bank = use(bank, f"{name}_evac", n1.done())
                for m in range(KD):
                    cols = slice(m * P, (m + 1) * P)
                    if name == "v":
                        ins = products(bank[:, m], [((h1_hi[:, k, cols], h1_lo[:, k, cols]),
                                                     (w_hi[:, i, k], w_lo[:, i, k])) for k in range(KD)])
                    else:
                        ins = products(bank[:, m], [((w_hi[:, i, k, cols], w_lo[:, i, k, cols]),
                                                     (h1_hi[:, k], h1_lo[:, k])) for k in range(KD)])
                ins.then_inc(s[f"{name}_ready"], 1)

            def step(n0, n1, n2, n3, n4, n5):
                for i in range(H):
                    if n2:
                        scores1(n2, i)
                    if n3 and i == 0:
                        transpose_max(n3, 3)
                    if n1 and i == 0:
                        pe.wait_ge(s["z_ready"], n1.done())
                        transposes(use(1, "h1_ready", n1.done()), z).then_inc(s["zT_ready"], 1)
                    if n4 and i == 2:
                        pe.wait_ge(s["o_lo_ready"], n4.done(2))
                        ge(pe, s["wo_split"], 2)
                        bank = use(0, "att_evac", n4.done())
                        for m in range(KD):
                            cols = slice(m * P, (m + 1) * P)
                            ins = products(bank[:, m], [((wo_hi[:, a, cols], wo_lo[:, a, cols]),
                                                         (o_hi[:, a], o_lo[:, a])) for a in range(NHG)])
                        ins.then_inc(s["att_ready"], 1)
                    if n3 and i in (3, 7, 11):
                        pv(n3, i // 4 + 1)
                    if n2 and i in (4, 8, 12):
                        transpose_max(n2, i // 4 - 1)
                    if n1 and i == 4:
                        project(n1, 0, "q", 0)
                    if n1 and i == 5:
                        project(n1, 1, "k", 1)
                    if n4 and i == 5:
                        pe.wait_ge(s["att_evac"], n4.done())
                        transposes(use(0, "x1_ready", n4.done()), att).then_inc(s["attT_ready"], 1)
                    if n4 and i == 12:
                        pe.wait_ge(s["z2_ready"], n4.done())
                        transposes(use(1, "h2_ready", n4.done()), z2).then_inc(s["z2T_ready"], 1)
                    if n1 and i == 13:
                        project(n1, 2, "v", 0)
                    if n5 and i == 13:
                        pe.wait_ge(s["comb_ready"], n5.done())
                        bank = use(1, "combT_evac", n5.done())
                        for j in range(TT):
                            ins = t.transpose(bank[0:E].rearrange("p a c -> p (a c)")[:, j * P:(j + 1) * P],
                                              comb[:, j], ident[:])
                        ins.then_inc(s["combT_ready"], 1)
                    if i < LAG and n3:
                        scores2(n3, i + H - LAG)
                    if i >= LAG and n2:
                        scores2(n2, i - LAG)
                    if n4 and i == 15:
                        pe.wait_ge(s["h2_ready"], n4.done())
                        bank = use(0, "g_exp_done", n4.done())
                        for j in range(TT):
                            for k in range(KD):
                                ins = t.matmul(bank[:, 0, j * E:(j + 1) * E], h2[:, k, j * P:(j + 1) * P], gw[:, k],
                                               start=k == 0, stop=k == KD - 1)
                        ins.then_inc(s["logits"], 1)
                    if n2 and i == 15:
                        pv(n2, 0)

            def loop_begins(n0, n1, n2, n3, n4, n5):
                last[:] = (s["g_exp_done"], n5.n + 1), (s["combT_evac"], n5.n)

            def loop_ends(n0, n1, n2, n3, n4, n5):
                last[:] = (s["g_exp_done"], n4.n + 1), (s["combT_evac"], n5.n + 1)

            steps(pe.Fori, step, loop_begins, loop_ends)


def ffn(nc, wall, h2_dram, x1_dram, cw_dram, gate2, out):
    ctx = ExitStack()
    with ctx:
        def sb(name, shape, dt=F32):
            return ctx.enter_context(nc.sbuf_tensor(name, shape, dt))

        def sem(name):
            return ctx.enter_context(nc.semaphore(name))

        NP = FT // 2
        GU = 2 * KD * P
        CT = CH // P
        ident = sb("ident_f", [P, P])
        w_sb = sb("w_sb", [P, FT + 1, WCOL])
        gu_hi = sb("gu_hi", [P, 2, GU], F32R)
        gu_lo = sb("gu_lo", [P, 2, GU], F32R)
        wd_hi = sb("wd_hi", [P, 2, D], F32R)
        wd_lo = sb("wd_lo", [P, 2, D], F32R)
        h = sb("h_in", [P, KD, CH])
        h_hi = sb("h_hi", [P, 2, KD, CH], F32R)
        h_lo = sb("h_lo", [P, 2, KD, CH], F32R)
        cw = sb("cw", [P, 2, CH])
        sg = sb("silu_g", [P, 2, CH])
        sw = sb("silu_gw", [P, 2, CH])
        a32 = sb("act32", [P, 2, CH])
        a_hi = sb("a_hi", [P, 2, CH], F32R)
        a_lo = sb("a_lo", [P, 2, CH], F32R)
        gy = sb("gate_y", [P, 2, KD])
        y_sb = sb("y_sb", [P, KD, CH])
        x1 = sb("x1_in", [P, CT, D])
        o_sb = sb("out_sb", [P, CT, D])
        ps_g = [ctx.enter_context(nc.psum_tensor(f"ps_g{i}", [P, CH], F32)) for i in range(2)]
        ps_u = [ctx.enter_context(nc.psum_tensor(f"ps_u{i}", [P, CH], F32)) for i in range(2)]
        ps_y = [ctx.enter_context(nc.psum_tensor(f"ps_y{i}", [P, KD, CH], F32)) for i in range(2)]
        names = """ident_zero_f ident_done_f h_loaded x1_loaded h_hi_done h_lo_done gy_done y_done y_evac yT_ready
            out_ready out_stored pool_apart_f""".split()
        s = {n: sem(n) for n in names}
        per_slot = "cw_loaded gu_hi_done gu_lo_done wd_hi_done wd_lo_done g_ready u_ready silu_done sw_done " \
                   "act_done a_hi_done a_lo_done down_done"
        s |= {n: [sem(f"{n}{i}") for i in range(2)] for n in per_slot.split()}
        w_loaded = [sem(f"w_loaded{i}") for i in range(3)]
        LOADS = ((0, 1), (1, 6), (6, FT + 1))
        block = ctx.enter_context(nc.Block())

        def chunks(fori, pair_of_tiles, between):
            def chunk(c, p):
                for jj in range(2):
                    pair_of_tiles(c, p, jj, c * NP + jj)
                between(c, p)
                with fori(2, NP) as jj:
                    pair_of_tiles(c, p, jj, c * NP + jj)

            for c in (0, 1):
                chunk(c, c)
            with fori(1, NCH // 2 - 1) as i:
                for p in range(2):
                    chunk(2 * i + p, p)
            for c in (NCH - 2, NCH - 1):
                chunk(c, c % 2)

        def tile(j):
            if isinstance(j, int):
                return w_sb[:, j]
            return w_sb[:, bass.ds(j, 1)].rearrange("p a c -> p (a c)")

        def first(c):
            return isinstance(c, int) and c == 0

        def weights_there(eng, jj):
            if isinstance(jj, int) and jj < 2:
                eng.wait_ge(w_loaded[1], 16)
            else:
                eng.wait_ge(w_loaded[2], 16)

        @block.sync
        def _(sp):
            def load_h(c):
                ge(sp, s["h_lo_done"], c)
                sp.dma_start(h[:], h2_dram[:, :, bass.ds(c * CH, CH)].rearrange("k p c -> p k c"))\
                    .then_inc(s["h_loaded"], 16)

            def pair_of_tiles(c, p, jj, k):
                for r in range(2):
                    ge(sp, s["sw_done"][r], k)
                    sp.dma_start(cw[:, r], cw_dram[bass.ds(8 * jj + 4 * r, 4), bass.ds(c * CH, CH)]
                                 .unsqueeze(1).broadcast_to([4, REP, CH])).then_inc(s["cw_loaded"][r], 16)

            def between(c, p):
                if not first(c):
                    ge(sp, s["out_ready"], c - 1)
                    sp.dma_start(x1[:], token_tiles(x1_dram, c - 1)).then_inc(s["x1_loaded"], 16)
                    store(c - 1)
                if not (isinstance(c, int) and c == NCH - 1):
                    load_h(c + 1)

            def token_tiles(dram, c):
                return dram.rearrange("b (t p) d -> p (b t) d", p=P)[:, bass.ds(c * CT, CT)]

            def store(c):
                sp.wait_ge(s["out_ready"], c + 1)
                sp.dma_start(token_tiles(out, c), o_sb[:]).then_inc(s["out_stored"], 16)

            load_h(0)
            for i, (j0, j1) in enumerate(LOADS):
                sp.dma_start(w_sb[:, j0:j1], wall[j0:j1].rearrange("j p c -> p j c")).then_inc(w_loaded[i], 16)
            chunks(sp.Fori, pair_of_tiles, between)
            sp.wait_ge(s["out_ready"], NCH - 1)
            sp.dma_start(x1[:], token_tiles(x1_dram, NCH - 1)).then_inc(s["x1_loaded"], 16)
            store(NCH - 1)
            sp.wait_ge(s["out_stored"], 16 * NCH)

        @block.gpsimd
        def _(pool):
            g = nc.gpsimd
            g.memset(ident[:], 0.0).then_inc(s["ident_zero_f"], 1)
            pool.wait_ge(s["ident_zero_f"], 1)
            g.affine_select(out=ident[:], in_=ident[:], compare_op=ALU.not_equal, fill=1.0, base=0,
                            pattern=[[-1, P]], channel_multiplier=1).then_inc(s["ident_done_f"], 1)

            def pair_of_tiles(c, p, jj, k):
                for r in range(2):
                    pool.wait_ge(s["silu_done"][r], k + 1)
                    pool.wait_ge(s["cw_loaded"][r], (k + 1) * 16)
                    ge(pool, s["act_done"][r], k)
                    g.tensor_tensor(sw[:, r], sg[:, r], cw[:, r], ALU.mult).then_inc(s["sw_done"][r], 1)

            def between(c, p):
                wait_apart(pool, s["y_evac"], c * 4, s["pool_apart_f"])
                g.tensor_copy(gy[:], gate2[:, bass.ds(2 * c, 2)]).then_inc(s["gy_done"], 1)

            chunks(pool.Fori, pair_of_tiles, between)

        @block.scalar
        def _(act):
            a = nc.scalar
            act.wait_ge(w_loaded[0], 16)
            a.activation(gu_hi[:, 0], w_sb[:, 0, 0:GU], ACT.Copy).then_inc(s["gu_hi_done"][0], 1)

            def pair_of_tiles(c, p, jj, k):
                if first(c):
                    weights_there(act, jj)
                for r in range(2):
                    j = 2 * jj + r
                    act.wait_ge(s["g_ready"][r], k + 1)
                    ge(act, s["sw_done"][r], k)
                    a.activation(sg[:, r], ps_g[r][:], ACT.Silu).then_inc(s["silu_done"][r], 1)
                    ge(act, s["u_ready"][1 - r], k + r)
                    ge(act, s["gu_lo_done"][1 - r], k + r)
                    a.activation(gu_hi[:, 1 - r], tile(j + 1)[:, 0:GU], ACT.Copy).then_inc(s["gu_hi_done"][1 - r], 1)
                    ge(act, s["down_done"][r], k)
                    a.activation(wd_hi[:, r], tile(j)[:, GU:WCOL], ACT.Copy).then_inc(s["wd_hi_done"][r], 1)
                    act.wait_ge(s["act_done"][r], k + 1)
                    a.activation(a_hi[:, r], a32[:, r], ACT.Copy).then_inc(s["a_hi_done"][r], 1)

            def between(c, p):
                if not first(c):
                    evacuate(c - 1, 1 - p)

            def evacuate(c, p):
                act.wait_ge(s["y_done"], c + 1)
                act.wait_ge(s["gy_done"], c + 1)
                ge(act, s["yT_ready"], c)
                for m in range(KD):
                    for b in range(2):
                        a.activation(y_sb[:, m, b * S:(b + 1) * S], ps_y[p][:, m, b * S:(b + 1) * S], ACT.Copy,
                                     scale=gy[:, b, m:m + 1]).then_inc(s["y_evac"], 1)

            chunks(act.Fori, pair_of_tiles, between)
            evacuate(NCH - 1, 1)

        @block.vector
        def _(dve):
            v = nc.vector

            def split_h(c, p):
                dve.wait_ge(s["h_loaded"], (c + 1) * 16)
                ge(dve, s["u_ready"][1], (c - 1) * NP)
                v.tensor_copy(h_hi[:, p], h[:]).then_inc(s["h_hi_done"], 1)
                dve.wait_ge(s["h_hi_done"], c + 1)
                v.tensor_tensor(h_lo[:, p], h[:], h_hi[:, p].bitcast(F32), ALU.subtract).then_inc(s["h_lo_done"], 1)

            def gu_low(slot, j, k):
                dve.wait_ge(s["gu_hi_done"][slot], k + 1)
                ge(dve, s["u_ready"][slot], k)
                v.tensor_tensor(gu_lo[:, slot], tile(j)[:, 0:GU], gu_hi[:, slot].bitcast(F32), ALU.subtract)\
                    .then_inc(s["gu_lo_done"][slot], 1)

            split_h(0, 0)
            dve.wait_ge(w_loaded[0], 16)
            gu_low(0, 0, 0)

            def pair_of_tiles(c, p, jj, k):
                if first(c):
                    weights_there(dve, jj)
                for r in range(2):
                    j = 2 * jj + r
                    gu_low(1 - r, j + 1, k + r)
                    dve.wait_ge(s["u_ready"][r], k + 1)
                    dve.wait_ge(s["sw_done"][r], k + 1)
                    ge(dve, s["a_lo_done"][r], k)
                    v.tensor_tensor(a32[:, r], ps_u[r][:], sw[:, r], ALU.mult).then_inc(s["act_done"][r], 1)
                    dve.wait_ge(s["wd_hi_done"][r], k + 1)
                    v.tensor_tensor(wd_lo[:, r], tile(j)[:, GU:WCOL], wd_hi[:, r].bitcast(F32), ALU.subtract)\
                        .then_inc(s["wd_lo_done"][r], 1)
                    dve.wait_ge(s["a_hi_done"][r], k + 1)
                    v.tensor_tensor(a_lo[:, r], a32[:, r], a_hi[:, r].bitcast(F32), ALU.subtract)\
                        .then_inc(s["a_lo_done"][r], 1)

            def between(c, p):
                if not first(c):
                    finish(c - 1, 1 - p)
                if not (isinstance(c, int) and c == NCH - 1):
                    split_h(c + 1, 1 - p)

            def finish(c, p):
                dve.wait_ge(s["yT_ready"], c + 1)
                dve.wait_ge(s["x1_loaded"], (c + 1) * 16)
                ge(dve, s["out_stored"], c * 16)
                v.tensor_tensor(o_sb.rearrange("p t d -> p (t d)"), ps_y[p][:].rearrange("p m c -> p (m c)"),
                                x1[:].rearrange("p t d -> p (t d)"), ALU.add).then_inc(s["out_ready"], 1)

            chunks(dve.Fori, pair_of_tiles, between)
            finish(NCH - 1, 1)

        @block.tensor
        def _(pe):
            t = nc.tensor

            def products(out, pairs, start=True, stop=True):
                terms = [(a, b) for (ah, al), (bh, bl) in pairs for a, b in ((ah, bh), (ah, bl), (al, bh))]
                for i, (a, b) in enumerate(terms):
                    ins = t.matmul(out, a, b, start=start and i == 0, stop=stop and i == len(terms) - 1,
                                   skip_group_check=not (start and stop))
                return ins

            def gate_up(c, p, r, k):
                pe.wait_ge(s["gu_lo_done"][r], k + 1)
                for which, (ps, used, ready) in enumerate(((ps_g[r], "silu_done", "g_ready"),
                                                           (ps_u[r], "act_done", "u_ready"))):
                    ge(pe, s[used][r], k)
                    cols = [slice((2 * which + i) * P, (2 * which + i + 1) * P) for i in range(KD)]
                    products(ps[:], [((gu_hi[:, r, cols[i]], gu_lo[:, r, cols[i]]), (h_hi[:, p, i], h_lo[:, p, i]))
                                     for i in range(KD)]).then_inc(s[ready][r], 1)

            def down(p, r, k, start=False, stop=False):
                pe.wait_ge(s["a_lo_done"][r], k + 1)
                pe.wait_ge(s["wd_lo_done"][r], k + 1)
                for m in range(KD):
                    cols = slice(m * P, (m + 1) * P)
                    ins = products(ps_y[p][:, m], [((wd_hi[:, r, cols], wd_lo[:, r, cols]),
                                                    (a_hi[:, r], a_lo[:, r]))], start, stop)
                ins.then_inc(s["down_done"][r], 1)
                return ins

            def last_down(c, p, r):
                down(p, r, c * NP + NP - 1, stop=r == 1)

            def pair_of_tiles(c, p, jj, k):
                for r in range(2):
                    if r == 0 and isinstance(jj, int) and jj == 0:
                        pe.wait_ge(s["h_lo_done"], c + 1)
                    gate_up(c, p, r, k)
                    if isinstance(jj, int) and jj == 0:
                        if not first(c):
                            last_down(c - 1, 1 - p, r)
                            if r == 1:
                                pe.wait_ge(s["down_done"][1], c * NP)
                                pe.sem_inc(s["y_done"], 1)
                    else:
                        if r == 0 and isinstance(jj, int) and jj == 1:
                            ge(pe, s["out_ready"], c - 1)
                        down(p, r, k - 1, start=isinstance(jj, int) and jj == 1 and r == 0)

            def between(c, p):
                if not first(c):
                    transpose_y(c - 1, 1 - p)

            def transpose_y(c, p):
                pe.wait_ge(s["y_evac"], (c + 1) * 4)
                flat = ps_y[p][:].rearrange("p m c -> p (m c)")
                for i in range(CT):
                    for m in range(KD):
                        ins = t.transpose(flat[:, i * D + m * P:i * D + (m + 1) * P], y_sb[:, m, i * P:(i + 1) * P],
                                          ident[:])
                ins.then_inc(s["yT_ready"], 1)

            pe.wait_ge(s["ident_done_f"], 1)
            chunks(pe.Fori, pair_of_tiles, between)
            for r in range(2):
                last_down(NCH - 1, 1, r)
            pe.wait_ge(s["down_done"][1], NCH * NP)
            pe.sem_inc(s["y_done"], 1)
            transpose_y(NCH - 1, 1)


def program(nc, x, cT, wmod, wqT, wkT, wvT, woT, bq, bk, bv, bo, spiral, helix, gate_w, wall, out):
    h2_dram = nc.dram_tensor("h2_scratch", [KD, P, TOK], F32, kind="Internal").ap()
    x1_dram = nc.dram_tensor("x1_scratch", [B, S, D], F32, kind="Internal").ap()
    cw_dram = nc.dram_tensor("cw_scratch", [4 * FT, TOK], F32, kind="Internal").ap()
    qk_dram = nc.dram_tensor("qk_scratch", [2, 2, 2, D, S], F32, kind="Internal").ap()
    max_dram = nc.dram_tensor("max_scratch", [NG, 2, HG, S], F32, kind="Internal").ap()
    with nc.sbuf_tensor("gate2", [P, B, KD], F32) as gate2:
        attention(nc, x, cT, wmod, wqT, wkT, wvT, woT, bq, bk, bv, bo, spiral, helix, gate_w, h2_dram, x1_dram,
                  cw_dram, qk_dram, max_dram, gate2)
        ffn(nc, wall, h2_dram, x1_dram, cw_dram, gate2, out)


def kernel(**inputs):
    import concourse.bacc as bacc
    from concourse.bass_utils import run_bass_kernel_spmd

    a = {k.removeprefix("L0_"): np.asarray(v) for k, v in inputs.items()}

    def halves(vector):
        return vector.reshape(KD, P).T

    def features(experts, shared):
        both = np.concatenate([experts.transpose(1, 0, 2).reshape(D, E * FE), shared], 1)
        both = np.pad(both, ((0, 0), (0, FT * P - both.shape[1])))
        return both.reshape(KD, P, FT, P).transpose(2, 1, 0, 3).reshape(FT, P, KD * P)

    down = np.pad(np.concatenate([a["ffn_wd"].reshape(E * FE, D), a["ffn_sd"]], 0), ((0, FT * P - E * FE - FS), (0, 0)))
    wall = np.concatenate([features(a["ffn_wg"], a["ffn_sg"]), features(a["ffn_wu"], a["ffn_su"]),
                           down.reshape(FT, P, D)], 2)
    wall = np.concatenate([wall, wall[:1]], 0)
    data = {
        "x": a["attn_x"], "cT": a["c"].T, "wmod": a["wmod"], "wqT": a["attn_Wq"].T, "wkT": a["attn_Wk"].T,
        "wvT": a["attn_Wv"].T, "woT": a["attn_Wo"].T, "bq": halves(a["attn_bq"]), "bk": halves(a["attn_bk"]),
        "bv": a["attn_bv"], "bo": halves(a["attn_bo"]), "spiral": halves(np.repeat(a["attn_spiral_weight"], DH)),
        "helix": halves(a["attn_helix_rotation"]),
        "gate_w": a["ffn_gate_w"], "wall": wall,
    }
    data = {k: np.ascontiguousarray(v) for k, v in data.items()}
    nc = bacc.Bacc("TRN2", target_bir_lowering=False, num_devices=1)
    args = [nc.dram_tensor(f"in_{k}", v.shape, mybir.dt.from_np(v.dtype), kind="ExternalInput").ap()
            for k, v in data.items()]
    out = nc.dram_tensor("out", (B, S, D), F32, kind="ExternalOutput").ap()
    program(nc, *args, out)
    r = run_bass_kernel_spmd(nc, [{f"in_{k}": v for k, v in data.items()}], core_ids=[0])
    return r.results[0]["out"]
```

```python
from contextlib import ExitStack

import numpy as np

import concourse.bass as bass
from concourse import mybir

F32 = mybir.dt.float32
F32R = mybir.dt.float32r
I32 = mybir.dt.int32
U32 = mybir.dt.uint32
ACT = mybir.ActivationFunctionType
ALU = mybir.AluOpType
AX = mybir.AxisListType

B, S, D = 16, 256, 256
H, DH = 16, 16
P = 128
KD = D // P
TT = S // P
HG = 4
NHG = NG = H // HG
LAG = 10
TOK = B * S
E, FE, FS, TOPK = 32, 96, 192, 6
FT = (E * FE + FS + P - 1) // P
WCOL = 2 * KD * P + D
REP = 32
CH = 512
NCH = TOK // CH
EPS = 1e-5
TWO_PI = float(2 * np.pi)
ROUND = 12582912.0

PART_ROWS = (0, 48)
MAX_ROW = 32
STACK = 80
MAX_BANK = (1, 0, 1, 2)

LN_SHIFT1, LN_SCALE1, GATE1, LN_SHIFT2, LN_SCALE2, GATE2 = 0, 2, 4, 6, 8, 10


def ge(eng, sem, value):
    if isinstance(value, int) and value <= 0:
        return
    eng.wait_ge(sem, value)


def wait_apart(eng, sem, value, waits_apart):
    ge(eng, sem, value)
    if not isinstance(value, int):
        eng.sem_inc(waits_apart, 1)


class Batch:

    def __init__(self, n, pair, parity):
        self.n, self.pair, self.p = n, pair, parity

    def done(self, per=1, k=None):
        return self.n * per + (per if k is None else k)


def steps(fori, body, loop_begins=None, loop_ends=None):
    def batches(t, i=None):
        out = []
        for n in range(t + 1, t - 5, -1):
            if i is None:
                out.append(Batch(n, n // 2, n % 2) if 0 <= n < B else None)
            else:
                out.append(Batch(2 * i + n, i + n // 2, n % 2))
        return out + [Batch(t + 1 if i is None else 2 * i + t + 1, None, None)]

    for t in range(-1, 5):
        body(*batches(t))
    with fori(0, 5) as i:
        for t in (5, 6):
            if loop_begins:
                loop_begins(*batches(t, i))
            body(*batches(t, i))
    if loop_ends:
        loop_ends(*batches(14))
    for t in range(15, 20):
        body(*batches(t))


def attention(nc, x, cT, wmod, wqT, wkT, wvT, woT, bq, bk, bv, bo, spiral, helix, gate_w, h2_dram, x1_dram, cw_dram,
              qk_dram, max_dram, gate2):
    ctx = ExitStack()
    with ctx:
        def sb(name, shape, dt=F32):
            return ctx.enter_context(nc.sbuf_tensor(name, shape, dt))

        def sem(name):
            return ctx.enter_context(nc.semaphore(name))

        ident = sb("ident", [P, P])
        iota_i = sb("iota_i", [P, E], I32)
        iota = sb("iota", [P, E])
        cT_sb = sb("cT_sb", [P, KD, B])
        c_exp = sb("c_exp", [P, KD, B])
        mod = sb("mod", [P, B, 12])
        mod_t = sb("mod_t", [P, B, 12])
        w_hi = sb("w_hi", [P, 4, KD, D], F32R)
        w_lo = sb("w_lo", [P, 4, KD, D], F32R)
        w_raw = sb("w_raw", [P, 4, KD, D])
        bias_qk = sb("bias_qk", [P, 2, KD])
        bo_sb = sb("bo_sb", [P, KD])
        bv_row = sb("bv_row", [P, D])
        spi = sb("spi", [P, KD])
        rot = sb("rot", [P, 2, KD])
        rot_t = sb("rot_t", [P, 2, KD])
        trig = sb("trig", [P, 2, KD])
        bias_s = sb("bias_s", [P, 2, KD])
        gw = sb("gw", [P, KD, E])
        ones_blk = sb("ones_blk", [8, CH])
        zero_blk = sb("zero_blk", [2, S], F32R)
        xs = sb("xs", [P, 2, TT, D])
        stats = sb("stats", [P, 2 * TT, 6])
        mv = sb("mv", [P, 2 * TT, 2])
        rs = sb("rs", [P, 2 * TT])
        nt = sb("nt", [P, 3, 2 * TT])
        z = sb("z", [P, TT, D])
        h1 = sb("h1", [P, KD, S])
        h1_hi = sb("h1_hi", [P, KD, S], F32R)
        h1_lo = sb("h1_lo", [P, KD, S], F32R)
        qk = sb("qk", [P, 2, KD, S])
        qk_hi = sb("qk_hi", [P, 2, KD, S], F32R)
        qk_lo = sb("qk_lo", [P, 2, KD, S], F32R)
        q_st = sb("q_st", [P, 2, H, S], F32R)
        k_st = sb("k_st", [P, 2, H, S], F32R)
        v_aug = sb("v_aug", [P, 2, TT, H, 2 * DH])
        mx = sb("mx", [P, TT, H])
        nmx = sb("nmx", [HG, NG, 2, S], F32R)
        pt = sb("pt", [P, 8, TT, S])
        o_sb = sb("o_sb", [P, NHG, S])
        o_inv = sb("o_inv", [P, TT, 2, HG])
        o_n = sb("o_n", [P, TT, D])
        o_hi = sb("o_hi", [P, KD, S], F32R)
        o_lo = sb("o_lo", [P, KD, S], F32R)
        wmod_sb = pt[:].rearrange("p a b c -> p (a b c)")[:, 0:KD * 6 * D].rearrange("p (k n) -> p k n", k=KD)
        cm1 = sb("cm1", [P, 2, 12])
        cm4 = sb("cm4", [P, 2, 14])
        att = sb("att", [P, KD, S])
        x4 = sb("x4", [P, TT, D])
        x1 = sb("x1", [P, TT, D])
        z2 = sb("z2", [P, TT, D])
        h2 = sb("h2", [P, KD, S])
        g_exp = sb("g_exp", [P, TT, E])
        sc1 = sb("sc1", [P, TT, E])
        sc = sb("sc", [P, TT, E])
        top = sb("top", [P, TT, 8])
        top_i = sb("top_i", [P, TT, 8], U32)
        top_f = sb("top_f", [P, TT, 8])
        eq = sb("eq", [P, TT, E, TOPK])
        mask = sb("mask", [P, TT, E])
        kept = sb("kept", [P, TT, E])
        ksum = sb("ksum", [P, TT])
        kinv = sb("kinv", [P, TT])
        comb = sb("comb", [P, TT, E])
        combT = sb("combT", [E, S])

        ps1 = [ctx.enter_context(nc.psum_tensor(f"ps1_{i}", [P, TT, S], F32)) for i in range(2)]
        ps2 = [ctx.enter_context(nc.psum_tensor(f"ps2_{i}", [P, TT, S], F32)) for i in range(2)]
        ps_o = ctx.enter_context(nc.psum_tensor("ps_o", [P, 2, S], F32))
        ps_m = [ctx.enter_context(nc.psum_tensor(f"ps_m{i}", [P, 2, 256], F32)) for i in range(3)]

        names = """c_loaded mod_loaded w_loaded b_loaded ident_zero ident_done iota_int iota_done
            c_exp_done silu_c mod_ready mod_done mod_step rot_step trig_done wsplit bias_done blocks_set
            zeros_set consts_stored stack_init moments_set
            ln_stats ln_aggr half_v seed rstd z_ready zT_ready h1_ready h1_lo_ready
            q_ready k_ready q_evac k_evac qk_split qk_stored v_ready v_evac
            scores1 max_done mxT_ready nmx_hi nmx_ready scores2 probs pv_done o_evac
            oT_ready o_recip o_norm oF_ready o_hi_ready o_lo_ready
            att_ready att_evac attT_ready x1_ready z2_ready z2T_ready h2_ready
            logits g_exp_done sc1_done sc_done top_done idx_done idxf_done eq_done mask_done kept_done ksum_done
            keps_done kinv_done comb_ready combT_ready combT_evac
            cm1_ready cm4_ready x4_loaded x1_stored h2_stored comb_stored pool_apart dve_apart sp_apart""".split()
        s = {n: sem(n) for n in names}
        x_loaded = [sem(f"x_loaded{i}") for i in range(2)]
        stacked = [[sem(f"stacked{i}{m}") for m in range(KD)] for i in range(2)]
        max_stored = [sem(f"max_stored{i}") for i in range(NG)]
        max_rows = [sem(f"max_rows{i}") for i in range(NG)]
        block = ctx.enter_context(nc.Block())

        STACK_LOADS = 16 * (2 * len(PART_ROWS) + 1)

        @block.sync
        def _(sp):
            sp.dma_start(cT_sb[:], cT.rearrange("(k p) b -> p k b", p=P)).then_inc(s["c_loaded"], 16)
            sp.dma_start(wmod_sb, wmod.rearrange("(k p) n -> p k n", p=P)).then_inc(s["mod_loaded"], 16)
            for i, w in enumerate((wqT, wkT, wvT, woT)):
                sp.dma_start(w_raw[:, i], w.rearrange("(k p) n -> p k n", p=P)).then_inc(s["w_loaded"], 16)
            sp.dma_start(bias_qk[:, 0], bq).then_inc(s["b_loaded"], 16)
            sp.dma_start(bias_qk[:, 1], bk).then_inc(s["b_loaded"], 16)
            sp.dma_start(bo_sb[:], bo).then_inc(s["b_loaded"], 16)
            sp.dma_start(spi[:], spiral).then_inc(s["b_loaded"], 16)
            sp.dma_start(rot[:, 1], helix).then_inc(s["b_loaded"], 16)
            sp.dma_start(bv_row[:], bv.partition_broadcast(P)).then_inc(s["b_loaded"], 16)
            sp.dma_start(gw[:], gate_w.rearrange("(k p) e -> p k e", p=P)).then_inc(s["b_loaded"], 16)
            sp.wait_ge(s["blocks_set"], 1)
            sp.dma_start(cw_dram[3 * E:3 * E + 8].rearrange("r (a c) -> r a c", c=CH),
                         ones_blk[:].unsqueeze(1).broadcast_to([8, NCH, CH])).then_inc(s["consts_stored"], 16)

            def step(n0, n1, n2, n3, n4, n5, m):
                if n0:
                    ge(sp, s["z_ready"], n0.n - 1)
                    sp.dma_start(xs[:, n0.p], tokens(x, n0)).then_inc(x_loaded[n0.p], 16)
                if n4:
                    ge(sp, s["x1_ready"], n4.n)
                    sp.dma_start(x4[:], tokens(x, n4)).then_inc(s["x4_loaded"], 16)
                if n1:
                    for m in range(KD):
                        wait_apart(sp, stacked[n1.p][m], n1.pair * STACK_LOADS, s["sp_apart"])
                    for i in range(2):
                        sp.wait_ge(s["qk_split"], n1.done(2, i + 1))
                        for j, part in enumerate((qk_hi, qk_lo)):
                            for k in range(KD):
                                sp.dma_start(qk_dram[n1.p, i, j, :, 8 * k:8 * k + 8].rearrange("d h c -> h d c"),
                                             part[:, i, k].bitcast(F32)).then_inc(s["qk_stored"], 16)
                if n4:
                    sp.wait_ge(s["x1_ready"], n4.done())
                    sp.dma_start(tokens(x1_dram, n4), x1[:]).then_inc(s["x1_stored"], 16)
                if n1:
                    ge(sp, s["stack_init"], 4)
                    ge(sp, s["zeros_set"], 1)
                    sp.wait_ge(s["qk_stored"], n1.done(128))
                    for m in range(KD):
                        ge(sp, s["scores2"], (n1.n - 1) * H - H // KD * (KD - 1 - m))
                        heads = slice(m * 8, (m + 1) * 8)
                        sp.dma_start(q_st[MAX_ROW:MAX_ROW + 2, n1.p, heads].bitcast(F32),
                                     zero_blk[:].bitcast(F32).unsqueeze(1).broadcast_to([2, 8, S]))\
                            .then_inc(stacked[n1.p][m], 16)
                        q_parts = qk_dram[n1.p, 0, :, :, heads].rearrange("j d h c -> (j d) (h c)")
                        for r0 in PART_ROWS:
                            sp.dma_start(q_st[r0:r0 + 2 * DH, n1.p, heads].bitcast(F32), q_parts)\
                                .then_inc(stacked[n1.p][m], 16)
                        for j, r0 in enumerate(PART_ROWS):
                            k_part = qk_dram[n1.p, 1, j, :, heads].rearrange("d h c -> d (h c)")
                            sp.dma_start(k_st[r0:r0 + 2 * DH, n1.p, heads].bitcast(F32),
                                         k_part.unsqueeze(0).broadcast_to([2, DH, 8 * S]))\
                                .then_inc(stacked[n1.p][m], 16)
                if n4:
                    sp.wait_ge(s["h2_ready"], n4.done())
                    sp.dma_start(h2_dram[:, :, bass.ds(n4.n * S, S)].rearrange("k p c -> p k c"), h2[:])\
                        .then_inc(s["h2_stored"], 16)
                if n5:
                    sp.wait_ge(s["combT_evac"], n5.done())
                    for r in range(FE // REP):
                        sp.dma_start(cw_dram[0:3 * E, bass.ds(n5.n * S, S)].rearrange("(e r) c -> e r c", r=3)[:, r],
                                     combT[:]).then_inc(s["comb_stored"], 16)

            def tokens(dram, n):
                return dram[bass.ds(n.n, 1)].rearrange("a (t p) d -> p (a t) d", p=P)

            steps(sp.Fori, step)
            sp.wait_ge(s["consts_stored"], 16)
            sp.wait_ge(s["x1_stored"], 16 * B)
            sp.wait_ge(s["h2_stored"], 16 * B)
            sp.wait_ge(s["comb_stored"], 48 * B)

        @block.gpsimd
        def _(pool):
            g = nc.gpsimd
            g.memset(ident[:], 0.0).then_inc(s["ident_zero"], 1)
            pool.wait_ge(s["ident_zero"], 1)
            g.affine_select(out=ident[:], in_=ident[:], compare_op=ALU.not_equal, fill=1.0, base=0,
                            pattern=[[-1, P]], channel_multiplier=1).then_inc(s["ident_done"], 1)
            g.iota(iota_i[:], pattern=[[1, E]], base=0, channel_multiplier=0).then_inc(s["iota_int"], 1)
            pool.wait_ge(s["iota_int"], 1)
            g.memset(ones_blk[:], 1.0).then_inc(s["blocks_set"], 1)
            pool.wait_ge(s["blocks_set"], 1)
            g.memset(zero_blk[:].bitcast(F32), 0.0).then_inc(s["zeros_set"], 1)
            pool.wait_ge(s["zeros_set"], 1)
            g.memset(q_st[32:64].bitcast(F32), 0.0).then_inc(s["stack_init"], 1)
            pool.wait_ge(s["stack_init"], 1)
            g.memset(k_st[32:64].bitcast(F32), 0.0).then_inc(s["stack_init"], 1)
            pool.wait_ge(s["stack_init"], 2)
            g.memset(k_st[MAX_ROW:MAX_ROW + 2].bitcast(F32), 1.0).then_inc(s["stack_init"], 1)
            pool.wait_ge(s["stack_init"], 3)
            g.memset(v_aug[:], 1.0).then_inc(s["stack_init"], 1)
            g.tensor_copy(iota[:], iota_i[:]).then_inc(s["iota_done"], 1)

            def newton(m):
                wait_apart(pool, s["seed"], m.done(), s["pool_apart"])
                for i in range(3):
                    ops = ((nt[:, 1], rs[:], rs[:], None), (nt[:, 1], nt[:, 1], nt[:, 0], None),
                           (nt[:, 2], nt[:, 1], None, 1.5), (rs[:], rs[:], nt[:, 2], None))
                    for j, (o, a, b, c) in enumerate(ops):
                        if i or j:
                            wait_apart(pool, s["rstd"], m.n * 12 + 4 * i + j, s["pool_apart"])
                        if c is None:
                            g.tensor_tensor(o, a, b, ALU.mult).then_inc(s["rstd"], 1)
                        else:
                            g.tensor_scalar(o, a, c, None, ALU.add).then_inc(s["rstd"], 1)

            def step(n0, n1, n2, n3, n4, n5, m):
                if n1:
                    pool.wait_ge(s["h1_ready"], n1.done())
                    ge(pool, s["v_ready"], n1.n)
                    g.tensor_tensor(h1_lo[:], h1[:], h1_hi[:].bitcast(F32), ALU.subtract)\
                        .then_inc(s["h1_lo_ready"], 1)
                    for i, name in enumerate(("q_evac", "k_evac")):
                        pool.wait_ge(s[name], n1.done())
                        ge(pool, s["qk_stored"], n1.n * 128)
                        g.tensor_tensor(qk_lo[:, i], qk[:, i], qk_hi[:, i].bitcast(F32), ALU.subtract)\
                            .then_inc(s["qk_split"], 1)
                if n0 or n4:
                    newton(m)
                if n3:
                    ge(pool, s["mod_done"], 1)
                    wait_apart(pool, s["h2_ready"], n3.n - 1, s["pool_apart"])
                    g.tensor_copy(cm4[:, n3.p, 0:12], mod[:, bass.ds(n3.n, 1)].rearrange("p a c -> p (a c)"))\
                        .then_inc(s["cm4_ready"], 1)
                    pool.wait_ge(s["cm4_ready"], n3.done(2, 1))
                    g.tensor_tensor(cm4[:, n3.p, 12:14], cm4[:, n3.p, GATE1:GATE1 + 2], bo_sb[:], ALU.mult)\
                        .then_inc(s["cm4_ready"], 1)
                if n0:
                    ge(pool, s["mod_done"], 1)
                    wait_apart(pool, s["h1_ready"], n0.n - 1, s["pool_apart"])
                    g.tensor_copy(cm1[:, n0.p], mod[:, bass.ds(n0.n, 1)].rearrange("p a c -> p (a c)"))\
                        .then_inc(s["cm1_ready"], 1)

            steps(pool.Fori, step)

        @block.scalar
        def _(act):
            a = nc.scalar
            act.wait_ge(s["c_loaded"], 16)
            a.activation(c_exp[:], cT_sb[:], ACT.Exp, scale=-1.0).then_inc(s["c_exp_done"], 1)
            act.wait_ge(s["rot_step"], 6)
            a.activation(trig[:], rot[:], ACT.Sin).then_inc(s["trig_done"], 1)

            def affine(out, bank, scales, shifts):
                for k in range(KD):
                    ins = a.activation(out[:, k], bank[:, k], ACT.Identity, bias=shifts[:, k:k + 1],
                                       scale=scales[:, k:k + 1])
                return ins

            def step(n0, n1, n2, n3, n4, n5, m):
                if n5:
                    act.wait_ge(s["logits"], n5.done())
                    ge(act, s["sc1_done"], n5.n)
                    a.activation(g_exp[:], ps_m[1][:, 0, 0:TT * E].rearrange("p (t e) -> p t e", t=TT),
                                 ACT.Exp, scale=-1.0).then_inc(s["g_exp_done"], 1)
                if n1:
                    act.wait_ge(s["zT_ready"], n1.done())
                    act.wait_ge(s["cm1_ready"], n1.done())
                    ge(act, s["h1_lo_ready"], n1.n)
                    ge(act, s["v_ready"], n1.n)
                    for out in (h1, h1_hi):
                        ins = affine(out, ps_m[1], cm1[:, n1.p, LN_SCALE1:], cm1[:, n1.p, LN_SHIFT1:])
                    ins.then_inc(s["h1_ready"], 1)
                for i in range(H):
                    if n3 and i == 1:
                        store_max(n3, 3)
                    if n2 and i % 4 == 1 and i > 1:
                        store_max(n2, i // 4 - 1)
                    if n3 and i in (0, 4):
                        load_max(n3, 2 + i // 4)
                    if n2 and i % 4 == 0 and i > 4:
                        load_max(n2, i // 4 - 2)
                    if n4 and i == 1:
                        act.wait_ge(s["oF_ready"], n4.done())
                        ge(act, s["att_ready"], n4.n)
                        a.activation(o_hi[:], ps_m[0][:], ACT.Copy).then_inc(s["o_hi_ready"], 1)
                    if n4 and i == 4:
                        act.wait_ge(s["att_ready"], n4.done())
                        act.wait_ge(s["cm4_ready"], n4.done(2))
                        ge(act, s["attT_ready"], n4.n)
                        affine(att, ps_m[2], cm4[:, n4.p, GATE1:], cm4[:, n4.p, 12:]).then_inc(s["att_evac"], 1)
                    if n3 and i == 4:
                        o_copy(n3, 0)
                    if n1 and i in (5, 6):
                        j = i - 5
                        act.wait_ge(s["qk"[j] + "_ready"], n1.done())
                        ge(act, s["qk_split"], n1.n * 2 - 1 + j)
                        ge(act, s["qk_stored"], n1.n * 128)
                        ge(act, s["bias_done"], 1)
                        for out in (qk, qk_hi):
                            ins = affine(out[:, j], ps_m[j], trig[:, j], bias_s[:, j])
                        ins.then_inc(s["qk"[j] + "_evac"], 1)
                    if n3 and i == 12:
                        o_copy(n3, 1)
                    if n4 and i == 14:
                        act.wait_ge(s["z2T_ready"], n4.done())
                        ge(act, s["h2_stored"], n4.n * 16)
                        ge(act, s["logits"], n4.n)
                        affine(h2, ps_m[2], cm4[:, n4.p, LN_SCALE2:], cm4[:, n4.p, LN_SHIFT2:])\
                            .then_inc(s["h2_ready"], 1)
                    if n5 and i == 12:
                        act.wait_ge(s["combT_ready"], n5.done())
                        ge(act, s["comb_stored"], n5.n * 48)
                        a.activation(combT[:], ps_m[0][0:E].rearrange("p a c -> p (a c)")[:, 0:S], ACT.Copy)\
                            .then_inc(s["combT_evac"], 1)
                    if i < LAG and n3:
                        exp(n3, i + H - LAG)
                    if i >= LAG and n2:
                        exp(n2, i - LAG)

            def exp(n, h):
                act.wait_ge(s["scores2"], n.done(H, h + 1))
                ge(act, s["pv_done"], n.n * NHG + h // HG - 1)
                a.activation(pt[:, h % 8], ps2[h % 2][:], ACT.Exp).then_inc(s["probs"], 1)

            def o_copy(n, half):
                act.wait_ge(s["pv_done"], n.done(NHG, 2 * half + 2))
                ge(act, s["oT_ready"], n.n * 2 + half - 1)
                a.activation(o_sb[:, 2 * half:2 * half + 2], ps_o[:], ACT.Copy).then_inc(s["o_evac"], 1)

            def store_max(n, g):
                act.wait_ge(s["nmx_ready"], n.done(NG, g + 1))
                ge(act, max_rows[g], n.n * 16)
                act.dma_start(max_dram[g].rearrange("r j c -> j r c"), nmx[:, g].bitcast(F32))\
                    .then_inc(max_stored[g], 16)

            def load_max(n, g):
                act.wait_ge(max_stored[g], n.done(16))
                act.wait_ge(s["scores1"], n.done(H, HG * g + HG))
                act.dma_start(q_st[MAX_ROW:MAX_ROW + 2, n.p, HG * g:HG * g + HG].bitcast(F32), max_dram[g])\
                    .then_inc(max_rows[g], 16)

            steps(act.Fori, step)

        @block.vector
        def _(dve):
            v = nc.vector
            dve.wait_ge(s["c_exp_done"], 1)
            v.tensor_scalar(c_exp[:], c_exp[:], 1.0, None, ALU.add).then_inc(s["silu_c"], 1)
            dve.wait_ge(s["silu_c"], 1)
            v.reciprocal(c_exp[:], c_exp[:]).then_inc(s["silu_c"], 1)
            dve.wait_ge(s["silu_c"], 2)
            v.tensor_tensor(cT_sb[:], cT_sb[:], c_exp[:], ALU.mult).then_inc(s["silu_c"], 1)
            v.memset(mv[:], 1.0).then_inc(s["moments_set"], 1)
            dve.wait_ge(s["b_loaded"], 7 * 16)
            v.tensor_scalar(rot[:, 0], rot[:, 1], TWO_PI / 4, None, ALU.add).then_inc(s["rot_step"], 1)
            dve.wait_ge(s["rot_step"], 1)
            v.tensor_scalar(rot_t[:], rot[:], 1.0 / TWO_PI, ROUND, ALU.mult, ALU.add).then_inc(s["rot_step"], 1)
            dve.wait_ge(s["rot_step"], 2)
            v.tensor_scalar(rot_t[:], rot_t[:], ROUND, None, ALU.subtract).then_inc(s["rot_step"], 1)
            high = 6.28125
            dve.wait_ge(s["rot_step"], 3)
            v.scalar_tensor_tensor(out=rot[:], in0=rot_t[:], scalar=-high, in1=rot[:], op0=ALU.mult, op1=ALU.add)\
                .then_inc(s["rot_step"], 1)
            dve.wait_ge(s["rot_step"], 4)
            v.scalar_tensor_tensor(out=rot[:], in0=rot_t[:], scalar=-(TWO_PI - high), in1=rot[:], op0=ALU.mult,
                                   op1=ALU.add).then_inc(s["rot_step"], 1)
            dve.wait_ge(s["rot_step"], 5)
            v.tensor_scalar(rot[:], rot[:], 3.1415925, -3.1415925, ALU.min, ALU.max).then_inc(s["rot_step"], 1)
            dve.wait_ge(s["w_loaded"], 64)
            v.tensor_copy(w_hi[:], w_raw[:]).then_inc(s["wsplit"], 1)
            dve.wait_ge(s["wsplit"], 1)
            v.tensor_tensor(w_lo[:], w_raw[:], w_hi[:].bitcast(F32), ALU.subtract).then_inc(s["wsplit"], 1)
            dve.wait_ge(s["trig_done"], 1)
            v.scalar_tensor_tensor(out=trig[:, 0], in0=trig[:, 0], scalar=float(DH) ** -0.5, in1=spi[:],
                                   op0=ALU.mult, op1=ALU.mult).then_inc(s["trig_done"], 1)
            dve.wait_ge(s["trig_done"], 2)
            v.tensor_tensor(bias_s[:], bias_qk[:], trig[:], ALU.mult).then_inc(s["bias_done"], 1)
            dve.wait_ge(s["mod_ready"], 1)
            v.tensor_copy(mod[:], ps1[0][:].rearrange("p a c -> p (a c)")[:, 0:12 * B]
                          .rearrange("p (j b) -> p b j", b=B)).then_inc(s["mod_step"], 1)
            n = 1
            for col in (LN_SCALE1, LN_SCALE2):
                dve.wait_ge(s["mod_step"], n)
                v.tensor_scalar(mod[:, :, col:col + 2], mod[:, :, col:col + 2], 1.0, None, ALU.add)\
                    .then_inc(s["mod_step"], 1)
                n += 1
            for col in (GATE1, GATE2):
                gate, tmp = mod[:, :, col:col + 2], mod_t[:, :, col:col + 2]
                dve.wait_ge(s["mod_step"], n)
                v.scalar_tensor_tensor(out=tmp, in0=gate, scalar=-1.0, in1=gate, op0=ALU.mult, op1=ALU.max)\
                    .then_inc(s["mod_step"], 1)
                v.tensor_scalar(mod_t[:, :, 0:2], gate, 0.0, 2.0, ALU.is_ge, ALU.mult).then_inc(s["mod_step"], 1)
                dve.wait_ge(s["mod_step"], n + 2)
                v.tensor_scalar(tmp, tmp, 0.25, None, ALU.max).then_inc(s["mod_step"], 1)
                dve.wait_ge(s["mod_step"], n + 3)
                v.scalar_tensor_tensor(out=gate, in0=mod_t[:, :, 0:2], scalar=-1.0, in1=tmp, op0=ALU.add,
                                       op1=ALU.mult).then_inc(s["mod_step"], 1)
                n += 4
            dve.wait_ge(s["mod_step"], n)
            v.tensor_copy(gate2[:], mod[:, :, GATE2:GATE2 + 2]).then_inc(s["mod_done"], 1)

            def moments(n0, n4, m, part):
                rows = ([(xs[:, n0.p], 0)] if n0 else []) + ([(x1, TT)] if n4 else [])
                if part == 0:
                    if n0:
                        dve.wait_ge(x_loaded[n0.p], (n0.pair + 1) * 16)
                    if n4:
                        dve.wait_ge(s["x1_ready"], n4.done())
                    for src, j0 in rows:
                        for j in range(TT):
                            ins = v.bn_stats(stats[:, j0 + j], src[:, j])
                    ins.then_inc(s["ln_stats"], 1)
                elif part == 1:
                    ge(dve, s["moments_set"], 1)
                    wait_apart(dve, s["ln_stats"], m.done(), s["dve_apart"])
                    for _, j0 in rows:
                        for j in range(TT):
                            ins = v.bn_aggr(mv[:, j0 + j], stats[:, j0 + j])
                    ins.then_inc(s["ln_aggr"], 1)
                elif part == 2:
                    dve.wait_ge(s["ln_aggr"], m.done())
                    ge(dve, s["rstd"], m.n * 12)
                    v.tensor_scalar(nt[:, 1], mv[:, :, 1], EPS, None, ALU.add).then_inc(s["half_v"], 1)
                elif part == 3:
                    dve.wait_ge(s["half_v"], m.done(2, 1))
                    v.tensor_scalar(nt[:, 2].bitcast(I32), nt[:, 1].bitcast(I32), 1, None, ALU.logical_shift_right)\
                        .then_inc(s["half_v"], 1)
                    v.tensor_scalar(nt[:, 0], nt[:, 1], -0.5, None, ALU.mult)
                else:
                    dve.wait_ge(s["half_v"], m.done(2, 2))
                    v.tensor_scalar(rs[:].bitcast(I32), nt[:, 2].bitcast(I32), -1.0, float(0x5F3759DF), ALU.mult,
                                    ALU.add).then_inc(s["seed"], 1)

            def centre(out, src, j0):
                for i in range(TT):
                    ins = v.tensor_scalar(out[:, i], src[:, i], mv[:, j0 + i, 0:1], rs[:, j0 + i:j0 + i + 1],
                                          ALU.subtract, ALU.mult)
                return ins

            def reduce(n2, h):
                dve.wait_ge(s["scores1"], n2.done(H, h + 1))
                if h % HG == 0:
                    ge(dve, s["mxT_ready"], (n2.n - 1) * NG + h // HG + 1)
                v.tensor_reduce(mx[:, :, h], ps1[h % 2][:], axis=AX.X, op=ALU.max).then_inc(s["max_done"], 1)

            def negate_max(n, g):
                bank = ps_m[MAX_BANK[g]][0:HG].rearrange("p a c -> p (a c)")[:, 0:S]
                dve.wait_ge(s["mxT_ready"], n.done(NG, g + 1))
                ge(dve, max_stored[g], n.n * 16)
                v.tensor_scalar(nmx[:, g, 0], bank, -1.0, None, ALU.mult).then_inc(s["nmx_hi"], 1)
                dve.wait_ge(s["nmx_hi"], n.done(NG, g + 1))
                v.scalar_tensor_tensor(out=nmx[:, g, 1], in0=bank, scalar=-1.0, in1=nmx[:, g, 0].bitcast(F32),
                                       op0=ALU.mult, op1=ALU.subtract).then_inc(s["nmx_ready"], 1)

            def normalise(n, half, part):
                bank = ps_m[1 - half][:].rearrange("p t (a g c) -> p t a g c", a=2, g=HG)
                if part == 0:
                    dve.wait_ge(s["oT_ready"], n.done(2, half + 1))
                    v.reciprocal(o_inv[:], bank[:, :, :, :, DH]).then_inc(s["o_recip"], 1)
                else:
                    dve.wait_ge(s["o_recip"], n.done(2, half + 1))
                    ge(dve, s["oF_ready"], n.n)
                    out = o_n[:, :, half * P:(half + 1) * P].rearrange("p t (h c) -> p t h c", c=DH)
                    for i in range(TT):
                        ins = v.tensor_tensor(out[:, i], bank[:, i, :, :, 0:DH].rearrange("p a g c -> p (a g) c"),
                                              o_inv[:, i].rearrange("p a g -> p (a g)").unsqueeze(2)
                                              .broadcast_to([P, 2 * HG, DH]), ALU.mult)
                    ins.then_inc(s["o_norm"], 1)

            def route(n5, i):
                if i == 0:
                    dve.wait_ge(s["g_exp_done"], n5.done())
                    v.tensor_scalar(sc1[:], g_exp[:], 1.0, None, ALU.add).then_inc(s["sc1_done"], 1)
                if i == 1:
                    dve.wait_ge(s["sc1_done"], n5.done())
                    v.reciprocal(sc[:], sc1[:]).then_inc(s["sc_done"], 1)
                if i == 2:
                    wait_apart(dve, s["sc_done"], n5.done(), s["dve_apart"])
                    for j in range(TT):
                        ins = v.max(top[:, j], sc[:, j])
                    ins.then_inc(s["top_done"], 1)
                if i == 3:
                    wait_apart(dve, s["top_done"], n5.done(), s["dve_apart"])
                    for j in range(TT):
                        ins = v.max_index(top_i[:, j], top[:, j], sc[:, j])
                    ins.then_inc(s["idx_done"], 1)
                if i == 4:
                    dve.wait_ge(s["idx_done"], n5.done())
                    v.tensor_copy(top_f[:], top_i[:]).then_inc(s["idxf_done"], 1)
                if i == 5:
                    dve.wait_ge(s["idxf_done"], n5.done())
                    ge(dve, s["iota_done"], 1)
                    for j in range(TT):
                        ins = v.tensor_tensor(eq[:, j], iota[:].unsqueeze(2).broadcast_to([P, E, TOPK]),
                                              top_f[:, j, 0:TOPK].unsqueeze(1).broadcast_to([P, E, TOPK]),
                                              ALU.is_equal)
                    ins.then_inc(s["eq_done"], 1)
                if i == 6:
                    dve.wait_ge(s["eq_done"], n5.done())
                    v.tensor_reduce(mask[:].rearrange("p t e -> p (t e)"),
                                    eq[:].rearrange("p t e k -> p (t e) k"), axis=AX.X, op=ALU.add)\
                        .then_inc(s["mask_done"], 1)
                if i == 7:
                    dve.wait_ge(s["mask_done"], n5.done())
                    v.tensor_tensor(kept[:], mask[:], sc[:], ALU.mult).then_inc(s["kept_done"], 1)
                if i == 8:
                    dve.wait_ge(s["kept_done"], n5.done())
                    v.tensor_reduce(ksum[:], kept[:], axis=AX.X, op=ALU.add).then_inc(s["ksum_done"], 1)
                if i == 9:
                    dve.wait_ge(s["ksum_done"], n5.done())
                    v.tensor_scalar(kinv[:], ksum[:], 1e-20, None, ALU.add).then_inc(s["keps_done"], 1)
                if i == 10:
                    dve.wait_ge(s["keps_done"], n5.done())
                    v.reciprocal(kinv[:], kinv[:]).then_inc(s["kinv_done"], 1)
                if i == 11:
                    dve.wait_ge(s["kinv_done"], n5.done())
                    ge(dve, s["combT_ready"], n5.n)
                    v.tensor_tensor(comb[:], kept[:], kinv[:].unsqueeze(2).broadcast_to([P, TT, E]), ALU.mult)\
                        .then_inc(s["comb_ready"], 1)

            def step(n0, n1, n2, n3, n4, n5, m):
                for h in range(H):
                    if n5 and h < 6:
                        route(n5, 2 * h)
                    if n2:
                        reduce(n2, h)
                    if n3 and h == 0:
                        negate_max(n3, 3)
                    if n2 and h in (4, 8, 12):
                        negate_max(n2, h // 4 - 1)
                    if n4 and h == 2:
                        dve.wait_ge(s["o_hi_ready"], n4.done())
                        ge(dve, s["att_ready"], n4.n)
                        v.tensor_tensor(o_lo[:], ps_m[0][:], o_hi[:].bitcast(F32), ALU.subtract)\
                            .then_inc(s["o_lo_ready"], 1)
                    if n4 and h == 6:
                        dve.wait_ge(s["attT_ready"], n4.done())
                        dve.wait_ge(s["x4_loaded"], n4.done(16))
                        ge(dve, s["x1_stored"], 16 * n4.n)
                        ge(dve, s["z2_ready"], n4.n)
                        v.tensor_tensor(x1[:], ps_m[2][:], x4[:], ALU.add).then_inc(s["x1_ready"], 1)
                    if (n0 or n4) and h in (6, 7):
                        moments(n0, n4, m, h - 6)
                    if (n0 or n4) and h == 7:
                        moments(n0, n4, m, 2)
                        moments(n0, n4, m, 3)
                        moments(n0, n4, m, 4)
                    if n3 and h in (9, 10):
                        normalise(n3, 0, h - 9)
                    if n1 and h == 11:
                        dve.wait_ge(s["v_ready"], n1.done())
                        ge(dve, s["pv_done"], (n1.n - 1) * NHG)
                        ge(dve, s["stack_init"], 4)
                        for i in range(TT):
                            ins = v.tensor_tensor(v_aug[:, n1.p, i, :, 0:DH],
                                                  ps_m[2][:, i].rearrange("p (h d) -> p h d", d=DH),
                                                  bv_row[:].rearrange("p (h d) -> p h d", d=DH), ALU.add)
                        ins.then_inc(s["v_evac"], 1)
                    if n4 and h == 12:
                        dve.wait_ge(s["rstd"], m.done(12))
                        ge(dve, s["z2T_ready"], n4.n)
                        centre(z2, x1, TT).then_inc(s["z2_ready"], 1)
                    if n0 and h == 13:
                        dve.wait_ge(s["rstd"], m.done(12))
                        ge(dve, s["zT_ready"], n0.n)
                        centre(z, xs[:, n0.p], 0).then_inc(s["z_ready"], 1)
                    if n3 and h in (14, 15):
                        normalise(n3, 1, h - 14)
                    if n5 and h < 6:
                        route(n5, 2 * h + 1)

            steps(dve.Fori, step)

        @block.tensor
        def _(pe):
            t = nc.tensor
            pe.wait_ge(s["silu_c"], 3)
            pe.wait_ge(s["mod_loaded"], 16)
            pm = ps1[0][:].rearrange("p a c -> p (a c)")
            for j in range(12):
                for k in range(KD):
                    ins = t.matmul(pm[:, j * B:(j + 1) * B], wmod_sb[:, k, j * P:(j + 1) * P], cT_sb[:, k],
                                   start=k == 0, stop=k == KD - 1)
            ins.then_inc(s["mod_ready"], 1)
            pe.wait_ge(s["ident_done"], 1)

            def products(out, pairs):
                terms = [(a, b) for (ah, al), (bh, bl) in pairs for a, b in ((ah, bh), (ah, bl), (al, bh))]
                for i, (a, b) in enumerate(terms):
                    ins = t.matmul(out, a, b, start=i == 0, stop=i == len(terms) - 1)
                return ins

            last = [None, None, None]

            def use(bank, evacuated, value):
                if last[bank]:
                    pe.wait_ge(*last[bank])
                last[bank] = s[evacuated], value
                return ps_m[bank]

            def transposes(out, src):
                for i in range(TT):
                    for k in range(2):
                        ins = t.transpose(out[:, k, i * P:(i + 1) * P], src[:, i, k * P:(k + 1) * P], ident[:])
                return ins

            def scores1(n, h):
                if h % 8 == 0:
                    pe.wait_ge(stacked[n.p][h // 8], (n.pair + 1) * STACK_LOADS)
                    ge(pe, s["mod_done"], 1)
                ge(pe, s["max_done"], n.n * H + h - 1)
                for i in range(TT):
                    ins = t.matmul(ps1[h % 2][:, i], q_st[0:STACK, n.p, h, i * P:(i + 1) * P], k_st[0:STACK, n.p, h],
                                   start=True, stop=True)
                ins.then_inc(s["scores1"], 1)

            def scores2(n, h):
                if h % HG == 0:
                    pe.wait_ge(max_rows[h // HG], n.done(16))
                ge(pe, s["probs"], n.n * H + h - 1)
                for i in range(TT):
                    ins = t.matmul(ps2[h % 2][:, i], k_st[0:STACK, n.p, h, i * P:(i + 1) * P], q_st[0:STACK, n.p, h],
                                   start=True, stop=True)
                ins.then_inc(s["scores2"], 1)

            def pv(n, hg):
                pe.wait_ge(s["probs"], n.done(H, HG * (hg + 1)))
                if hg == 0:
                    pe.wait_ge(s["v_evac"], n.done())
                if hg % 2 == 0:
                    ge(pe, s["o_evac"], n.n * 2 + hg // 2)
                for i in range(TT):
                    for g in range(HG):
                        h = hg * HG + g
                        ins = t.matmul(ps_o[32 * g:32 * g + 32, hg % 2], v_aug[:, n.p, i, h], pt[:, h % 8, i],
                                       start=i == 0, stop=i == TT - 1, tile_position=(0, 32 * g))
                ins.then_inc(s["pv_done"], 1)

            def transpose_max(n, g):
                pe.wait_ge(s["max_done"], n.done(H, HG * g + HG))
                bank = use(MAX_BANK[g], "nmx_ready", n.done(NG, g + 1))
                for i in range(TT):
                    ins = t.transpose(bank[0:HG].rearrange("p a c -> p (a c)")[:, i * P:(i + 1) * P],
                                      mx[:, i, HG * g:HG * g + HG], ident[:])
                ins.then_inc(s["mxT_ready"], 1)

            def project(n1, i, name, bank):
                if i == 0:
                    pe.wait_ge(s["wsplit"], 2)
                    pe.wait_ge(s["h1_lo_ready"], n1.done())
                bank = use(bank, f"{name}_evac", n1.done())
                for m in range(KD):
                    cols = slice(m * P, (m + 1) * P)
                    if name == "v":
                        ins = products(bank[:, m], [((h1_hi[:, k, cols], h1_lo[:, k, cols]),
                                                     (w_hi[:, i, k], w_lo[:, i, k])) for k in range(KD)])
                    else:
                        ins = products(bank[:, m], [((w_hi[:, i, k, cols], w_lo[:, i, k, cols]),
                                                     (h1_hi[:, k], h1_lo[:, k])) for k in range(KD)])
                ins.then_inc(s[f"{name}_ready"], 1)

            def transpose_heads(n, half):
                pe.wait_ge(s["o_evac"], n.done(2, half + 1))
                bank = use(1 - half, "o_norm", n.done(2, half + 1))
                for i in range(TT):
                    for a in range(2):
                        ins = t.transpose(bank[:, i, a * P:(a + 1) * P], o_sb[:, 2 * half + a, i * P:(i + 1) * P],
                                          ident[:])
                ins.then_inc(s["oT_ready"], 1)

            def step(n0, n1, n2, n3, n4, n5, m):
                for i in range(H):
                    if n2:
                        scores1(n2, i)
                    if n3 and i == 0:
                        transpose_max(n3, 3)
                    if n1 and i == 0:
                        pe.wait_ge(s["z_ready"], n1.done())
                        transposes(use(1, "h1_ready", n1.done()), z).then_inc(s["zT_ready"], 1)
                    if n4 and i == 1:
                        pe.wait_ge(s["o_norm"], n4.done(2))
                        transposes(use(0, "o_lo_ready", n4.done()), o_n).then_inc(s["oF_ready"], 1)
                    if n4 and i == 3:
                        pe.wait_ge(s["o_lo_ready"], n4.done())
                        bank = use(2, "att_evac", n4.done())
                        for k in range(KD):
                            cols = slice(k * P, (k + 1) * P)
                            ins = products(bank[:, k], [((w_hi[:, 3, a, cols], w_lo[:, 3, a, cols]),
                                                         (o_hi[:, a], o_lo[:, a])) for a in range(KD)])
                        ins.then_inc(s["att_ready"], 1)
                    if n2 and i in (4, 8, 12):
                        transpose_max(n2, i // 4 - 1)
                    if n3 and i in (3, 7, 11):
                        pv(n3, i // 4 + 1)
                    if n1 and i == 4:
                        project(n1, 0, "q", 0)
                    if n4 and i == 5:
                        pe.wait_ge(s["att_evac"], n4.done())
                        transposes(use(2, "x1_ready", n4.done()), att).then_inc(s["attT_ready"], 1)
                    if n1 and i == 5:
                        project(n1, 1, "k", 1)
                    if n3 and i == 9:
                        transpose_heads(n3, 0)
                    if n1 and i == 10:
                        project(n1, 2, "v", 2)
                    if n5 and i == 11:
                        pe.wait_ge(s["comb_ready"], n5.done())
                        bank = use(0, "combT_evac", n5.done())
                        for j in range(TT):
                            ins = t.transpose(bank[0:E].rearrange("p a c -> p (a c)")[:, j * P:(j + 1) * P],
                                              comb[:, j], ident[:])
                        ins.then_inc(s["combT_ready"], 1)
                    if n4 and i == 13:
                        pe.wait_ge(s["z2_ready"], n4.done())
                        transposes(use(2, "h2_ready", n4.done()), z2).then_inc(s["z2T_ready"], 1)
                    if n3 and i == 14:
                        transpose_heads(n3, 1)
                    if i < LAG and n3:
                        scores2(n3, i + H - LAG)
                    if i >= LAG and n2:
                        scores2(n2, i - LAG)
                    if n4 and i == 15:
                        pe.wait_ge(s["h2_ready"], n4.done())
                        bank = use(1, "g_exp_done", n4.done())
                        for j in range(TT):
                            for k in range(KD):
                                ins = t.matmul(bank[:, 0, j * E:(j + 1) * E], h2[:, k, j * P:(j + 1) * P], gw[:, k],
                                               start=k == 0, stop=k == KD - 1)
                        ins.then_inc(s["logits"], 1)
                    if n2 and i == 15:
                        pv(n2, 0)

            def loop_begins(n0, n1, n2, n3, n4, n5, m):
                last[:] = (s["o_norm"], n4.done(2)), (s["g_exp_done"], n5.done()), (s["h2_ready"], n5.done())

            def loop_ends(n0, n1, n2, n3, n4, n5, m):
                last[:] = (s["o_norm"], n3.done(2)), (s["g_exp_done"], n4.done()), (s["h2_ready"], n4.done())

            steps(pe.Fori, step, loop_begins, loop_ends)


def ffn(nc, wall, h2_dram, x1_dram, cw_dram, gate2, out):
    ctx = ExitStack()
    with ctx:
        def sb(name, shape, dt=F32):
            return ctx.enter_context(nc.sbuf_tensor(name, shape, dt))

        def sem(name):
            return ctx.enter_context(nc.semaphore(name))

        NP = FT // 2
        GU = 2 * KD * P
        CT = CH // P
        ident = sb("ident_f", [P, P])
        w_sb = sb("w_sb", [P, FT + 1, WCOL])
        gu_hi = sb("gu_hi", [P, 2, GU], F32R)
        gu_lo = sb("gu_lo", [P, 2, GU], F32R)
        wd_hi = sb("wd_hi", [P, 2, D], F32R)
        wd_lo = sb("wd_lo", [P, 2, D], F32R)
        h = sb("h_in", [P, KD, CH])
        h_hi = sb("h_hi", [P, 2, KD, CH], F32R)
        h_lo = sb("h_lo", [P, 2, KD, CH], F32R)
        cw = sb("cw", [P, 2, CH])
        sg = sb("silu_g", [P, 2, CH])
        sw = sb("silu_gw", [P, 2, CH])
        a32 = sb("act32", [P, 2, CH])
        a_hi = sb("a_hi", [P, 2, CH], F32R)
        a_lo = sb("a_lo", [P, 2, CH], F32R)
        gy = sb("gate_y", [P, 2, KD])
        y_sb = sb("y_sb", [P, KD, CH])
        x1 = sb("x1_in", [P, CT, D])
        o_sb = sb("out_sb", [P, CT, D])
        ps_g = [ctx.enter_context(nc.psum_tensor(f"ps_g{i}", [P, CH], F32)) for i in range(2)]
        ps_u = [ctx.enter_context(nc.psum_tensor(f"ps_u{i}", [P, CH], F32)) for i in range(2)]
        ps_y = [ctx.enter_context(nc.psum_tensor(f"ps_y{i}", [P, KD, CH], F32)) for i in range(2)]
        names = """ident_zero_f ident_done_f h_loaded x1_loaded h_hi_done h_lo_done gy_done y_done y_evac yT_ready
            out_ready out_stored pool_apart_f""".split()
        s = {n: sem(n) for n in names}
        per_slot = "cw_loaded gu_hi_done gu_lo_done wd_hi_done wd_lo_done g_ready u_ready silu_done sw_done " \
                   "act_done a_hi_done a_lo_done down_done"
        s |= {n: [sem(f"{n}{i}") for i in range(2)] for n in per_slot.split()}
        w_loaded = [sem(f"w_loaded{i}") for i in range(3)]
        LOADS = ((0, 1), (1, 6), (6, FT + 1))
        block = ctx.enter_context(nc.Block())

        def chunks(fori, pair_of_tiles, between):
            def chunk(c, p):
                for jj in range(2):
                    pair_of_tiles(c, p, jj, c * NP + jj)
                between(c, p)
                with fori(2, NP) as jj:
                    pair_of_tiles(c, p, jj, c * NP + jj)

            for c in (0, 1):
                chunk(c, c)
            with fori(1, NCH // 2 - 1) as i:
                for p in range(2):
                    chunk(2 * i + p, p)
            for c in (NCH - 2, NCH - 1):
                chunk(c, c % 2)

        def tile(j):
            if isinstance(j, int):
                return w_sb[:, j]
            return w_sb[:, bass.ds(j, 1)].rearrange("p a c -> p (a c)")

        def first(c):
            return isinstance(c, int) and c == 0

        def weights_there(eng, jj):
            if isinstance(jj, int) and jj < 2:
                eng.wait_ge(w_loaded[1], 16)
            else:
                eng.wait_ge(w_loaded[2], 16)

        @block.sync
        def _(sp):
            def load_h(c):
                ge(sp, s["h_lo_done"], c)
                sp.dma_start(h[:], h2_dram[:, :, bass.ds(c * CH, CH)].rearrange("k p c -> p k c"))\
                    .then_inc(s["h_loaded"], 16)

            def pair_of_tiles(c, p, jj, k):
                for r in range(2):
                    ge(sp, s["sw_done"][r], k)
                    sp.dma_start(cw[:, r], cw_dram[bass.ds(8 * jj + 4 * r, 4), bass.ds(c * CH, CH)]
                                 .unsqueeze(1).broadcast_to([4, REP, CH])).then_inc(s["cw_loaded"][r], 16)

            def between(c, p):
                if not first(c):
                    ge(sp, s["out_ready"], c - 1)
                    sp.dma_start(x1[:], token_tiles(x1_dram, c - 1)).then_inc(s["x1_loaded"], 16)
                    store(c - 1)
                if not (isinstance(c, int) and c == NCH - 1):
                    load_h(c + 1)

            def token_tiles(dram, c):
                return dram.rearrange("b (t p) d -> p (b t) d", p=P)[:, bass.ds(c * CT, CT)]

            def store(c):
                sp.wait_ge(s["out_ready"], c + 1)
                sp.dma_start(token_tiles(out, c), o_sb[:]).then_inc(s["out_stored"], 16)

            load_h(0)
            for i, (j0, j1) in enumerate(LOADS):
                sp.dma_start(w_sb[:, j0:j1], wall[j0:j1].rearrange("j p c -> p j c")).then_inc(w_loaded[i], 16)
            chunks(sp.Fori, pair_of_tiles, between)
            sp.wait_ge(s["out_ready"], NCH - 1)
            sp.dma_start(x1[:], token_tiles(x1_dram, NCH - 1)).then_inc(s["x1_loaded"], 16)
            store(NCH - 1)
            sp.wait_ge(s["out_stored"], 16 * NCH)

        @block.gpsimd
        def _(pool):
            g = nc.gpsimd
            g.memset(ident[:], 0.0).then_inc(s["ident_zero_f"], 1)
            pool.wait_ge(s["ident_zero_f"], 1)
            g.affine_select(out=ident[:], in_=ident[:], compare_op=ALU.not_equal, fill=1.0, base=0,
                            pattern=[[-1, P]], channel_multiplier=1).then_inc(s["ident_done_f"], 1)

            def pair_of_tiles(c, p, jj, k):
                for r in range(2):
                    pool.wait_ge(s["silu_done"][r], k + 1)
                    pool.wait_ge(s["cw_loaded"][r], (k + 1) * 16)
                    ge(pool, s["act_done"][r], k)
                    g.tensor_tensor(sw[:, r], sg[:, r], cw[:, r], ALU.mult).then_inc(s["sw_done"][r], 1)

            def between(c, p):
                wait_apart(pool, s["y_evac"], c * 4, s["pool_apart_f"])
                g.tensor_copy(gy[:], gate2[:, bass.ds(2 * c, 2)]).then_inc(s["gy_done"], 1)

            chunks(pool.Fori, pair_of_tiles, between)

        @block.scalar
        def _(act):
            a = nc.scalar
            act.wait_ge(w_loaded[0], 16)
            a.activation(gu_hi[:, 0], w_sb[:, 0, 0:GU], ACT.Copy).then_inc(s["gu_hi_done"][0], 1)

            def pair_of_tiles(c, p, jj, k):
                if first(c):
                    weights_there(act, jj)
                for r in range(2):
                    j = 2 * jj + r
                    act.wait_ge(s["g_ready"][r], k + 1)
                    ge(act, s["sw_done"][r], k)
                    a.activation(sg[:, r], ps_g[r][:], ACT.Silu).then_inc(s["silu_done"][r], 1)
                    ge(act, s["u_ready"][1 - r], k + r)
                    ge(act, s["gu_lo_done"][1 - r], k + r)
                    a.activation(gu_hi[:, 1 - r], tile(j + 1)[:, 0:GU], ACT.Copy).then_inc(s["gu_hi_done"][1 - r], 1)
                    ge(act, s["down_done"][r], k)
                    a.activation(wd_hi[:, r], tile(j)[:, GU:WCOL], ACT.Copy).then_inc(s["wd_hi_done"][r], 1)
                    act.wait_ge(s["act_done"][r], k + 1)
                    a.activation(a_hi[:, r], a32[:, r], ACT.Copy).then_inc(s["a_hi_done"][r], 1)

            def between(c, p):
                if not first(c):
                    evacuate(c - 1, 1 - p)

            def evacuate(c, p):
                act.wait_ge(s["y_done"], c + 1)
                act.wait_ge(s["gy_done"], c + 1)
                ge(act, s["yT_ready"], c)
                for m in range(KD):
                    for b in range(2):
                        a.activation(y_sb[:, m, b * S:(b + 1) * S], ps_y[p][:, m, b * S:(b + 1) * S], ACT.Copy,
                                     scale=gy[:, b, m:m + 1]).then_inc(s["y_evac"], 1)

            chunks(act.Fori, pair_of_tiles, between)
            evacuate(NCH - 1, 1)

        @block.vector
        def _(dve):
            v = nc.vector

            def split_h(c, p):
                dve.wait_ge(s["h_loaded"], (c + 1) * 16)
                ge(dve, s["u_ready"][1], (c - 1) * NP)
                v.tensor_copy(h_hi[:, p], h[:]).then_inc(s["h_hi_done"], 1)
                dve.wait_ge(s["h_hi_done"], c + 1)
                v.tensor_tensor(h_lo[:, p], h[:], h_hi[:, p].bitcast(F32), ALU.subtract).then_inc(s["h_lo_done"], 1)

            def gu_low(slot, j, k):
                dve.wait_ge(s["gu_hi_done"][slot], k + 1)
                ge(dve, s["u_ready"][slot], k)
                v.tensor_tensor(gu_lo[:, slot], tile(j)[:, 0:GU], gu_hi[:, slot].bitcast(F32), ALU.subtract)\
                    .then_inc(s["gu_lo_done"][slot], 1)

            split_h(0, 0)
            dve.wait_ge(w_loaded[0], 16)
            gu_low(0, 0, 0)

            def pair_of_tiles(c, p, jj, k):
                if first(c):
                    weights_there(dve, jj)
                for r in range(2):
                    j = 2 * jj + r
                    gu_low(1 - r, j + 1, k + r)
                    dve.wait_ge(s["u_ready"][r], k + 1)
                    dve.wait_ge(s["sw_done"][r], k + 1)
                    ge(dve, s["a_lo_done"][r], k)
                    v.tensor_tensor(a32[:, r], ps_u[r][:], sw[:, r], ALU.mult).then_inc(s["act_done"][r], 1)
                    dve.wait_ge(s["wd_hi_done"][r], k + 1)
                    v.tensor_tensor(wd_lo[:, r], tile(j)[:, GU:WCOL], wd_hi[:, r].bitcast(F32), ALU.subtract)\
                        .then_inc(s["wd_lo_done"][r], 1)
                    dve.wait_ge(s["a_hi_done"][r], k + 1)
                    v.tensor_tensor(a_lo[:, r], a32[:, r], a_hi[:, r].bitcast(F32), ALU.subtract)\
                        .then_inc(s["a_lo_done"][r], 1)

            def between(c, p):
                if not first(c):
                    finish(c - 1, 1 - p)
                if not (isinstance(c, int) and c == NCH - 1):
                    split_h(c + 1, 1 - p)

            def finish(c, p):
                dve.wait_ge(s["yT_ready"], c + 1)
                dve.wait_ge(s["x1_loaded"], (c + 1) * 16)
                ge(dve, s["out_stored"], c * 16)
                v.tensor_tensor(o_sb.rearrange("p t d -> p (t d)"), ps_y[p][:].rearrange("p m c -> p (m c)"),
                                x1[:].rearrange("p t d -> p (t d)"), ALU.add).then_inc(s["out_ready"], 1)

            chunks(dve.Fori, pair_of_tiles, between)
            finish(NCH - 1, 1)

        @block.tensor
        def _(pe):
            t = nc.tensor

            def products(out, pairs, start=True, stop=True):
                terms = [(a, b) for (ah, al), (bh, bl) in pairs for a, b in ((ah, bh), (ah, bl), (al, bh))]
                for i, (a, b) in enumerate(terms):
                    ins = t.matmul(out, a, b, start=start and i == 0, stop=stop and i == len(terms) - 1,
                                   skip_group_check=not (start and stop))
                return ins

            def gate_up(c, p, r, k):
                pe.wait_ge(s["gu_lo_done"][r], k + 1)
                for which, (ps, used, ready) in enumerate(((ps_g[r], "silu_done", "g_ready"),
                                                           (ps_u[r], "act_done", "u_ready"))):
                    ge(pe, s[used][r], k)
                    cols = [slice((2 * which + i) * P, (2 * which + i + 1) * P) for i in range(KD)]
                    products(ps[:], [((gu_hi[:, r, cols[i]], gu_lo[:, r, cols[i]]), (h_hi[:, p, i], h_lo[:, p, i]))
                                     for i in range(KD)]).then_inc(s[ready][r], 1)

            def down(p, r, k, start=False, stop=False):
                pe.wait_ge(s["a_lo_done"][r], k + 1)
                pe.wait_ge(s["wd_lo_done"][r], k + 1)
                for m in range(KD):
                    cols = slice(m * P, (m + 1) * P)
                    ins = products(ps_y[p][:, m], [((wd_hi[:, r, cols], wd_lo[:, r, cols]),
                                                    (a_hi[:, r], a_lo[:, r]))], start, stop)
                ins.then_inc(s["down_done"][r], 1)
                return ins

            def last_down(c, p, r):
                down(p, r, c * NP + NP - 1, stop=r == 1)

            def pair_of_tiles(c, p, jj, k):
                for r in range(2):
                    if r == 0 and isinstance(jj, int) and jj == 0:
                        pe.wait_ge(s["h_lo_done"], c + 1)
                    gate_up(c, p, r, k)
                    if isinstance(jj, int) and jj == 0:
                        if not first(c):
                            last_down(c - 1, 1 - p, r)
                            if r == 1:
                                pe.wait_ge(s["down_done"][1], c * NP)
                                pe.sem_inc(s["y_done"], 1)
                    else:
                        if r == 0 and isinstance(jj, int) and jj == 1:
                            ge(pe, s["out_ready"], c - 1)
                        down(p, r, k - 1, start=isinstance(jj, int) and jj == 1 and r == 0)

            def between(c, p):
                if not first(c):
                    transpose_y(c - 1, 1 - p)

            def transpose_y(c, p):
                pe.wait_ge(s["y_evac"], (c + 1) * 4)
                flat = ps_y[p][:].rearrange("p m c -> p (m c)")
                for i in range(CT):
                    for m in range(KD):
                        ins = t.transpose(flat[:, i * D + m * P:i * D + (m + 1) * P], y_sb[:, m, i * P:(i + 1) * P],
                                          ident[:])
                ins.then_inc(s["yT_ready"], 1)

            pe.wait_ge(s["ident_done_f"], 1)
            chunks(pe.Fori, pair_of_tiles, between)
            for r in range(2):
                last_down(NCH - 1, 1, r)
            pe.wait_ge(s["down_done"][1], NCH * NP)
            pe.sem_inc(s["y_done"], 1)
            transpose_y(NCH - 1, 1)


def program(nc, x, cT, wmod, wqT, wkT, wvT, woT, bq, bk, bv, bo, spiral, helix, gate_w, wall, out):
    h2_dram = nc.dram_tensor("h2_scratch", [KD, P, TOK], F32, kind="Internal").ap()
    x1_dram = nc.dram_tensor("x1_scratch", [B, S, D], F32, kind="Internal").ap()
    cw_dram = nc.dram_tensor("cw_scratch", [4 * FT, TOK], F32, kind="Internal").ap()
    qk_dram = nc.dram_tensor("qk_scratch", [2, 2, 2, DH, H, S], F32, kind="Internal").ap()
    max_dram = nc.dram_tensor("max_scratch", [NG, 2, HG, S], F32, kind="Internal").ap()
    with nc.sbuf_tensor("gate2", [P, B, KD], F32) as gate2:
        attention(nc, x, cT, wmod, wqT, wkT, wvT, woT, bq, bk, bv, bo, spiral, helix, gate_w, h2_dram, x1_dram,
                  cw_dram, qk_dram, max_dram, gate2)
        ffn(nc, wall, h2_dram, x1_dram, cw_dram, gate2, out)


def kernel(**inputs):
    import concourse.bacc as bacc
    from concourse.bass_utils import run_bass_kernel_spmd

    a = {k.removeprefix("L0_"): np.asarray(v) for k, v in inputs.items()}

    def halves(vector):
        return vector.reshape(KD, P).T

    def features(experts, shared):
        both = np.concatenate([experts.transpose(1, 0, 2).reshape(D, E * FE), shared], 1)
        both = np.pad(both, ((0, 0), (0, FT * P - both.shape[1])))
        return both.reshape(KD, P, FT, P).transpose(2, 1, 0, 3).reshape(FT, P, KD * P)

    down = np.pad(np.concatenate([a["ffn_wd"].reshape(E * FE, D), a["ffn_sd"]], 0), ((0, FT * P - E * FE - FS), (0, 0)))
    wall = np.concatenate([features(a["ffn_wg"], a["ffn_sg"]), features(a["ffn_wu"], a["ffn_su"]),
                           down.reshape(FT, P, D)], 2)
    wall = np.concatenate([wall, wall[:1]], 0)
    data = {
        "x": a["attn_x"], "cT": a["c"].T, "wmod": a["wmod"], "wqT": a["attn_Wq"].T, "wkT": a["attn_Wk"].T,
        "wvT": a["attn_Wv"].T, "woT": a["attn_Wo"].T, "bq": halves(a["attn_bq"]), "bk": halves(a["attn_bk"]),
        "bv": a["attn_bv"], "bo": halves(a["attn_bo"]), "spiral": halves(np.repeat(a["attn_spiral_weight"], DH)),
        "helix": halves(a["attn_helix_rotation"]),
        "gate_w": a["ffn_gate_w"], "wall": wall,
    }
    data = {k: np.ascontiguousarray(v) for k, v in data.items()}
    nc = bacc.Bacc("TRN2", target_bir_lowering=False, num_devices=1)
    args = [nc.dram_tensor(f"in_{k}", v.shape, mybir.dt.from_np(v.dtype), kind="ExternalInput").ap()
            for k, v in data.items()]
    out = nc.dram_tensor("out", (B, S, D), F32, kind="ExternalOutput").ap()
    program(nc, *args, out)
    r = run_bass_kernel_spmd(nc, [{f"in_{k}": v for k, v in data.items()}], core_ids=[0])
    return r.results[0]["out"]
```

```python
from contextlib import ExitStack

import numpy as np

import concourse.bass as bass
from concourse import mybir

F32 = mybir.dt.float32
F32R = mybir.dt.float32r
I32 = mybir.dt.int32
U32 = mybir.dt.uint32
ACT = mybir.ActivationFunctionType
ALU = mybir.AluOpType
AX = mybir.AxisListType

B, S, D = 16, 256, 256
H, DH = 16, 16
P = 128
KD = D // P
TT = S // P
HG = 4
NHG = NG = H // HG
LAG = 9
TOK = B * S
E, FE, FS, TOPK = 32, 96, 192, 6
FT = (E * FE + FS + P - 1) // P
WCOL = 2 * KD * P + D
REP = 32
CH = 512
NCH = TOK // CH
EARLY = 10
LOOP_STEP = 6
EPS = 1e-5
TWO_PI = float(2 * np.pi)
ROUND = 12582912.0

PART_ROWS = (0, 48)
MAX_ROW = 32
GAP = PART_ROWS[1] - MAX_ROW - 2
STACK = 80
MAX_BANK = (1, 0, 1, 2)

LN_SHIFT1, LN_SCALE1, GATE1, LN_SHIFT2, LN_SCALE2, GATE2 = 0, 2, 4, 6, 8, 10


def ge(eng, sem, value):
    if isinstance(value, int) and value <= 0:
        return
    eng.wait_ge(sem, value)


def wait_apart(eng, sem, value, waits_apart):
    ge(eng, sem, value)
    if not isinstance(value, int):
        eng.sem_inc(waits_apart, 1)


class Batch:

    def __init__(self, n, pair, parity):
        self.n, self.pair, self.p = n, pair, parity

    def done(self, per=1, k=None):
        return self.n * per + (per if k is None else k)


def first(batch):
    return isinstance(batch.n, int) and batch.n == 0


def steps(fori, body, loop_begins=None, loop_ends=None):
    def batches(t, i=None):
        out = []
        for n in range(t + 1, t - 5, -1):
            if i is None:
                out.append(Batch(n, n // 2, n % 2) if 0 <= n < B else None)
            else:
                out.append(Batch(2 * i + n, i + n // 2, n % 2))
        return out + [Batch(t + 1 if i is None else 2 * i + t + 1, None, None)]

    for t in range(-1, 5):
        body(*batches(t))
    with fori(0, 5) as i:
        for t in (5, 6):
            if loop_begins:
                loop_begins(*batches(t, i))
            body(*batches(t, i))
    if loop_ends:
        loop_ends(*batches(14))
    for t in range(15, 20):
        body(*batches(t))


def attention(nc, x, cT, wmod, wqT, wkT, wvT, woT, bq, bk, bv, bo, spiral, helix, gate_w, h2_dram, x1_dram, cw_dram,
              qk_dram, max_dram, gate2, wall, w_sb):
    ctx = ExitStack()
    with ctx:
        def sb(name, shape, dt=F32):
            return ctx.enter_context(nc.sbuf_tensor(name, shape, dt))

        def sem(name):
            return ctx.enter_context(nc.semaphore(name))

        late = w_sb[:, EARLY:].rearrange("p j c -> p (j c)")
        taken = [0]

        def carve(shape, dt=F32):
            n = int(np.prod(shape[1:]))
            part = late[0:shape[0], taken[0]:taken[0] + n].bitcast(dt)
            taken[0] += n
            letters = "abc"[:len(shape) - 1]
            return part.rearrange(f"p ({' '.join(letters)}) -> p {' '.join(letters)}",
                                  **dict(zip(letters, shape[1:])))

        ident = sb("ident", [P, P])
        iota_i = sb("iota_i", [P, E], I32)
        iota = sb("iota", [P, E])
        cT_sb = sb("cT_sb", [P, KD, B])
        c_exp = sb("c_exp", [P, KD, B])
        mod = sb("mod", [P, B, 12])
        mod_t = sb("mod_t", [P, B, 12])
        w_hi = sb("w_hi", [P, 4, KD, D], F32R)
        w_lo = sb("w_lo", [P, 4, KD, D], F32R)
        w_raw = carve([P, 4, KD, D])
        bias_qk = sb("bias_qk", [P, 2, KD])
        bo_sb = sb("bo_sb", [P, KD])
        bv_row = sb("bv_row", [P, D])
        spi = sb("spi", [P, KD])
        rot = sb("rot", [P, 2, KD])
        rot_t = sb("rot_t", [P, 2, KD])
        trig = sb("trig", [P, 2, KD])
        bias_s = sb("bias_s", [P, 2, KD])
        gw = sb("gw", [P, KD, E])
        ones_blk = sb("ones_blk", [8, CH])
        zero_blk = sb("zero_blk", [GAP, S], F32R)
        xs = sb("xs", [P, 2, TT, D])
        stats = sb("stats", [P, 2 * TT, 6])
        mv = sb("mv", [P, 2 * TT, 2])
        rs = sb("rs", [P, 2 * TT])
        nt = sb("nt", [P, 3, 2 * TT])
        z = carve([P, TT, D])
        h1 = carve([P, KD, S])
        h1_hi = sb("h1_hi", [P, KD, S], F32R)
        h1_lo = sb("h1_lo", [P, KD, S], F32R)
        qk = sb("qk", [P, 2, KD, S])
        qk_hi = sb("qk_hi", [P, 2, KD, S], F32R)
        qk_lo = sb("qk_lo", [P, 2, KD, S], F32R)
        q_st = sb("q_st", [P, 2, H, S], F32R)
        k_st = sb("k_st", [P, 2, H, S], F32R)
        v_aug = sb("v_aug", [P, 2, TT, H, 2 * DH])
        mx = sb("mx", [P, TT, H])
        nmx = carve([HG, NG, 2, S], F32R)
        pt = carve([P, 8, TT, S])
        o_sb = carve([P, NHG, S])
        o_inv = sb("o_inv", [P, TT, 2, HG])
        o_n = sb("o_n", [P, TT, D])
        o_hi = sb("o_hi", [P, KD, S], F32R)
        o_lo = sb("o_lo", [P, KD, S], F32R)
        wmod_sb = pt.rearrange("p a b c -> p (a b c)")[:, 0:KD * 6 * D].rearrange("p (k n) -> p k n", k=KD)
        cm1 = sb("cm1", [P, 2, 12])
        cm4 = sb("cm4", [P, 2, 14])
        att = carve([P, KD, S])
        x4 = carve([P, TT, D])
        x1 = carve([P, TT, D])
        z2 = carve([P, TT, D])
        h2 = carve([P, KD, S])
        g_exp = sb("g_exp", [P, TT, E])
        sc1 = sb("sc1", [P, TT, E])
        sc = sb("sc", [P, TT, E])
        top = sb("top", [P, TT, 8])
        top_i = sb("top_i", [P, TT, 8], U32)
        top_f = sb("top_f", [P, TT, 8])
        eq = sb("eq", [P, TT, E, TOPK])
        mask = sb("mask", [P, TT, E])
        kept = sb("kept", [P, TT, E])
        ksum = sb("ksum", [P, TT])
        kinv = sb("kinv", [P, TT])
        comb = sb("comb", [P, TT, E])
        combT = sb("combT", [E, S])

        ps1 = [ctx.enter_context(nc.psum_tensor(f"ps1_{i}", [P, TT, S], F32)) for i in range(2)]
        ps2 = [ctx.enter_context(nc.psum_tensor(f"ps2_{i}", [P, TT, S], F32)) for i in range(2)]
        ps_o = ctx.enter_context(nc.psum_tensor("ps_o", [P, 2, S], F32))
        ps_m = [ctx.enter_context(nc.psum_tensor(f"ps_m{i}", [P, 2, 256], F32)) for i in range(3)]

        names = """c_loaded mod_loaded w_loaded b_loaded ident_zero ident_done iota_int iota_done
            c_exp_done silu_c mod_ready mod_done mod_step rot_step trig_done wsplit bias_done blocks_set
            zeros_set consts_stored stacks_set v_ones moments_set
            ln_stats ln_aggr half_v seed rstd z_ready zT_ready h1_ready h1_lo_ready
            q_ready k_ready q_evac k_evac qk_split q_stored k_stored v_ready v_evac
            scores1 max_done mxT_ready nmx_hi nmx_ready scores2 probs pv_done o_evac
            oT_ready o_recip o_norm oF_ready o_hi_ready o_lo_ready
            att_ready att_evac attT_ready x1_ready z2_ready z2T_ready h2_ready
            logits g_exp_done sc1_done sc_done top_done idx_done idxf_done eq_done mask_done kept_done ksum_done
            keps_done kinv_done comb_ready combT_ready combT_evac
            cm1_ready cm4_ready x4_loaded x1_stored h2_stored comb_stored w_early
            pool_apart dve_apart sp_apart""".split()
        s = {n: sem(n) for n in names}
        x_loaded = [sem(f"x_loaded{i}") for i in range(2)]
        stacked = [[sem(f"stacked{i}{m}") for m in range(KD)] for i in range(2)]
        max_stored = [sem(f"max_stored{i}") for i in range(NG)]
        max_rows = [sem(f"max_rows{i}") for i in range(NG)]
        block = ctx.enter_context(nc.Block())

        STACK_LOADS = 16 * (2 * len(PART_ROWS) + 1)

        @block.sync
        def _(sp):
            sp.dma_start(xs[:, 0], x[0].rearrange("(t p) d -> p t d", p=P)).then_inc(x_loaded[0], 16)
            sp.dma_start(cT_sb[:], cT.rearrange("(k p) b -> p k b", p=P)).then_inc(s["c_loaded"], 16)
            sp.dma_start(wmod_sb, wmod.rearrange("(k p) n -> p k n", p=P)).then_inc(s["mod_loaded"], 16)
            for i, w in enumerate((wqT, wkT, wvT, woT)):
                sp.dma_start(w_raw[:, i], w.rearrange("(k p) n -> p k n", p=P)).then_inc(s["w_loaded"], 16)
            sp.dma_start(bias_qk[:, 0], bq).then_inc(s["b_loaded"], 16)
            sp.dma_start(bias_qk[:, 1], bk).then_inc(s["b_loaded"], 16)
            sp.dma_start(bo_sb[:], bo).then_inc(s["b_loaded"], 16)
            sp.dma_start(spi[:], spiral).then_inc(s["b_loaded"], 16)
            sp.dma_start(rot[:, 1], helix).then_inc(s["b_loaded"], 16)
            sp.dma_start(bv_row[:], bv.partition_broadcast(P)).then_inc(s["b_loaded"], 16)
            sp.dma_start(gw[:], gate_w.rearrange("(k p) e -> p k e", p=P)).then_inc(s["b_loaded"], 16)
            sp.wait_ge(s["blocks_set"], 1)
            sp.dma_start(cw_dram[3 * E:3 * E + 8].rearrange("r (a c) -> r a c", c=CH),
                         ones_blk[:].unsqueeze(1).broadcast_to([8, NCH, CH])).then_inc(s["consts_stored"], 16)
            sp.wait_ge(s["zeros_set"], 1)
            for st, r0, blk in ((q_st, MAX_ROW + 2, zero_blk), (k_st, MAX_ROW + 2, zero_blk),
                                (k_st, MAX_ROW, ones_blk)):
                rows = GAP if blk is zero_blk else 2
                for i in range(2):
                    src = blk[0:rows] if blk is zero_blk else blk[0:rows, 0:S]
                    sp.dma_start(st[r0:r0 + rows, i].bitcast(F32),
                                 (src.bitcast(F32) if blk is zero_blk else src).unsqueeze(1)
                                 .broadcast_to([rows, H, S])).then_inc(s["stacks_set"], 16)

            def step(n0, n1, n2, n3, n4, n5, m):
                if n0 and not first(n0):
                    ge(sp, s["z_ready"], n0.n - 1)
                    sp.dma_start(xs[:, n0.p], tokens(x, n0)).then_inc(x_loaded[n0.p], 16)
                if n4:
                    ge(sp, s["x1_ready"], n4.n)
                    sp.dma_start(x4[:], tokens(x, n4)).then_inc(s["x4_loaded"], 16)
                if n1:
                    for half in range(KD):
                        wait_apart(sp, stacked[n1.p][half], n1.pair * STACK_LOADS, s["sp_apart"])
                    for i in range(2):
                        sp.wait_ge(s["qk_split"], n1.done(2, i + 1))
                        for j, part in enumerate((qk_hi, qk_lo)):
                            for k in range(KD):
                                sp.dma_start(qk_dram[n1.p, i, j, :, 8 * k:8 * k + 8].rearrange("d h c -> h d c"),
                                             part[:, i, k].bitcast(F32)).then_inc(s["qk"[i] + "_stored"], 16)
                if n4:
                    sp.wait_ge(s["x1_ready"], n4.done())
                    sp.dma_start(tokens(x1_dram, n4), x1[:]).then_inc(s["x1_stored"], 16)
                if n1:
                    for half in range(KD):
                        ge(sp, s["scores2"], (n1.n - 1) * H - H // KD * (KD - 1 - half))
                        heads = slice(half * 8, (half + 1) * 8)
                        sp.dma_start(q_st[MAX_ROW:MAX_ROW + 2, n1.p, heads].bitcast(F32),
                                     zero_blk[0:2].bitcast(F32).unsqueeze(1).broadcast_to([2, 8, S]))\
                            .then_inc(stacked[n1.p][half], 16)
                        q_parts = qk_dram[n1.p, 0, :, :, heads].rearrange("j d h c -> (j d) (h c)")
                        if half == 0:
                            sp.wait_ge(s["q_stored"], n1.done(64))
                        for r0 in PART_ROWS:
                            sp.dma_start(q_st[r0:r0 + 2 * DH, n1.p, heads].bitcast(F32), q_parts)\
                                .then_inc(stacked[n1.p][half], 16)
                        if half == 0:
                            sp.wait_ge(s["k_stored"], n1.done(64))
                        for j, r0 in enumerate(PART_ROWS):
                            k_part = qk_dram[n1.p, 1, j, :, heads].rearrange("d h c -> d (h c)")
                            sp.dma_start(k_st[r0:r0 + 2 * DH, n1.p, heads].bitcast(F32),
                                         k_part.unsqueeze(0).broadcast_to([2, DH, 8 * S]))\
                                .then_inc(stacked[n1.p][half], 16)
                if n4:
                    sp.wait_ge(s["h2_ready"], n4.done())
                    sp.dma_start(h2_dram[:, :, bass.ds(n4.n * S, S)].rearrange("k p c -> p k c"), h2[:])\
                        .then_inc(s["h2_stored"], 16)
                if n5:
                    sp.wait_ge(s["combT_evac"], n5.done())
                    for r in range(FE // REP):
                        sp.dma_start(cw_dram[0:3 * E, bass.ds(n5.n * S, S)].rearrange("(e r) c -> e r c", r=3)[:, r],
                                     combT[:]).then_inc(s["comb_stored"], 16)
                if not isinstance(m.n, int):
                    sp.dma_start(w_sb[:, bass.ds(m.n - LOOP_STEP, 1)],
                                 wall[bass.ds(m.n - LOOP_STEP, 1)].rearrange("j p c -> p j c"))\
                        .then_inc(s["w_early"], 16)

            def tokens(dram, n):
                return dram[bass.ds(n.n, 1)].rearrange("a (t p) d -> p (a t) d", p=P)

            steps(sp.Fori, step)
            sp.wait_ge(s["consts_stored"], 16)
            sp.wait_ge(s["x1_stored"], 16 * B)
            sp.wait_ge(s["h2_stored"], 16 * B)
            sp.wait_ge(s["comb_stored"], 48 * B)
            sp.wait_ge(s["w_early"], 16 * EARLY)

        @block.gpsimd
        def _(pool):
            g = nc.gpsimd
            g.memset(ident[:], 0.0).then_inc(s["ident_zero"], 1)
            pool.wait_ge(s["ident_zero"], 1)
            g.affine_select(out=ident[:], in_=ident[:], compare_op=ALU.not_equal, fill=1.0, base=0,
                            pattern=[[-1, P]], channel_multiplier=1).then_inc(s["ident_done"], 1)
            g.iota(iota_i[:], pattern=[[1, E]], base=0, channel_multiplier=0).then_inc(s["iota_int"], 1)
            pool.wait_ge(s["iota_int"], 1)
            g.memset(ones_blk[:], 1.0).then_inc(s["blocks_set"], 1)
            pool.wait_ge(s["blocks_set"], 1)
            g.memset(zero_blk[:].bitcast(F32), 0.0).then_inc(s["zeros_set"], 1)
            g.tensor_copy(iota[:], iota_i[:]).then_inc(s["iota_done"], 1)

            def newton(m):
                wait_apart(pool, s["seed"], m.done(), s["pool_apart"])
                for i in range(3):
                    ops = ((nt[:, 1], rs[:], rs[:], None), (nt[:, 1], nt[:, 1], nt[:, 0], None),
                           (nt[:, 2], nt[:, 1], None, 1.5), (rs[:], rs[:], nt[:, 2], None))
                    for j, (o, a, b, c) in enumerate(ops):
                        if i or j:
                            wait_apart(pool, s["rstd"], m.n * 12 + 4 * i + j, s["pool_apart"])
                        if c is None:
                            g.tensor_tensor(o, a, b, ALU.mult).then_inc(s["rstd"], 1)
                        else:
                            g.tensor_scalar(o, a, c, None, ALU.add).then_inc(s["rstd"], 1)

            def step(n0, n1, n2, n3, n4, n5, m):
                if n1:
                    pool.wait_ge(s["h1_ready"], n1.done())
                    ge(pool, s["v_ready"], n1.n)
                    g.tensor_tensor(h1_lo[:], h1[:], h1_hi[:].bitcast(F32), ALU.subtract)\
                        .then_inc(s["h1_lo_ready"], 1)
                    for i, name in enumerate(("q_evac", "k_evac")):
                        pool.wait_ge(s[name], n1.done())
                        ge(pool, s["qk"[i] + "_stored"], n1.n * 64)
                        g.tensor_tensor(qk_lo[:, i], qk[:, i], qk_hi[:, i].bitcast(F32), ALU.subtract)\
                            .then_inc(s["qk_split"], 1)
                if n0 or n4:
                    newton(m)
                if n0:
                    ge(pool, s["zT_ready"], n0.n)
                    wait_apart(pool, s["rstd"], m.done(12), s["pool_apart"])
                    for i in range(TT):
                        ins = g.tensor_scalar(z[:, i], xs[:, n0.p, i], mv[:, i, 0:1], rs[:, i:i + 1],
                                              ALU.subtract, ALU.mult)
                    ins.then_inc(s["z_ready"], 1)
                if n3:
                    ge(pool, s["mod_done"], 1)
                    wait_apart(pool, s["h2_ready"], n3.n - 1, s["pool_apart"])
                    g.tensor_copy(cm4[:, n3.p, 0:12], mod[:, bass.ds(n3.n, 1)].rearrange("p a c -> p (a c)"))\
                        .then_inc(s["cm4_ready"], 1)
                    pool.wait_ge(s["cm4_ready"], n3.done(2, 1))
                    g.tensor_tensor(cm4[:, n3.p, 12:14], cm4[:, n3.p, GATE1:GATE1 + 2], bo_sb[:], ALU.mult)\
                        .then_inc(s["cm4_ready"], 1)
                if n0:
                    ge(pool, s["mod_done"], 1)
                    wait_apart(pool, s["h1_ready"], n0.n - 1, s["pool_apart"])
                    g.tensor_copy(cm1[:, n0.p], mod[:, bass.ds(n0.n, 1)].rearrange("p a c -> p (a c)"))\
                        .then_inc(s["cm1_ready"], 1)

            steps(pool.Fori, step)

        @block.scalar
        def _(act):
            a = nc.scalar
            act.wait_ge(s["c_loaded"], 16)
            a.activation(c_exp[:], cT_sb[:], ACT.Exp, scale=-1.0).then_inc(s["c_exp_done"], 1)
            act.wait_ge(s["rot_step"], 6)
            a.activation(trig[:], rot[:], ACT.Sin).then_inc(s["trig_done"], 1)

            def affine(out, bank, scales, shifts):
                for k in range(KD):
                    ins = a.activation(out[:, k], bank[:, k], ACT.Identity, bias=shifts[:, k:k + 1],
                                       scale=scales[:, k:k + 1])
                return ins

            def step(n0, n1, n2, n3, n4, n5, m):
                if n5:
                    act.wait_ge(s["logits"], n5.done())
                    ge(act, s["sc1_done"], n5.n)
                    a.activation(g_exp[:], ps_m[1][:, 0, 0:TT * E].rearrange("p (t e) -> p t e", t=TT),
                                 ACT.Exp, scale=-1.0).then_inc(s["g_exp_done"], 1)
                for i in range(H):
                    if n3 and i == 0:
                        negate_max(n3, 3)
                    if n2 and i in (4, 8, 12):
                        negate_max(n2, i // 4 - 1)
                    if n1 and i == 0:
                        act.wait_ge(s["zT_ready"], n1.done())
                        act.wait_ge(s["cm1_ready"], n1.done())
                        ge(act, s["h1_lo_ready"], n1.n)
                        affine(h1, ps_m[1], cm1[:, n1.p, LN_SCALE1:], cm1[:, n1.p, LN_SHIFT1:])
                    if n3 and i == 1:
                        store_max(n3, 3)
                    if n1 and i == 1:
                        ge(act, s["v_ready"], n1.n)
                        affine(h1_hi, ps_m[1], cm1[:, n1.p, LN_SCALE1:], cm1[:, n1.p, LN_SHIFT1:])\
                            .then_inc(s["h1_ready"], 1)
                    if n2 and i % 4 == 1 and i > 1:
                        store_max(n2, i // 4 - 1)
                    if n3 and i == 3:
                        load_max(n3, 3)
                    if n2 and i in (7, 11, 15):
                        load_max(n2, i // 4 - 1)
                    if n4 and i == 1:
                        act.wait_ge(s["oF_ready"], n4.done())
                        ge(act, s["att_ready"], n4.n)
                        a.activation(o_hi[:], ps_m[0][:], ACT.Copy).then_inc(s["o_hi_ready"], 1)
                    if n4 and i == 4:
                        act.wait_ge(s["att_ready"], n4.done())
                        act.wait_ge(s["cm4_ready"], n4.done(2))
                        ge(act, s["attT_ready"], n4.n)
                        affine(att, ps_m[2], cm4[:, n4.p, GATE1:], cm4[:, n4.p, 12:]).then_inc(s["att_evac"], 1)
                    if n3 and i == 4:
                        o_copy(n3, 0)
                    if n1 and i in (5, 7):
                        j = i // 7
                        act.wait_ge(s["qk"[j] + "_ready"], n1.done())
                        ge(act, s["qk_split"], n1.n * 2 - 1 + j)
                        ge(act, s["qk"[j] + "_stored"], n1.n * 64)
                        ge(act, s["bias_done"], 1)
                        for out in (qk, qk_hi):
                            ins = affine(out[:, j], ps_m[j], trig[:, j], bias_s[:, j])
                        ins.then_inc(s["qk"[j] + "_evac"], 1)
                    if n3 and i == 12:
                        o_copy(n3, 1)
                    if n4 and i == 14:
                        act.wait_ge(s["z2T_ready"], n4.done())
                        ge(act, s["h2_stored"], n4.n * 16)
                        ge(act, s["logits"], n4.n)
                        affine(h2, ps_m[2], cm4[:, n4.p, LN_SCALE2:], cm4[:, n4.p, LN_SHIFT2:])\
                            .then_inc(s["h2_ready"], 1)
                    if n5 and i == 12:
                        act.wait_ge(s["combT_ready"], n5.done())
                        ge(act, s["comb_stored"], n5.n * 48)
                        a.activation(combT[:], ps_m[0][0:E].rearrange("p a c -> p (a c)")[:, 0:S], ACT.Copy)\
                            .then_inc(s["combT_evac"], 1)
                    if i < LAG and n3:
                        exp(n3, i + H - LAG)
                    if i >= LAG and n2:
                        exp(n2, i - LAG)

            def exp(n, h):
                act.wait_ge(s["scores2"], n.done(H, h + 1))
                ge(act, s["pv_done"], n.n * NHG + h // HG - 1)
                a.activation(pt[:, h % 8], ps2[h % 2][:], ACT.Exp).then_inc(s["probs"], 1)

            def o_copy(n, half):
                act.wait_ge(s["pv_done"], n.done(NHG, 2 * half + 2))
                ge(act, s["oT_ready"], n.n * 2 + half - 1)
                a.activation(o_sb[:, 2 * half:2 * half + 2], ps_o[:], ACT.Copy).then_inc(s["o_evac"], 1)

            def negate_max(n, g):
                act.wait_ge(s["mxT_ready"], n.done(NG, g + 1))
                ge(act, max_stored[g], n.n * 16)
                a.activation(nmx[:, g, 0], ps_m[MAX_BANK[g]][0:HG].rearrange("p a c -> p (a c)")[:, 0:S], ACT.Copy,
                             scale=-1.0).then_inc(s["nmx_hi"], 1)

            def store_max(n, g):
                act.wait_ge(s["nmx_ready"], n.done(NG, g + 1))
                ge(act, max_rows[g], n.n * 16)
                act.dma_start(max_dram[g].rearrange("r j c -> j r c"), nmx[:, g].bitcast(F32))\
                    .then_inc(max_stored[g], 16)

            def load_max(n, g):
                act.wait_ge(max_stored[g], n.done(16))
                act.wait_ge(s["scores1"], n.done(H, HG * g + HG))
                act.dma_start(q_st[MAX_ROW:MAX_ROW + 2, n.p, HG * g:HG * g + HG].bitcast(F32), max_dram[g])\
                    .then_inc(max_rows[g], 16)

            steps(act.Fori, step)

        @block.vector
        def _(dve):
            v = nc.vector
            dve.wait_ge(s["c_exp_done"], 1)
            v.tensor_scalar(c_exp[:], c_exp[:], 1.0, None, ALU.add).then_inc(s["silu_c"], 1)
            dve.wait_ge(s["silu_c"], 1)
            v.reciprocal(c_exp[:], c_exp[:]).then_inc(s["silu_c"], 1)
            dve.wait_ge(s["silu_c"], 2)
            v.tensor_tensor(cT_sb[:], cT_sb[:], c_exp[:], ALU.mult).then_inc(s["silu_c"], 1)
            v.memset(v_aug[:], 1.0).then_inc(s["v_ones"], 1)
            v.memset(mv[:], 1.0).then_inc(s["moments_set"], 1)
            dve.wait_ge(s["b_loaded"], 7 * 16)
            v.tensor_scalar(rot[:, 0], rot[:, 1], TWO_PI / 4, None, ALU.add).then_inc(s["rot_step"], 1)
            dve.wait_ge(s["rot_step"], 1)
            v.tensor_scalar(rot_t[:], rot[:], 1.0 / TWO_PI, ROUND, ALU.mult, ALU.add).then_inc(s["rot_step"], 1)
            dve.wait_ge(s["rot_step"], 2)
            v.tensor_scalar(rot_t[:], rot_t[:], ROUND, None, ALU.subtract).then_inc(s["rot_step"], 1)
            high = 6.28125
            dve.wait_ge(s["rot_step"], 3)
            v.scalar_tensor_tensor(out=rot[:], in0=rot_t[:], scalar=-high, in1=rot[:], op0=ALU.mult, op1=ALU.add)\
                .then_inc(s["rot_step"], 1)
            dve.wait_ge(s["rot_step"], 4)
            v.scalar_tensor_tensor(out=rot[:], in0=rot_t[:], scalar=-(TWO_PI - high), in1=rot[:], op0=ALU.mult,
                                   op1=ALU.add).then_inc(s["rot_step"], 1)
            dve.wait_ge(s["rot_step"], 5)
            v.tensor_scalar(rot[:], rot[:], 3.1415925, -3.1415925, ALU.min, ALU.max).then_inc(s["rot_step"], 1)
            dve.wait_ge(s["w_loaded"], 64)
            v.tensor_copy(w_hi[:], w_raw[:]).then_inc(s["wsplit"], 1)
            dve.wait_ge(s["wsplit"], 1)
            v.tensor_tensor(w_lo[:], w_raw[:], w_hi[:].bitcast(F32), ALU.subtract).then_inc(s["wsplit"], 1)
            dve.wait_ge(s["trig_done"], 1)
            v.scalar_tensor_tensor(out=trig[:, 0], in0=trig[:, 0], scalar=float(DH) ** -0.5, in1=spi[:],
                                   op0=ALU.mult, op1=ALU.mult).then_inc(s["trig_done"], 1)
            dve.wait_ge(s["trig_done"], 2)
            v.tensor_tensor(bias_s[:], bias_qk[:], trig[:], ALU.mult).then_inc(s["bias_done"], 1)
            def modulation():
                dve.wait_ge(s["mod_ready"], 1)
                v.tensor_copy(mod[:], ps1[0][:].rearrange("p a c -> p (a c)")[:, 0:12 * B]
                              .rearrange("p (j b) -> p b j", b=B)).then_inc(s["mod_step"], 1)
                n = 1
                for col in (LN_SCALE1, LN_SCALE2):
                    dve.wait_ge(s["mod_step"], n)
                    v.tensor_scalar(mod[:, :, col:col + 2], mod[:, :, col:col + 2], 1.0, None, ALU.add)\
                        .then_inc(s["mod_step"], 1)
                    n += 1
                for col in (GATE1, GATE2):
                    gate, tmp = mod[:, :, col:col + 2], mod_t[:, :, col:col + 2]
                    dve.wait_ge(s["mod_step"], n)
                    v.scalar_tensor_tensor(out=tmp, in0=gate, scalar=-1.0, in1=gate, op0=ALU.mult, op1=ALU.max)\
                        .then_inc(s["mod_step"], 1)
                    v.tensor_scalar(mod_t[:, :, 0:2], gate, 0.0, 2.0, ALU.is_ge, ALU.mult).then_inc(s["mod_step"], 1)
                    dve.wait_ge(s["mod_step"], n + 2)
                    v.tensor_scalar(tmp, tmp, 0.25, None, ALU.max).then_inc(s["mod_step"], 1)
                    dve.wait_ge(s["mod_step"], n + 3)
                    v.scalar_tensor_tensor(out=gate, in0=mod_t[:, :, 0:2], scalar=-1.0, in1=tmp, op0=ALU.add,
                                           op1=ALU.mult).then_inc(s["mod_step"], 1)
                    n += 4
                dve.wait_ge(s["mod_step"], n)
                v.tensor_copy(gate2[:], mod[:, :, GATE2:GATE2 + 2]).then_inc(s["mod_done"], 1)

            def moments(n0, n4, m, part):
                rows = ([(xs[:, n0.p], 0)] if n0 else []) + ([(x1, TT)] if n4 else [])
                if part == 0:
                    if n0:
                        dve.wait_ge(x_loaded[n0.p], (n0.pair + 1) * 16)
                    if n4:
                        dve.wait_ge(s["x1_ready"], n4.done())
                    for src, j0 in rows:
                        for j in range(TT):
                            ins = v.bn_stats(stats[:, j0 + j], src[:, j])
                    ins.then_inc(s["ln_stats"], 1)
                elif part == 1:
                    ge(dve, s["moments_set"], 1)
                    ge(dve, s["z_ready"], min(m.n, B) if isinstance(m.n, int) else m.n)
                    wait_apart(dve, s["ln_stats"], m.done(), s["dve_apart"])
                    for _, j0 in rows:
                        for j in range(TT):
                            ins = v.bn_aggr(mv[:, j0 + j], stats[:, j0 + j])
                    ins.then_inc(s["ln_aggr"], 1)
                elif part == 2:
                    dve.wait_ge(s["ln_aggr"], m.done())
                    ge(dve, s["rstd"], m.n * 12)
                    v.tensor_scalar(nt[:, 1], mv[:, :, 1], EPS, None, ALU.add).then_inc(s["half_v"], 1)
                elif part == 3:
                    dve.wait_ge(s["half_v"], m.done(2, 1))
                    v.tensor_scalar(nt[:, 2].bitcast(I32), nt[:, 1].bitcast(I32), 1, None, ALU.logical_shift_right)\
                        .then_inc(s["half_v"], 1)
                    v.tensor_scalar(nt[:, 0], nt[:, 1], -0.5, None, ALU.mult)
                else:
                    dve.wait_ge(s["half_v"], m.done(2, 2))
                    v.tensor_scalar(rs[:].bitcast(I32), nt[:, 2].bitcast(I32), -1.0, float(0x5F3759DF), ALU.mult,
                                    ALU.add).then_inc(s["seed"], 1)

            def centre(out, src, j0):
                for i in range(TT):
                    ins = v.tensor_scalar(out[:, i], src[:, i], mv[:, j0 + i, 0:1], rs[:, j0 + i:j0 + i + 1],
                                          ALU.subtract, ALU.mult)
                return ins

            def reduce(n2, h):
                dve.wait_ge(s["scores1"], n2.done(H, h + 1))
                if h % HG == 0:
                    ge(dve, s["mxT_ready"], (n2.n - 1) * NG + h // HG + 1)
                v.tensor_reduce(mx[:, :, h], ps1[h % 2][:], axis=AX.X, op=ALU.max).then_inc(s["max_done"], 1)

            def negate_max(n, g):
                bank = ps_m[MAX_BANK[g]][0:HG].rearrange("p a c -> p (a c)")[:, 0:S]
                ge(dve, max_stored[g], n.n * 16)
                dve.wait_ge(s["nmx_hi"], n.done(NG, g + 1))
                v.scalar_tensor_tensor(out=nmx[:, g, 1], in0=bank, scalar=-1.0, in1=nmx[:, g, 0].bitcast(F32),
                                       op0=ALU.mult, op1=ALU.subtract).then_inc(s["nmx_ready"], 1)

            def normalise(n, half, part):
                bank = ps_m[1 - half][:].rearrange("p t (a g c) -> p t a g c", a=2, g=HG)
                if part == 0:
                    dve.wait_ge(s["oT_ready"], n.done(2, half + 1))
                    v.reciprocal(o_inv[:], bank[:, :, :, :, DH]).then_inc(s["o_recip"], 1)
                else:
                    dve.wait_ge(s["o_recip"], n.done(2, half + 1))
                    ge(dve, s["oF_ready"], n.n)
                    out = o_n[:, :, half * P:(half + 1) * P].rearrange("p t (h c) -> p t h c", c=DH)
                    for i in range(TT):
                        ins = v.tensor_tensor(out[:, i], bank[:, i, :, :, 0:DH].rearrange("p a g c -> p (a g) c"),
                                              o_inv[:, i].rearrange("p a g -> p (a g)").unsqueeze(2)
                                              .broadcast_to([P, 2 * HG, DH]), ALU.mult)
                    ins.then_inc(s["o_norm"], 1)

            ROUTE_BEFORE = {0: 0, 1: 2, 2: 4, 3: 6, 4: 8, 5: 10}
            ROUTE_AFTER = {0: (1,), 1: (3,), 2: (5,), 3: (7,), 4: (9,), 5: (11,)}

            def route(n5, i):
                if i == 0:
                    dve.wait_ge(s["g_exp_done"], n5.done())
                    v.tensor_scalar(sc1[:], g_exp[:], 1.0, None, ALU.add).then_inc(s["sc1_done"], 1)
                if i == 1:
                    dve.wait_ge(s["sc1_done"], n5.done())
                    v.reciprocal(sc[:], sc1[:]).then_inc(s["sc_done"], 1)
                if i == 2:
                    wait_apart(dve, s["sc_done"], n5.done(), s["dve_apart"])
                    for j in range(TT):
                        ins = v.max(top[:, j], sc[:, j])
                    ins.then_inc(s["top_done"], 1)
                if i == 3:
                    wait_apart(dve, s["top_done"], n5.done(), s["dve_apart"])
                    for j in range(TT):
                        ins = v.max_index(top_i[:, j], top[:, j], sc[:, j])
                    ins.then_inc(s["idx_done"], 1)
                if i == 4:
                    dve.wait_ge(s["idx_done"], n5.done())
                    v.tensor_copy(top_f[:], top_i[:]).then_inc(s["idxf_done"], 1)
                if i == 5:
                    dve.wait_ge(s["idxf_done"], n5.done())
                    ge(dve, s["iota_done"], 1)
                    for j in range(TT):
                        ins = v.tensor_tensor(eq[:, j], iota[:].unsqueeze(2).broadcast_to([P, E, TOPK]),
                                              top_f[:, j, 0:TOPK].unsqueeze(1).broadcast_to([P, E, TOPK]),
                                              ALU.is_equal)
                    ins.then_inc(s["eq_done"], 1)
                if i == 6:
                    dve.wait_ge(s["eq_done"], n5.done())
                    v.tensor_reduce(mask[:].rearrange("p t e -> p (t e)"),
                                    eq[:].rearrange("p t e k -> p (t e) k"), axis=AX.X, op=ALU.add)\
                        .then_inc(s["mask_done"], 1)
                if i == 7:
                    dve.wait_ge(s["mask_done"], n5.done())
                    v.tensor_tensor(kept[:], mask[:], sc[:], ALU.mult).then_inc(s["kept_done"], 1)
                if i == 8:
                    dve.wait_ge(s["kept_done"], n5.done())
                    v.tensor_reduce(ksum[:], kept[:], axis=AX.X, op=ALU.add).then_inc(s["ksum_done"], 1)
                if i == 9:
                    dve.wait_ge(s["ksum_done"], n5.done())
                    v.tensor_scalar(kinv[:], ksum[:], 1e-20, None, ALU.add).then_inc(s["keps_done"], 1)
                if i == 10:
                    dve.wait_ge(s["keps_done"], n5.done())
                    v.reciprocal(kinv[:], kinv[:]).then_inc(s["kinv_done"], 1)
                if i == 11:
                    dve.wait_ge(s["kinv_done"], n5.done())
                    ge(dve, s["combT_ready"], n5.n)
                    v.tensor_tensor(comb[:], kept[:], kinv[:].unsqueeze(2).broadcast_to([P, TT, E]), ALU.mult)\
                        .then_inc(s["comb_ready"], 1)

            def step(n0, n1, n2, n3, n4, n5, m):
                for h in range(H):
                    if n5 and h in ROUTE_BEFORE:
                        route(n5, ROUTE_BEFORE[h])
                    if n2:
                        reduce(n2, h)
                    if n4 and h == 2:
                        dve.wait_ge(s["o_hi_ready"], n4.done())
                        ge(dve, s["att_ready"], n4.n)
                        v.tensor_tensor(o_lo[:], ps_m[0][:], o_hi[:].bitcast(F32), ALU.subtract)\
                            .then_inc(s["o_lo_ready"], 1)
                    if n4 and h == 6:
                        dve.wait_ge(s["attT_ready"], n4.done())
                        dve.wait_ge(s["x4_loaded"], n4.done(16))
                        ge(dve, s["x1_stored"], 16 * n4.n)
                        ge(dve, s["z2_ready"], n4.n)
                        v.tensor_tensor(x1[:], ps_m[2][:], x4[:], ALU.add).then_inc(s["x1_ready"], 1)
                    if (n0 or n4) and h in (6, 7):
                        moments(n0, n4, m, h - 6)
                    if (n0 or n4) and h == 7:
                        moments(n0, n4, m, 2)
                        moments(n0, n4, m, 3)
                        moments(n0, n4, m, 4)
                        if first(m):
                            modulation()
                    if n3 and h in (9, 10):
                        normalise(n3, 0, h - 9)
                    if n1 and h == 11:
                        dve.wait_ge(s["v_ready"], n1.done())
                        ge(dve, s["pv_done"], (n1.n - 1) * NHG)
                        ge(dve, s["v_ones"], 1)
                        for i in range(TT):
                            ins = v.tensor_tensor(v_aug[:, n1.p, i, :, 0:DH],
                                                  ps_m[2][:, i].rearrange("p (h d) -> p h d", d=DH),
                                                  bv_row[:].rearrange("p (h d) -> p h d", d=DH), ALU.add)
                        ins.then_inc(s["v_evac"], 1)
                    if n4 and h == 12:
                        dve.wait_ge(s["rstd"], m.done(12))
                        ge(dve, s["z2T_ready"], n4.n)
                        centre(z2, x1, TT).then_inc(s["z2_ready"], 1)
                    if n3 and h in (14, 15):
                        normalise(n3, 1, h - 14)
                    if n3 and h == 0:
                        negate_max(n3, 3)
                    if n2 and h in (4, 8, 12):
                        negate_max(n2, h // 4 - 1)
                    for part in ROUTE_AFTER.get(h, ()) if n5 else ():
                        route(n5, part)

            steps(dve.Fori, step)

        @block.tensor
        def _(pe):
            t = nc.tensor
            pe.wait_ge(s["silu_c"], 3)
            pe.wait_ge(s["mod_loaded"], 16)
            pm = ps1[0][:].rearrange("p a c -> p (a c)")
            for j in range(12):
                for k in range(KD):
                    ins = t.matmul(pm[:, j * B:(j + 1) * B], wmod_sb[:, k, j * P:(j + 1) * P], cT_sb[:, k],
                                   start=k == 0, stop=k == KD - 1)
            ins.then_inc(s["mod_ready"], 1)
            pe.wait_ge(s["ident_done"], 1)

            def products(out, pairs):
                terms = [(a, b) for (ah, al), (bh, bl) in pairs for a, b in ((ah, bh), (ah, bl), (al, bh))]
                for i, (a, b) in enumerate(terms):
                    ins = t.matmul(out, a, b, start=i == 0, stop=i == len(terms) - 1)
                return ins

            last = [None, None, None]

            def use(bank, evacuated, value):
                if last[bank]:
                    pe.wait_ge(*last[bank])
                last[bank] = s[evacuated], value
                return ps_m[bank]

            def transposes(out, src):
                for i in range(TT):
                    for k in range(2):
                        ins = t.transpose(out[:, k, i * P:(i + 1) * P], src[:, i, k * P:(k + 1) * P], ident[:])
                return ins

            def scores1(n, h):
                if h % 8 == 0:
                    ge(pe, s["stacks_set"], 16 * 6)
                    pe.wait_ge(stacked[n.p][h // 8], (n.pair + 1) * STACK_LOADS)
                    ge(pe, s["mod_done"], 1)
                ge(pe, s["max_done"], n.n * H + h - 1)
                for i in range(TT):
                    ins = t.matmul(ps1[h % 2][:, i], q_st[0:STACK, n.p, h, i * P:(i + 1) * P], k_st[0:STACK, n.p, h],
                                   start=True, stop=True)
                ins.then_inc(s["scores1"], 1)

            def scores2(n, h):
                if h % HG == 0:
                    pe.wait_ge(max_rows[h // HG], n.done(16))
                ge(pe, s["probs"], n.n * H + h - 1)
                for i in range(TT):
                    ins = t.matmul(ps2[h % 2][:, i], k_st[0:STACK, n.p, h, i * P:(i + 1) * P], q_st[0:STACK, n.p, h],
                                   start=True, stop=True)
                ins.then_inc(s["scores2"], 1)

            def pv(n, hg):
                pe.wait_ge(s["probs"], n.done(H, HG * (hg + 1)))
                if hg == 0:
                    pe.wait_ge(s["v_evac"], n.done())
                if hg % 2 == 0:
                    ge(pe, s["o_evac"], n.n * 2 + hg // 2)
                for i in range(TT):
                    for g in range(HG):
                        h = hg * HG + g
                        ins = t.matmul(ps_o[32 * g:32 * g + 32, hg % 2], v_aug[:, n.p, i, h], pt[:, h % 8, i],
                                       start=i == 0, stop=i == TT - 1, tile_position=(0, 32 * g))
                ins.then_inc(s["pv_done"], 1)

            def transpose_max(n, g):
                pe.wait_ge(s["max_done"], n.done(H, HG * g + HG))
                bank = use(MAX_BANK[g], "nmx_ready", n.done(NG, g + 1))
                for i in range(TT):
                    ins = t.transpose(bank[0:HG].rearrange("p a c -> p (a c)")[:, i * P:(i + 1) * P],
                                      mx[:, i, HG * g:HG * g + HG], ident[:])
                ins.then_inc(s["mxT_ready"], 1)

            def project(n1, i, name, bank):
                if i == 0:
                    pe.wait_ge(s["wsplit"], 2)
                    pe.wait_ge(s["h1_lo_ready"], n1.done())
                bank = use(bank, f"{name}_evac", n1.done())
                for m in range(KD):
                    cols = slice(m * P, (m + 1) * P)
                    if name == "v":
                        ins = products(bank[:, m], [((h1_hi[:, k, cols], h1_lo[:, k, cols]),
                                                     (w_hi[:, i, k], w_lo[:, i, k])) for k in range(KD)])
                    else:
                        ins = products(bank[:, m], [((w_hi[:, i, k, cols], w_lo[:, i, k, cols]),
                                                     (h1_hi[:, k], h1_lo[:, k])) for k in range(KD)])
                ins.then_inc(s[f"{name}_ready"], 1)

            def transpose_heads(n, half):
                pe.wait_ge(s["o_evac"], n.done(2, half + 1))
                bank = use(1 - half, "o_norm", n.done(2, half + 1))
                for i in range(TT):
                    for a in range(2):
                        ins = t.transpose(bank[:, i, a * P:(a + 1) * P], o_sb[:, 2 * half + a, i * P:(i + 1) * P],
                                          ident[:])
                ins.then_inc(s["oT_ready"], 1)

            def step(n0, n1, n2, n3, n4, n5, m):
                for i in range(H):
                    if n2:
                        scores1(n2, i)
                    if n3 and i == 0:
                        transpose_max(n3, 3)
                    if n4 and i == 3:
                        pe.wait_ge(s["o_lo_ready"], n4.done())
                        bank = use(2, "att_evac", n4.done())
                        for k in range(KD):
                            cols = slice(k * P, (k + 1) * P)
                            ins = products(bank[:, k], [((w_hi[:, 3, a, cols], w_lo[:, 3, a, cols]),
                                                         (o_hi[:, a], o_lo[:, a])) for a in range(KD)])
                        ins.then_inc(s["att_ready"], 1)
                    if n2 and i in (4, 8, 12):
                        transpose_max(n2, i // 4 - 1)
                    if n3 and i in (7, 11):
                        pv(n3, i // 4 + 1)
                    if n1 and i == 4:
                        project(n1, 0, "q", 0)
                    if n1 and i == 6:
                        project(n1, 1, "k", 1)
                    if n1 and i == 10:
                        project(n1, 2, "v", 2)
                    if i < LAG and n3:
                        scores2(n3, i + H - LAG)
                    if i >= LAG and n2:
                        scores2(n2, i - LAG)
                    if n1 and i == 0:
                        pe.wait_ge(s["z_ready"], n1.done())
                        transposes(use(1, "h1_ready", n1.done()), z).then_inc(s["zT_ready"], 1)
                    if n4 and i == 1:
                        pe.wait_ge(s["o_norm"], n4.done(2))
                        transposes(use(0, "o_lo_ready", n4.done()), o_n).then_inc(s["oF_ready"], 1)
                    if n3 and i == 2:
                        pv(n3, 1)
                    if n4 and i == 5:
                        pe.wait_ge(s["att_evac"], n4.done())
                        transposes(use(2, "x1_ready", n4.done()), att).then_inc(s["attT_ready"], 1)
                    if n3 and i == 9:
                        transpose_heads(n3, 0)
                    if n5 and i == 11:
                        pe.wait_ge(s["comb_ready"], n5.done())
                        bank = use(0, "combT_evac", n5.done())
                        for j in range(TT):
                            ins = t.transpose(bank[0:E].rearrange("p a c -> p (a c)")[:, j * P:(j + 1) * P],
                                              comb[:, j], ident[:])
                        ins.then_inc(s["combT_ready"], 1)
                    if n4 and i == 13:
                        pe.wait_ge(s["z2_ready"], n4.done())
                        transposes(use(2, "h2_ready", n4.done()), z2).then_inc(s["z2T_ready"], 1)
                    if n3 and i == 14:
                        transpose_heads(n3, 1)
                    if n4 and i == 15:
                        pe.wait_ge(s["h2_ready"], n4.done())
                        bank = use(1, "g_exp_done", n4.done())
                        for j in range(TT):
                            for k in range(KD):
                                ins = t.matmul(bank[:, 0, j * E:(j + 1) * E], h2[:, k, j * P:(j + 1) * P], gw[:, k],
                                               start=k == 0, stop=k == KD - 1)
                        ins.then_inc(s["logits"], 1)
                    if n2 and i == 15:
                        pv(n2, 0)

            def loop_begins(n0, n1, n2, n3, n4, n5, m):
                last[:] = (s["o_norm"], n4.done(2)), (s["g_exp_done"], n5.done()), (s["h2_ready"], n5.done())

            def loop_ends(n0, n1, n2, n3, n4, n5, m):
                last[:] = (s["o_norm"], n3.done(2)), (s["g_exp_done"], n4.done()), (s["h2_ready"], n4.done())

            steps(pe.Fori, step, loop_begins, loop_ends)


def ffn(nc, wall, w_sb, h2_dram, x1_dram, cw_dram, gate2, out):
    ctx = ExitStack()
    with ctx:
        def sb(name, shape, dt=F32):
            return ctx.enter_context(nc.sbuf_tensor(name, shape, dt))

        def sem(name):
            return ctx.enter_context(nc.semaphore(name))

        NP = FT // 2
        GU = 2 * KD * P
        CT = CH // P
        ident = sb("ident_f", [P, P])
        gu_hi = sb("gu_hi", [P, 2, GU], F32R)
        gu_lo = sb("gu_lo", [P, 2, GU], F32R)
        wd_hi = sb("wd_hi", [P, 2, D], F32R)
        wd_lo = sb("wd_lo", [P, 2, D], F32R)
        h = sb("h_in", [P, KD, CH])
        h_hi = sb("h_hi", [P, 2, KD, CH], F32R)
        h_lo = sb("h_lo", [P, 2, KD, CH], F32R)
        cw = sb("cw", [P, 2, CH])
        sg = sb("silu_g", [P, 2, CH])
        sw = sb("silu_gw", [P, 2, CH])
        a32 = sb("act32", [P, 2, CH])
        a_hi = sb("a_hi", [P, 2, CH], F32R)
        a_lo = sb("a_lo", [P, 2, CH], F32R)
        gy = sb("gate_y", [P, 2, KD])
        y_sb = sb("y_sb", [P, KD, CH])
        x1 = sb("x1_in", [P, CT, D])
        o_sb = sb("out_sb", [P, CT, D])
        ps_g = [ctx.enter_context(nc.psum_tensor(f"ps_g{i}", [P, CH], F32)) for i in range(2)]
        ps_u = [ctx.enter_context(nc.psum_tensor(f"ps_u{i}", [P, CH], F32)) for i in range(2)]
        ps_y = [ctx.enter_context(nc.psum_tensor(f"ps_y{i}", [P, KD, CH], F32)) for i in range(2)]
        names = """ident_zero_f ident_done_f h_loaded x1_loaded h_hi_done h_lo_done gy_done y_done y_evac yT_ready
            out_ready out_stored pool_apart_f""".split()
        s = {n: sem(n) for n in names}
        per_slot = "cw_loaded gu_hi_done gu_lo_done wd_hi_done wd_lo_done g_ready u_ready silu_done sw_done " \
                   "act_done a_hi_done a_lo_done down_done"
        s |= {n: [sem(f"{n}{i}") for i in range(2)] for n in per_slot.split()}
        w_loaded = sem("w_late")
        LATE = (FT + 1 - EARLY + 3) // 4
        block = ctx.enter_context(nc.Block())

        def chunks(fori, pair_of_tiles, between):
            def chunk(c, p):
                pair_of_tiles(c, p, 0, c * NP)
                between(c, p, 0)
                pair_of_tiles(c, p, 1, c * NP + 1)
                between(c, p, 1)
                with fori(2, NP) as jj:
                    pair_of_tiles(c, p, jj, c * NP + jj)

            for c in (0, 1):
                chunk(c, c)
            with fori(1, NCH // 2 - 1) as i:
                for p in range(2):
                    chunk(2 * i + p, p)
            for c in (NCH - 2, NCH - 1):
                chunk(c, c % 2)

        def tile(j):
            if isinstance(j, int):
                return w_sb[:, j]
            return w_sb[:, bass.ds(j, 1)].rearrange("p a c -> p (a c)")

        def is_first(c):
            return isinstance(c, int) and c == 0

        def weights_there(eng, jj):
            if not isinstance(jj, int):
                eng.wait_ge(w_loaded, 4 * 16)

        def load_h(eng, c):
            ge(eng, s["h_lo_done"], c)
            eng.dma_start(h[:], h2_dram[:, :, bass.ds(c * CH, CH)].rearrange("k p c -> p k c"))\
                .then_inc(s["h_loaded"], 16)

        def token_tiles(dram, c):
            return dram.rearrange("b (t p) d -> p (b t) d", p=P)[:, bass.ds(c * CT, CT)]

        def load_x1(act, c):
            ge(act, s["out_ready"], c)
            act.dma_start(x1[:], token_tiles(x1_dram, c)).then_inc(s["x1_loaded"], 16)

        def store(act, c):
            act.wait_ge(s["out_ready"], c + 1)
            act.dma_start(token_tiles(out, c), o_sb[:]).then_inc(s["out_stored"], 16)

        @block.sync
        def _(sp):
            def pair_of_tiles(c, p, jj, k):
                for r in range(2):
                    ge(sp, s["sw_done"][r], k)
                    sp.dma_start(cw[:, r], cw_dram[bass.ds(8 * jj + 4 * r, 4), bass.ds(c * CH, CH)]
                                 .unsqueeze(1).broadcast_to([4, REP, CH])).then_inc(s["cw_loaded"][r], 16)
                    if is_first(c) and isinstance(jj, int):
                        j0, j1 = EARLY + (2 * jj + r) * LATE, min(EARLY + (2 * jj + r + 1) * LATE, FT + 1)
                        sp.dma_start(w_sb[:, j0:j1], wall[j0:j1].rearrange("j p c -> p j c")).then_inc(w_loaded, 16)

            def between(c, p, step):
                if is_first(c) and step == 1:
                    load_h(sp, 1)

            load_h(sp, 0)
            chunks(sp.Fori, pair_of_tiles, between)
            sp.wait_ge(s["out_stored"], 16 * NCH)

        @block.gpsimd
        def _(pool):
            g = nc.gpsimd
            g.memset(ident[:], 0.0).then_inc(s["ident_zero_f"], 1)
            pool.wait_ge(s["ident_zero_f"], 1)
            g.affine_select(out=ident[:], in_=ident[:], compare_op=ALU.not_equal, fill=1.0, base=0,
                            pattern=[[-1, P]], channel_multiplier=1).then_inc(s["ident_done_f"], 1)

            def pair_of_tiles(c, p, jj, k):
                for r in range(2):
                    pool.wait_ge(s["silu_done"][r], k + 1)
                    pool.wait_ge(s["cw_loaded"][r], (k + 1) * 16)
                    ge(pool, s["act_done"][r], k)
                    g.tensor_tensor(sw[:, r], sg[:, r], cw[:, r], ALU.mult).then_inc(s["sw_done"][r], 1)

            def between(c, p, step):
                if step == 0:
                    return
                wait_apart(pool, s["y_evac"], c * 4, s["pool_apart_f"])
                g.tensor_copy(gy[:], gate2[:, bass.ds(2 * c, 2)]).then_inc(s["gy_done"], 1)

            chunks(pool.Fori, pair_of_tiles, between)

        @block.scalar
        def _(act):
            a = nc.scalar
            a.activation(gu_hi[:, 0], w_sb[:, 0, 0:GU], ACT.Copy).then_inc(s["gu_hi_done"][0], 1)

            def pair_of_tiles(c, p, jj, k):
                if is_first(c):
                    weights_there(act, jj)
                for r in range(2):
                    j = 2 * jj + r
                    act.wait_ge(s["g_ready"][r], k + 1)
                    ge(act, s["sw_done"][r], k)
                    a.activation(sg[:, r], ps_g[r][:], ACT.Silu).then_inc(s["silu_done"][r], 1)
                    ge(act, s["u_ready"][1 - r], k + r)
                    ge(act, s["gu_lo_done"][1 - r], k + r)
                    a.activation(gu_hi[:, 1 - r], tile(j + 1)[:, 0:GU], ACT.Copy).then_inc(s["gu_hi_done"][1 - r], 1)
                    ge(act, s["down_done"][r], k)
                    a.activation(wd_hi[:, r], tile(j)[:, GU:WCOL], ACT.Copy).then_inc(s["wd_hi_done"][r], 1)
                    act.wait_ge(s["act_done"][r], k + 1)
                    a.activation(a_hi[:, r], a32[:, r], ACT.Copy).then_inc(s["a_hi_done"][r], 1)

            def between(c, p, step):
                if step == 0 and not is_first(c):
                    load_x1(act, c - 1)
                    if not (isinstance(c, int) and c == 1):
                        store(act, c - 2)
                    evacuate(c - 1, 1 - p)
                if step == 1 and not (isinstance(c, int) and c + 2 >= NCH):
                    load_h(act, c + 2)

            def evacuate(c, p):
                act.wait_ge(s["y_done"], c + 1)
                act.wait_ge(s["gy_done"], c + 1)
                ge(act, s["yT_ready"], c)
                for m in range(KD):
                    for b in range(2):
                        a.activation(y_sb[:, m, b * S:(b + 1) * S], ps_y[p][:, m, b * S:(b + 1) * S], ACT.Copy,
                                     scale=gy[:, b, m:m + 1]).then_inc(s["y_evac"], 1)

            chunks(act.Fori, pair_of_tiles, between)
            load_x1(act, NCH - 1)
            store(act, NCH - 2)
            evacuate(NCH - 1, 1)
            store(act, NCH - 1)

        @block.vector
        def _(dve):
            v = nc.vector

            def split_h(c, p):
                dve.wait_ge(s["h_loaded"], (c + 1) * 16)
                ge(dve, s["u_ready"][1], (c - 1) * NP)
                v.tensor_copy(h_hi[:, p], h[:]).then_inc(s["h_hi_done"], 1)
                dve.wait_ge(s["h_hi_done"], c + 1)
                v.tensor_tensor(h_lo[:, p], h[:], h_hi[:, p].bitcast(F32), ALU.subtract).then_inc(s["h_lo_done"], 1)

            def gu_low(slot, j, k):
                dve.wait_ge(s["gu_hi_done"][slot], k + 1)
                ge(dve, s["u_ready"][slot], k)
                v.tensor_tensor(gu_lo[:, slot], tile(j)[:, 0:GU], gu_hi[:, slot].bitcast(F32), ALU.subtract)\
                    .then_inc(s["gu_lo_done"][slot], 1)

            split_h(0, 0)
            gu_low(0, 0, 0)

            def pair_of_tiles(c, p, jj, k):
                if is_first(c):
                    weights_there(dve, jj)
                for r in range(2):
                    j = 2 * jj + r
                    gu_low(1 - r, j + 1, k + r)
                    dve.wait_ge(s["u_ready"][r], k + 1)
                    dve.wait_ge(s["sw_done"][r], k + 1)
                    ge(dve, s["a_lo_done"][r], k)
                    v.tensor_tensor(a32[:, r], ps_u[r][:], sw[:, r], ALU.mult).then_inc(s["act_done"][r], 1)
                    dve.wait_ge(s["wd_hi_done"][r], k + 1)
                    v.tensor_tensor(wd_lo[:, r], tile(j)[:, GU:WCOL], wd_hi[:, r].bitcast(F32), ALU.subtract)\
                        .then_inc(s["wd_lo_done"][r], 1)
                    dve.wait_ge(s["a_hi_done"][r], k + 1)
                    v.tensor_tensor(a_lo[:, r], a32[:, r], a_hi[:, r].bitcast(F32), ALU.subtract)\
                        .then_inc(s["a_lo_done"][r], 1)

            def between(c, p, step):
                if step == 1 and not is_first(c):
                    finish(c - 1, 1 - p)
                if step == (1 if is_first(c) else 0) and not (isinstance(c, int) and c == NCH - 1):
                    split_h(c + 1, 1 - p)

            def finish(c, p):
                dve.wait_ge(s["yT_ready"], c + 1)
                dve.wait_ge(s["x1_loaded"], (c + 1) * 16)
                ge(dve, s["out_stored"], c * 16)
                v.tensor_tensor(o_sb.rearrange("p t d -> p (t d)"), ps_y[p][:].rearrange("p m c -> p (m c)"),
                                x1[:].rearrange("p t d -> p (t d)"), ALU.add).then_inc(s["out_ready"], 1)

            chunks(dve.Fori, pair_of_tiles, between)
            finish(NCH - 1, 1)

        @block.tensor
        def _(pe):
            t = nc.tensor

            def products(out, pairs, start=True, stop=True):
                terms = [(a, b) for (ah, al), (bh, bl) in pairs for a, b in ((ah, bh), (ah, bl), (al, bh))]
                for i, (a, b) in enumerate(terms):
                    ins = t.matmul(out, a, b, start=start and i == 0, stop=stop and i == len(terms) - 1,
                                   skip_group_check=not (start and stop))
                return ins

            def gate_up(c, p, r, k):
                pe.wait_ge(s["gu_lo_done"][r], k + 1)
                for which, (ps, used, ready) in enumerate(((ps_g[r], "silu_done", "g_ready"),
                                                           (ps_u[r], "act_done", "u_ready"))):
                    ge(pe, s[used][r], k)
                    cols = [slice((2 * which + i) * P, (2 * which + i + 1) * P) for i in range(KD)]
                    products(ps[:], [((gu_hi[:, r, cols[i]], gu_lo[:, r, cols[i]]), (h_hi[:, p, i], h_lo[:, p, i]))
                                     for i in range(KD)]).then_inc(s[ready][r], 1)

            def down(p, r, k, start=False, stop=False):
                pe.wait_ge(s["a_lo_done"][r], k + 1)
                pe.wait_ge(s["wd_lo_done"][r], k + 1)
                for m in range(KD):
                    cols = slice(m * P, (m + 1) * P)
                    ins = products(ps_y[p][:, m], [((wd_hi[:, r, cols], wd_lo[:, r, cols]),
                                                    (a_hi[:, r], a_lo[:, r]))], start, stop)
                ins.then_inc(s["down_done"][r], 1)
                return ins

            def last_down(c, p, r):
                down(p, r, c * NP + NP - 1, stop=r == 1)

            def pair_of_tiles(c, p, jj, k):
                for r in range(2):
                    if r == 0 and isinstance(jj, int) and jj == 0:
                        pe.wait_ge(s["h_lo_done"], c + 1)
                    gate_up(c, p, r, k)
                    if isinstance(jj, int) and jj == 0:
                        if not is_first(c):
                            last_down(c - 1, 1 - p, r)
                            if r == 1:
                                pe.wait_ge(s["down_done"][1], c * NP)
                                pe.sem_inc(s["y_done"], 1)
                    else:
                        if r == 0 and isinstance(jj, int) and jj == 1:
                            ge(pe, s["out_ready"], c - 1)
                        down(p, r, k - 1, start=isinstance(jj, int) and jj == 1 and r == 0)

            def between(c, p, step):
                if step == 1 and not is_first(c):
                    transpose_y(c - 1, 1 - p)

            def transpose_y(c, p):
                pe.wait_ge(s["y_evac"], (c + 1) * 4)
                flat = ps_y[p][:].rearrange("p m c -> p (m c)")
                for i in range(CT):
                    for m in range(KD):
                        ins = t.transpose(flat[:, i * D + m * P:i * D + (m + 1) * P], y_sb[:, m, i * P:(i + 1) * P],
                                          ident[:])
                ins.then_inc(s["yT_ready"], 1)

            pe.wait_ge(s["ident_done_f"], 1)
            chunks(pe.Fori, pair_of_tiles, between)
            for r in range(2):
                last_down(NCH - 1, 1, r)
            pe.wait_ge(s["down_done"][1], NCH * NP)
            pe.sem_inc(s["y_done"], 1)
            transpose_y(NCH - 1, 1)


def program(nc, x, cT, wmod, wqT, wkT, wvT, woT, bq, bk, bv, bo, spiral, helix, gate_w, wall, out):
    h2_dram = nc.dram_tensor("h2_scratch", [KD, P, TOK], F32, kind="Internal").ap()
    x1_dram = nc.dram_tensor("x1_scratch", [B, S, D], F32, kind="Internal").ap()
    cw_dram = nc.dram_tensor("cw_scratch", [4 * FT, TOK], F32, kind="Internal").ap()
    qk_dram = nc.dram_tensor("qk_scratch", [2, 2, 2, DH, H, S], F32, kind="Internal").ap()
    max_dram = nc.dram_tensor("max_scratch", [NG, 2, HG, S], F32, kind="Internal").ap()
    with nc.sbuf_tensor("gate2", [P, B, KD], F32) as gate2, nc.sbuf_tensor("w_sb", [P, FT + 1, WCOL], F32) as w_sb:
        attention(nc, x, cT, wmod, wqT, wkT, wvT, woT, bq, bk, bv, bo, spiral, helix, gate_w, h2_dram, x1_dram,
                  cw_dram, qk_dram, max_dram, gate2, wall, w_sb)
        ffn(nc, wall, w_sb, h2_dram, x1_dram, cw_dram, gate2, out)


def kernel(**inputs):
    import concourse.bacc as bacc
    from concourse.bass_utils import run_bass_kernel_spmd

    a = {k.removeprefix("L0_"): np.asarray(v) for k, v in inputs.items()}

    def halves(vector):
        return vector.reshape(KD, P).T

    def features(experts, shared):
        both = np.concatenate([experts.transpose(1, 0, 2).reshape(D, E * FE), shared], 1)
        both = np.pad(both, ((0, 0), (0, FT * P - both.shape[1])))
        return both.reshape(KD, P, FT, P).transpose(2, 1, 0, 3).reshape(FT, P, KD * P)

    down = np.pad(np.concatenate([a["ffn_wd"].reshape(E * FE, D), a["ffn_sd"]], 0), ((0, FT * P - E * FE - FS), (0, 0)))
    wall = np.concatenate([features(a["ffn_wg"], a["ffn_sg"]), features(a["ffn_wu"], a["ffn_su"]),
                           down.reshape(FT, P, D)], 2)
    wall = np.concatenate([wall, wall[:1]], 0)
    data = {
        "x": a["attn_x"], "cT": a["c"].T, "wmod": a["wmod"], "wqT": a["attn_Wq"].T, "wkT": a["attn_Wk"].T,
        "wvT": a["attn_Wv"].T, "woT": a["attn_Wo"].T, "bq": halves(a["attn_bq"]), "bk": halves(a["attn_bk"]),
        "bv": a["attn_bv"], "bo": halves(a["attn_bo"]), "spiral": halves(np.repeat(a["attn_spiral_weight"], DH)),
        "helix": halves(a["attn_helix_rotation"]),
        "gate_w": a["ffn_gate_w"], "wall": wall,
    }
    data = {k: np.ascontiguousarray(v) for k, v in data.items()}
    nc = bacc.Bacc("TRN2", target_bir_lowering=False, num_devices=1)
    args = [nc.dram_tensor(f"in_{k}", v.shape, mybir.dt.from_np(v.dtype), kind="ExternalInput").ap()
            for k, v in data.items()]
    out = nc.dram_tensor("out", (B, S, D), F32, kind="ExternalOutput").ap()
    program(nc, *args, out)
    r = run_bass_kernel_spmd(nc, [{f"in_{k}": v for k, v in data.items()}], core_ids=[0])
    return r.results[0]["out"]
```
